# Optimizing a Trainium2 kernel written in Bass

```python
import numpy as np
import jax
import jax.numpy as jnp

def _softmax(x, axis=-1):
    return jax.nn.softmax(x, axis=axis)

def _gelu(x):
    return jax.nn.gelu(x, approximate=True)

def _silu(x):
    return jax.nn.silu(x)

def _sigmoid(x):
    return jax.nn.sigmoid(x)

def _layernorm(x, axis=-1, eps=1e-05):
    m = jnp.mean(x, axis=axis, keepdims=True)
    v = jnp.var(x, axis=axis, keepdims=True)
    return (x - m) / jnp.sqrt(v + eps)

def _scatter_add(tgt, idx, src, axis=0):
    return tgt.at[idx].add(src)

def _segment_sum(src, seg, n):
    return jax.ops.segment_sum(src, seg, n)
kernel_name = 'mk_macaron_d2_jaxref_r4_ebbcf2'

def setup_inputs(seed: int=0):
    np.random.seed(seed)
    _w = jnp.asarray

    def _L0_attn_setup():
        import jax, jax.numpy as jnp
        import numpy as np
        D_MODEL = 256
        N_HEADS = 16
        D_K = D_MODEL // N_HEADS
        BASE = 10000.0

        def _rope(x):
            S = x.shape[1]
            freqs = BASE ** (-(jnp.arange(0, D_K, 2, dtype=jnp.float32) / D_MODEL))
            angles = jnp.arange(S, dtype=jnp.float32)[:, None] * freqs[None, :]
            cos = jnp.cos(angles)[None, :, None, :]
            sin = jnp.sin(angles)[None, :, None, :]
            xe, xo = (x[..., 0::2], x[..., 1::2])
            x1 = xe * cos - xo * sin
            x2 = xe * sin + xo * cos
            return jnp.stack([x1, x2], axis=-1).reshape(x.shape)
        key = jax.random.key(seed)
        ks = jax.random.split(key, 7)
        B, S = (4, 1024)
        scale = 1.0 / np.sqrt(D_MODEL)
        return {'x': jax.random.normal(ks[0], (B, S, D_MODEL), jnp.float32), 'Wq': jax.random.normal(ks[1], (D_MODEL, D_MODEL), jnp.float32) * scale, 'bq': jnp.zeros((D_MODEL,), jnp.float32), 'Wk': jax.random.normal(ks[2], (D_MODEL, D_MODEL), jnp.float32) * scale, 'bk': jnp.zeros((D_MODEL,), jnp.float32), 'Wv': jax.random.normal(ks[3], (D_MODEL, D_MODEL), jnp.float32) * scale, 'bv': jnp.zeros((D_MODEL,), jnp.float32)}
    _L0_attn_in = _L0_attn_setup()

    def _L0_ffn_setup():
        import jax, jax.numpy as jnp
        import numpy as np
        TEMPERATURE = 0.5
        CAPACITY_FACTOR = 1.25
        TOP_K = 1
        key = jax.random.key(seed)
        ks = jax.random.split(key, 5)
        B, S, D, H, E = (4, 512, 256, 512, 8)
        s = 0.02
        return {'x': jax.random.normal(ks[0], (B, S, D), jnp.float32), 'gate_w': jax.random.normal(ks[1], (E, D), jnp.float32) * s, 'gate_b': jnp.zeros((E,), jnp.float32), 'rms_w': jnp.ones((E,), jnp.float32), 'w1': jax.random.normal(ks[2], (E, D, H), jnp.float32) * s, 'b1': jnp.zeros((E, H), jnp.float32), 'w2': jax.random.normal(ks[3], (E, H, D), jnp.float32) * s, 'b2': jnp.zeros((E, D), jnp.float32)}
    _L0_ffn_in = _L0_ffn_setup()

    def _L1_attn_setup():
        import jax, jax.numpy as jnp
        import numpy as np
        B, L, D = (2, 512, 256)
        H, HD = (16, 64)
        LD = 64
        key = jax.random.key(seed)
        ks = jax.random.split(key, 6)
        s = lambda fan_in: 1.0 / np.sqrt(fan_in)
        x_bld = jax.random.normal(ks[0], (B, L, D), dtype=jnp.float32)
        Wq = jax.random.normal(ks[1], (D, H, HD), dtype=jnp.float32) * s(D)
        Wkv_down = jax.random.normal(ks[2], (D, LD), dtype=jnp.float32) * s(D)
        Wk_up = jax.random.normal(ks[3], (LD, H, HD), dtype=jnp.float32) * s(LD)
        Wv_up = jax.random.normal(ks[4], (LD, H, HD), dtype=jnp.float32) * s(LD)
        Wout = jax.random.normal(ks[5], (H, HD, D), dtype=jnp.float32) * s(H * HD)
        return {'x_bld': x_bld, 'Wq': Wq, 'Wkv_down': Wkv_down, 'Wk_up': Wk_up, 'Wv_up': Wv_up, 'Wout': Wout}
    _L1_attn_in = _L1_attn_setup()

    def _L1_ffn_setup():
        import jax, jax.numpy as jnp
        import numpy as np
        B, S, D, H, F = (4, 1024, 256, 16, 1024)
        CAP = 0.125
        ROPE_BASE = 10000.0

        def rmsnorm(x, g):
            return x * jax.lax.rsqrt(jnp.mean(x * x, -1, keepdims=True) + 1e-06) * g

        def rope(t, pos):
            hd = t.shape[-1]
            inv = 1.0 / ROPE_BASE ** (jnp.arange(0, hd, 2, dtype=jnp.float32) / hd)
            f = pos[:, None, :, None].astype(jnp.float32) * inv
            emb = jnp.concatenate([f, f], axis=-1)
            cos, sin = (jnp.cos(emb), jnp.sin(emb))
            rot = jnp.concatenate([-t[..., hd // 2:], t[..., :hd // 2]], axis=-1)
            return t * cos + rot * sin
        key = jax.random.key(seed)
        ks = jax.random.split(key, 9)
        scale = 0.02
        x = jax.random.normal(ks[0], (B, S, D), jnp.float32)
        causal = jnp.where(jnp.tril(jnp.ones((S, S), bool)), 0.0, -1000000000.0).astype(jnp.float32)
        attention_mask = jnp.broadcast_to(causal[None, None], (B, 1, S, S))
        position_ids = jnp.broadcast_to(jnp.arange(S, dtype=jnp.int32), (B, S))
        return {'x': x, 'attention_mask': attention_mask, 'position_ids': position_ids, 'router_w': jax.random.normal(ks[1], (D, 1), jnp.float32) * scale, 'router_b': jnp.zeros((1,), jnp.float32), 'wq': jax.random.normal(ks[2], (D, D), jnp.float32) * scale, 'wk': jax.random.normal(ks[3], (D, D), jnp.float32) * scale, 'wv': jax.random.normal(ks[4], (D, D), jnp.float32) * scale, 'wo': jax.random.normal(ks[5], (D, D), jnp.float32) * scale, 'w1': jax.random.normal(ks[6], (D, F), jnp.float32) * scale, 'w2': jax.random.normal(ks[7], (F, D), jnp.float32) * scale, 'ln1': jnp.ones((D,), jnp.float32), 'ln2': jnp.ones((D,), jnp.float32)}
    _L1_ffn_in = _L1_ffn_setup()
    _d = {'L0_attn_x': _L0_attn_in['x'], 'L0_attn_Wq': _L0_attn_in['Wq'], 'L0_attn_bq': _L0_attn_in['bq'], 'L0_attn_Wk': _L0_attn_in['Wk'], 'L0_attn_bk': _L0_attn_in['bk'], 'L0_attn_Wv': _L0_attn_in['Wv'], 'L0_attn_bv': _L0_attn_in['bv'], 'L0_ffn_gate_w': _L0_ffn_in['gate_w'], 'L0_ffn_gate_b': _L0_ffn_in['gate_b'], 'L0_ffn_rms_w': _L0_ffn_in['rms_w'], 'L0_ffn_w1': _L0_ffn_in['w1'], 'L0_ffn_b1': _L0_ffn_in['b1'], 'L0_ffn_w2': _L0_ffn_in['w2'], 'L0_ffn_b2': _L0_ffn_in['b2'], 'L1_attn_Wq': _L1_attn_in['Wq'], 'L1_attn_Wkv_down': _L1_attn_in['Wkv_down'], 'L1_attn_Wk_up': _L1_attn_in['Wk_up'], 'L1_attn_Wv_up': _L1_attn_in['Wv_up'], 'L1_attn_Wout': _L1_attn_in['Wout'], 'L1_ffn_attention_mask': _L1_ffn_in['attention_mask'], 'L1_ffn_position_ids': _L1_ffn_in['position_ids'], 'L1_ffn_router_w': _L1_ffn_in['router_w'], 'L1_ffn_router_b': _L1_ffn_in['router_b'], 'L1_ffn_wq': _L1_ffn_in['wq'], 'L1_ffn_wk': _L1_ffn_in['wk'], 'L1_ffn_wv': _L1_ffn_in['wv'], 'L1_ffn_wo': _L1_ffn_in['wo'], 'L1_ffn_w1': _L1_ffn_in['w1'], 'L1_ffn_w2': _L1_ffn_in['w2'], 'L1_ffn_ln1': _L1_ffn_in['ln1'], 'L1_ffn_ln2': _L1_ffn_in['ln2']}
    _x0 = _d['L0_attn_x']
    _d['L0_attn_x'] = jax.random.normal(jax.random.fold_in(jax.random.key(seed), 1), (8, 512, 256), dtype=_x0.dtype)
    del _x0
    return _d

def reference(L0_attn_x, L0_attn_Wq, L0_attn_bq, L0_attn_Wk, L0_attn_bk, L0_attn_Wv, L0_attn_bv, L0_ffn_gate_w, L0_ffn_gate_b, L0_ffn_rms_w, L0_ffn_w1, L0_ffn_b1, L0_ffn_w2, L0_ffn_b2, L1_attn_Wq, L1_attn_Wkv_down, L1_attn_Wk_up, L1_attn_Wv_up, L1_attn_Wout, L1_ffn_attention_mask, L1_ffn_position_ids, L1_ffn_router_w, L1_ffn_router_b, L1_ffn_wq, L1_ffn_wk, L1_ffn_wv, L1_ffn_wo, L1_ffn_w1, L1_ffn_w2, L1_ffn_ln1, L1_ffn_ln2):

    def _L0_attn_ref(x, Wq, bq, Wk, bk, Wv, bv):
        import jax, jax.numpy as jnp
        import numpy as np
        D_MODEL = 256
        N_HEADS = 16
        D_K = D_MODEL // N_HEADS
        BASE = 10000.0

        def _rope(x):
            S = x.shape[1]
            freqs = BASE ** (-(jnp.arange(0, D_K, 2, dtype=jnp.float32) / D_MODEL))
            angles = jnp.arange(S, dtype=jnp.float32)[:, None] * freqs[None, :]
            cos = jnp.cos(angles)[None, :, None, :]
            sin = jnp.sin(angles)[None, :, None, :]
            xe, xo = (x[..., 0::2], x[..., 1::2])
            x1 = xe * cos - xo * sin
            x2 = xe * sin + xo * cos
            return jnp.stack([x1, x2], axis=-1).reshape(x.shape)
        B, S, D = x.shape
        Q = (x @ Wq + bq).reshape(B, S, N_HEADS, D_K)
        K = (x @ Wk + bk).reshape(B, S, N_HEADS, D_K)
        V = (x @ Wv + bv).reshape(B, S, N_HEADS, D_K)
        Q = _rope(Q)
        K = _rope(K)
        score = jnp.einsum('bsid,bsjd->bsij', Q, K) / jnp.sqrt(jnp.float32(D_K))
        attn = jax.nn.softmax(score, axis=-1)
        out = jnp.einsum('bsij,bsjd->bsid', attn, V)
        return out.reshape(B, S, D)

    def _L0_ffn_ref(x, gate_w, gate_b, rms_w, w1, b1, w2, b2):
        import jax, jax.numpy as jnp
        import numpy as np
        TEMPERATURE = 0.5
        CAPACITY_FACTOR = 1.25
        TOP_K = 1
        B, S, D = x.shape
        E = gate_w.shape[0]
        xf = x.reshape(-1, D)
        N = xf.shape[0]
        logits = xf @ gate_w.T + gate_b
        eps = jnp.finfo(logits.dtype).eps
        ms = jnp.mean(logits * logits, axis=-1, keepdims=True)
        logits = logits * jax.lax.rsqrt(ms + eps) * rms_w
        gates = jax.nn.softmax(logits / TEMPERATURE, axis=-1)
        g, idx = jax.lax.top_k(gates, TOP_K)
        g, idx = (g[:, 0], idx[:, 0])
        capacity = min(int(np.ceil(N * TOP_K / E * CAPACITY_FACTOR)), N)
        counts = jnp.zeros((E,), jnp.int32).at[idx].add(1)
        active = (counts > 0) & (capacity >= 1)
        mask = active[idx].astype(gates.dtype)
        masked = g * mask
        norm_g = masked / (masked + 1e-06)
        h = jax.nn.gelu(jnp.einsum('nd,edh->neh', xf, w1) + b1, approximate=False)
        y = jnp.einsum('neh,ehd->ned', h, w2) + b2
        out = (y * norm_g[:, None, None]).sum(axis=1)
        return out.reshape(B, S, D)

    def _L1_attn_ref(x_bld, Wq, Wkv_down, Wk_up, Wv_up, Wout):
        import jax, jax.numpy as jnp
        import numpy as np
        B, L, D = (2, 512, 256)
        H, HD = (16, 64)
        LD = 64
        q_blhd = jnp.einsum('bld,dhk->blhk', x_bld, Wq)
        latent_bll = jnp.einsum('bld,dc->blc', x_bld, Wkv_down)
        k_blhd = jnp.einsum('blc,chk->blhk', latent_bll, Wk_up)
        v_blhd = jnp.einsum('blc,chk->blhk', latent_bll, Wv_up)
        attn = jnp.einsum('bqhd,bkhd->bhqk', q_blhd, k_blhd) / jnp.sqrt(jnp.asarray(HD, dtype=x_bld.dtype))
        l = x_bld.shape[1]
        mask = (jnp.arange(l)[None, :] <= jnp.arange(l)[:, None])[None, None]
        neg_inf = jnp.finfo(attn.dtype).min
        attn = jax.nn.softmax(jnp.where(mask, attn, neg_inf), axis=-1)
        y_blhd = jnp.einsum('bhqk,bkhd->bqhd', attn, v_blhd)
        return jnp.einsum('bqhd,hdo->bqo', y_blhd, Wout)

    def _L1_ffn_ref(x, attention_mask, position_ids, router_w, router_b, wq, wk, wv, wo, w1, w2, ln1, ln2):
        import jax, jax.numpy as jnp
        import numpy as np
        B, S, D, H, F = (4, 1024, 256, 16, 1024)
        CAP = 0.125
        ROPE_BASE = 10000.0

        def rmsnorm(x, g):
            return x * jax.lax.rsqrt(jnp.mean(x * x, -1, keepdims=True) + 1e-06) * g

        def rope(t, pos):
            hd = t.shape[-1]
            inv = 1.0 / ROPE_BASE ** (jnp.arange(0, hd, 2, dtype=jnp.float32) / hd)
            f = pos[:, None, :, None].astype(jnp.float32) * inv
            emb = jnp.concatenate([f, f], axis=-1)
            cos, sin = (jnp.cos(emb), jnp.sin(emb))
            rot = jnp.concatenate([-t[..., hd // 2:], t[..., :hd // 2]], axis=-1)
            return t * cos + rot * sin
        b, s, d = x.shape
        hd = d // H
        weights = (x @ router_w)[..., 0] + router_b[0]
        k = int(CAP * s)
        topv, topi = jax.lax.top_k(weights, k)
        thr = topv[:, -1]
        sel_mask = (weights > thr[:, None]).astype(x.dtype)
        kc = k - 1
        sel_idx = jnp.sort(topi[:, :kc], axis=1)
        bidx = jnp.arange(b)[:, None]
        x_sel = x[bidx, sel_idx]
        pos_sel = position_ids[bidx, sel_idx]
        w_sel = weights[bidx, sel_idx]
        m = attention_mask[:, 0]
        m_sel = m[bidx[:, :, None], sel_idx[:, :, None], sel_idx[:, None, :]]
        hn = rmsnorm(x_sel, ln1)

        def heads(t):
            return t.reshape(b, kc, H, hd).transpose(0, 2, 1, 3)
        q = rope(heads(hn @ wq), pos_sel)
        kk = rope(heads(hn @ wk), pos_sel)
        v = heads(hn @ wv)
        sc = jnp.einsum('bhqd,bhkd->bhqk', q, kk) / np.sqrt(hd).astype(np.float32)
        sc = sc + m_sel[:, None]
        a = jax.nn.softmax(sc, axis=-1)
        o = jnp.einsum('bhqk,bhkd->bhqd', a, v).transpose(0, 2, 1, 3).reshape(b, kc, d) @ wo
        x1 = x_sel + o
        x2 = x1 + jax.nn.gelu(rmsnorm(x1, ln2) @ w1) @ w2
        proc = x2 * w_sel[..., None]
        out = jnp.zeros_like(x).at[bidx, sel_idx].set(proc)
        return out + x * (1.0 - sel_mask)[..., None]
    x = L0_attn_x
    x = x + 0.5 * _L0_ffn_ref(_layernorm(x, axis=-1), L0_ffn_gate_w, L0_ffn_gate_b, L0_ffn_rms_w, L0_ffn_w1, L0_ffn_b1, L0_ffn_w2, L0_ffn_b2)
    x = x + _L0_attn_ref(_layernorm(x, axis=-1), L0_attn_Wq, L0_attn_bq, L0_attn_Wk, L0_attn_bk, L0_attn_Wv, L0_attn_bv)
    x = x + 0.5 * _L0_ffn_ref(_layernorm(x, axis=-1), L0_ffn_gate_w, L0_ffn_gate_b, L0_ffn_rms_w, L0_ffn_w1, L0_ffn_b1, L0_ffn_w2, L0_ffn_b2)
    x = x + 0.5 * _L1_ffn_ref(_layernorm(x, axis=-1), L1_ffn_attention_mask, L1_ffn_position_ids, L1_ffn_router_w, L1_ffn_router_b, L1_ffn_wq, L1_ffn_wk, L1_ffn_wv, L1_ffn_wo, L1_ffn_w1, L1_ffn_w2, L1_ffn_ln1, L1_ffn_ln2)
    x = x + _L1_attn_ref(_layernorm(x, axis=-1), L1_attn_Wq, L1_attn_Wkv_down, L1_attn_Wk_up, L1_attn_Wv_up, L1_attn_Wout)
    x = x + 0.5 * _L1_ffn_ref(_layernorm(x, axis=-1), L1_ffn_attention_mask, L1_ffn_position_ids, L1_ffn_router_w, L1_ffn_router_b, L1_ffn_wq, L1_ffn_wk, L1_ffn_wv, L1_ffn_wo, L1_ffn_w1, L1_ffn_w2, L1_ffn_ln1, L1_ffn_ln2)
    return x

_drawn_inputs = setup_inputs


def setup_inputs(seed=0):
    import zlib

    import numpy as np

    out = dict(_drawn_inputs(seed))
    spreads = {'L0_attn_bq': (0.0, 0.1),
     'L0_attn_bk': (0.0, 0.1),
     'L0_attn_bv': (0.0, 0.1),
     'L0_ffn_gate_b': (0.0, 0.8),
     'L0_ffn_rms_w': (1.0, 0.6),
     'L0_ffn_b1': (0.0, 0.1),
     'L0_ffn_b2': (0.0, 0.1),
     'L1_ffn_ln1': (1.0, 0.6),
     'L1_ffn_ln2': (1.0, 0.6)}
    factors = {'L0_ffn_gate_w': 8.0,
     'L1_ffn_wq': 8.0,
     'L1_ffn_wk': 8.0,
     'L1_ffn_wv': 7.374,
     'L1_ffn_wo': 7.867,
     'L1_ffn_w1': 4.223,
     'L1_ffn_w2': 4.233}
    for name, (base, spread) in spreads.items():
        noise = np.random.default_rng([zlib.crc32(name.encode()), seed]).standard_normal(out[name].shape)
        drawn = base * np.exp(spread * noise) if base else spread * noise
        out[name] = jnp.asarray(drawn.astype(out[name].dtype))
    for name, factor in factors.items():
        out[name] = (out[name] * factor).astype(out[name].dtype)
    return out
```

```python
from contextlib import ExitStack

import numpy as np

import concourse.bass as bass
from concourse import mybir

F32 = mybir.dt.float32
F16 = mybir.dt.float16
I32 = mybir.dt.int32
U32 = mybir.dt.uint32
ALU = mybir.AluOpType
ACT = mybir.ActivationFunctionType
AX = mybir.AxisListType

P = 128
BATCH, SEQ, D = 8, 512, 256
TILES = SEQ // P
KD = D // P
EXPERTS, EXPERT_HID = 8, 512
HID_TILES = EXPERTS * EXPERT_HID // P
HEADS, HEAD_DIM = 16, 16
QKV = 3 * D
LN_EPS = 1e-5
F32_EPS = float(np.finfo(np.float32).eps)

WS = 16.0

RSQRT_STEPS = 11
LN_STEPS = TILES + 7 + RSQRT_STEPS + TILES
GATE_STEPS = 24
HEAD_STEPS = 102
STAGES = 2 * BATCH


def rsqrt_newton(dve, step, at, v, y, t):
    yi = y.bitcast(I32)
    dve.wait_ge(step, at)
    dve.tensor_scalar(yi, v.bitcast(I32), 1, None, ALU.logical_shift_right).then_inc(step, 1)
    dve.wait_ge(step, at + 1)
    dve.tensor_scalar(yi, yi, -1.0, float(0x5F3759DF), ALU.mult, ALU.add).then_inc(step, 1)
    for n in range(3):
        dve.wait_ge(step, at + 2 + 3 * n)
        dve.tensor_tensor(t, y, y, ALU.mult).then_inc(step, 1)
        dve.wait_ge(step, at + 3 + 3 * n)
        dve.scalar_tensor_tensor(t, t, -0.5, v, ALU.mult, ALU.mult).then_inc(step, 1)
        dve.wait_ge(step, at + 4 + 3 * n)
        dve.scalar_tensor_tensor(y, t, 1.5, y, ALU.add, ALU.mult).then_inc(step, 1)


def layernorm_batch(dve, step, at, x4, y4, stats, col, var, rstd, tmp):
    for t in range(TILES):
        dve.bn_stats(stats[:, t, :], x4[:, t, :]).then_inc(step, 1)
    twice_mean, gap, squares, mean = (col[:, i, :] for i in range(4))
    dve.wait_ge(step, at + TILES)
    dve.tensor_tensor(twice_mean, stats[:, :, 1], stats[:, :, 4], ALU.add).then_inc(step, 1)
    dve.tensor_tensor(gap, stats[:, :, 1], stats[:, :, 4], ALU.subtract).then_inc(step, 1)
    dve.tensor_tensor(squares, stats[:, :, 2], stats[:, :, 5], ALU.add).then_inc(step, 1)
    dve.wait_ge(step, at + TILES + 3)
    dve.tensor_scalar(mean, twice_mean, 0.5, None, ALU.mult).then_inc(step, 1)
    dve.tensor_tensor(gap, gap, gap, ALU.mult).then_inc(step, 1)
    dve.tensor_scalar(squares, squares, 1.0 / D, LN_EPS, ALU.mult, ALU.add).then_inc(step, 1)
    dve.wait_ge(step, at + TILES + 6)
    dve.scalar_tensor_tensor(var, gap, 0.25, squares, ALU.mult, ALU.add).then_inc(step, 1)
    rsqrt_newton(dve, step, at + TILES + 7, var, rstd, tmp)
    dve.wait_ge(step, at + TILES + 7 + RSQRT_STEPS)
    for t in range(TILES):
        dve.tensor_scalar(y4[:, t, :], x4[:, t, :], mean[:, t:t + 1], rstd[:, t:t + 1],
                          ALU.subtract, ALU.mult).then_inc(step, 1)


def transpose_tiles(pe, y4, out2, ident):
    for k in range(KD):
        for t in range(TILES):
            last = pe.transpose(out2[:, k, t * P:(t + 1) * P], y4[:, t, k * P:(k + 1) * P], ident)
    return last


def split_matmul(pe, out, w_hi, w_lo, v_hi, v_lo, first, final):
    pe.matmul(out, w_hi, v_hi, start=first, stop=False)
    pe.matmul(out, w_hi, v_lo, start=False, stop=False)
    return pe.matmul(out, w_lo, v_hi, start=False, stop=final)


def expert_and_head_layers(nc, keep, x, ident, io):
    with ExitStack() as ctx:
        def sb(name, shape, dt=F32):
            return ctx.enter_context(nc.sbuf_tensor(name, shape, dt))

        def sem(name):
            return keep.enter_context(nc.semaphore(name))

        w1_hi = sb("w1_hi", [P, KD, HID_TILES * P], F16)
        w1_lo = sb("w1_lo", [P, KD, HID_TILES * P], F16)
        w2_hi = sb("w2_hi", [P, HID_TILES, D], F16)
        w2_lo = sb("w2_lo", [P, HID_TILES, D], F16)
        wqkv_hi = sb("wqkv_hi", [P, KD, QKV], F16)
        wqkv_lo = sb("wqkv_lo", [P, KD, QKV], F16)
        gate_hi = sb("gate_hi", [P, KD, EXPERTS], F16)
        gate_lo = sb("gate_lo", [P, KD, EXPERTS], F16)
        gate_bias = sb("gate_bias", [EXPERTS, 1])
        rms_w = sb("rms_w", [P, EXPERTS])
        b1_col = sb("b1_col", [P, HID_TILES])
        b2_sum = sb("b2_sum", [P, KD])
        qkv_bias = sb("qkv_bias", [P, QKV])
        rope = sb("rope", [P, TILES, 2, HEAD_DIM // 2])

        with ExitStack() as setup:
            def tmp(name, shape, dt=F32):
                return setup.enter_context(nc.sbuf_tensor(name, shape, dt))

            def tsem(name):
                return keep.enter_context(nc.semaphore(name))

            SLOTS = 4
            CHUNK = KD * EXPERT_HID
            stage = tmp("stage", [P, SLOTS, CHUNK])
            b1_rows = tmp("b1_rows", [HID_TILES, P])
            gate_rows = tmp("gate_rows", [EXPERTS, D])
            b2_rows = tmp("b2_rows", [EXPERTS, D])
            ones = tmp("ones", [EXPERTS, 1])
            gate_t = tmp("gate_t", [P, KD, EXPERTS])
            small = setup.enter_context(nc.psum_tensor("small", [P, 3, 512], F32))
            slot_in = [tsem(f"slot_in{i}") for i in range(SLOTS)]
            small_in = tsem("small_in")
            head_done = tsem("head_done")
            tail_done = tsem("tail_done")
            small_t = tsem("small_t")
            ones_set = tsem("ones_set")
            gate_step = tsem("gate_split_step")

            chunks = []
            for w, lo, hi in ((io["Wq"], 0, D), (io["Wk"], D, 2 * D), (io["Wv"], 2 * D, QKV)):
                chunks.append((w.rearrange("(k p) n -> p k n", p=P), (KD, D),
                               wqkv_hi[:, :, lo:hi], wqkv_lo[:, :, lo:hi]))
            for e in range(EXPERTS):
                cols = slice(e * EXPERT_HID, (e + 1) * EXPERT_HID)
                chunks.append((io["w1"][e].rearrange("(k p) h -> p k h", p=P), (KD, EXPERT_HID),
                               w1_hi[:, :, cols], w1_lo[:, :, cols]))
                rows = slice(e * EXPERT_HID // P, (e + 1) * EXPERT_HID // P)
                chunks.append((io["w2"][e].rearrange("(j p) d -> p j d", p=P), (EXPERT_HID // P, D),
                               w2_hi[:, rows, :], w2_lo[:, rows, :]))

            def staged(c):
                a, b = chunks[c][1]
                return stage[:, c % SLOTS, 0:a * b].rearrange("p (a b) -> p a b", a=a)

            SMALL_LOADS = 8
            with nc.Block() as block:
                @block.sync
                def _(sp):
                    for c, (src, _, _, _) in enumerate(chunks):
                        if c >= SLOTS:
                            sp.wait_ge(tail_done, c - SLOTS + 1)
                        sp.dma_start(staged(c), src).then_inc(slot_in[c % SLOTS], 16)

                @block.gpsimd
                def _(pool):
                    pool.memset(ones[:, :], 1.0).then_inc(ones_set, 1)
                    pool.dma_start(b1_rows[:, :], io["b1"].rearrange("e (j p) -> (e j) p", p=P)).then_inc(small_in, 16)
                    pool.dma_start(gate_rows[:, :], io["gate_w"]).then_inc(small_in, 16)
                    pool.dma_start(b2_rows[:, :], io["b2"]).then_inc(small_in, 16)
                    pool.dma_start(gate_bias[:, :], io["gate_b"].rearrange("(e o) -> e o", o=1)).then_inc(small_in, 16)
                    pool.dma_start(rms_w[:, :], io["rms_w"].partition_broadcast(P)).then_inc(small_in, 16)
                    for i, name in enumerate(("bq", "bk", "bv")):
                        pool.dma_start(qkv_bias[:, i * D:(i + 1) * D],
                                       io[name].partition_broadcast(P)).then_inc(small_in, 16)
                    pool.dma_start(rope[:, :, :, :],
                                   io["rope_tab"].rearrange("(t p) c i -> p t c i", p=P)).then_inc(small_in, 16)

                @block.scalar
                def _(act):
                    for c, (_, _, hi, _) in enumerate(chunks):
                        act.wait_ge(slot_in[c % SLOTS], 16 * (c // SLOTS + 1))
                        act.activation(hi, staged(c), ACT.Copy, scale=WS).then_inc(head_done, 1)

                @block.vector
                def _(dve):
                    for c, (_, _, hi, lo) in enumerate(chunks):
                        dve.wait_ge(head_done, c + 1)
                        dve.scalar_tensor_tensor(lo, staged(c), WS, hi, ALU.mult,
                                                 ALU.subtract).then_inc(tail_done, 1)
                    dve.wait_ge(small_t, 3)
                    dve.tensor_copy(b1_col[:, :], small[:, 0, 0:HID_TILES])
                    dve.tensor_copy(b2_sum[:, :], small[:, 1, 0:KD])
                    dve.tensor_scalar(gate_t[:, :, :], small[:, 2, 0:KD * EXPERTS].rearrange("p (k e) -> p k e", k=KD),
                                      WS, None, ALU.mult).then_inc(gate_step, 1)
                    dve.wait_ge(gate_step, 1)
                    dve.tensor_copy(gate_hi[:, :, :], gate_t[:, :, :]).then_inc(gate_step, 1)
                    dve.wait_ge(gate_step, 2)
                    dve.tensor_tensor(gate_lo[:, :, :], gate_t[:, :, :], gate_hi[:, :, :], ALU.subtract)

                @block.tensor
                def _(pe):
                    pe.wait_ge(small_in, 16 * (SMALL_LOADS + 1))
                    pe.wait_ge(ones_set, 1)
                    pe.transpose(small[:, 0, 0:HID_TILES], b1_rows[:, :],
                                 ident[0:HID_TILES, 0:HID_TILES]).then_inc(small_t, 1)
                    for k in range(KD):
                        last = pe.matmul(small[:, 1, k:k + 1], b2_rows[:, k * P:(k + 1) * P], ones[:, :],
                                         start=True, stop=True)
                    last.then_inc(small_t, 1)
                    for k in range(KD):
                        last = pe.transpose(small[:, 2, k * EXPERTS:(k + 1) * EXPERTS],
                                            gate_rows[:, k * P:(k + 1) * P], ident[0:EXPERTS, 0:EXPERTS])
                    last.then_inc(small_t, 1)

        GBUF = 4
        GROUP = 4
        y = sb("y", [P, TILES, D])
        y_hi = sb("y_hi", [P, KD, SEQ], F16)
        y_lo = sb("y_lo", [P, KD, SEQ], F16)
        z_hi = sb("z_hi", [P, KD, SEQ], F16)
        z_lo = sb("z_lo", [P, KD, SEQ], F16)
        g_full = sb("g_full", [P, GBUF, SEQ])
        g_hi = sb("g_hi", [P, GBUF, SEQ], F16)
        g_lo = sb("g_lo", [P, GBUF, SEQ], F16)
        acc_sb = sb("acc_sb", [P, KD, SEQ])
        stats = sb("stats", [P, TILES, 6])
        ln_col = sb("ln_col", [P, 4, TILES])
        var = sb("var", [P, TILES])
        rstd = sb("rstd", [P, TILES])
        newton = sb("newton", [P, TILES])
        logit_rows = sb("logit_rows", [EXPERTS, SEQ])
        logit = sb("logit", [P, TILES, EXPERTS])
        logit_sq = sb("logit_sq", [P, TILES, EXPERTS])
        gate_c = sb("gate_c", [P, 5, TILES])
        half_gain = sb("half_gain", [P, TILES])
        qk = sb("qk", [P, 2 * D])
        qk_rot = sb("qk_rot", [P, 2 * D])
        rot = sb("rot", [P, 4, D])
        v_rows = sb("v_rows", [P, TILES, D])
        prod = sb("prod", [P, GROUP * HEADS * HEAD_DIM])
        score = sb("score", [P, TILES * HEADS, HEADS])
        s_col = sb("s_col", [P, 3, TILES * HEADS])
        o_rows = sb("o_rows", [P, TILES, D])
        hid = ctx.enter_context(nc.psum_tensor("hid", [P, 4, SEQ], F32))
        acc = ctx.enter_context(nc.psum_tensor("acc", [P, KD, SEQ], F32))
        turn = ctx.enter_context(nc.psum_tensor("turn", [P, 2, 512], F32))
        turn_rows = turn[:, :, :].rearrange("p a (b d) -> p (a b) d", d=D)

        norm_step = sem("norm_step")
        y_turned = sem("y_turned")
        y_split = sem("y_split")
        up_done = sem("up_done")
        gelu_done = sem("gelu_done")
        tail_done = sem("g_tail_done")
        down_done = sem("down_done")
        acc_out = sem("acc_out")
        acc_turned = sem("acc_turned")
        x_added = sem("x_added")
        logit_done = sem("logit_done")
        logit_turned = sem("logit_turned")
        gate_step = sem("gate_step")
        gate_exp = sem("gate_exp")
        z_turned = sem("z_turned")
        z_split = sem("z_split")
        qkv_done = sem("qkv_done")
        head_step = sem("head_step")
        head_exp = sem("head_exp")

        DENSE, FRONT, BACK = "dense", "front", "back"
        GROUPS = HEADS // GROUP
        TILE_PIECES = 1 + GROUPS
        SHIFT = TILES * TILE_PIECES
        PIECES = SHIFT + 2 + TILES * GROUPS + 1
        EXP_AT = {DENSE: 20, BACK: 6}
        GAIN_AT = {DENSE: 22, BACK: 8, FRONT: 9, None: 9}

        def slot_of(piece, mode):
            if mode == DENSE:
                return 8 + piece // 2 + (3 if piece > SHIFT else 0)
            return 8 + 5 * piece // 4 + (5 if piece > SHIFT else 0)

        def pieces_at(ht, mode):
            slot = ht + (HID_TILES if mode == BACK else 0)
            return [i for i in range(PIECES) if slot_of(i, mode) == slot] if mode else []

        def qkv_at(ht, mode):
            slot = ht + (HID_TILES if mode == BACK else 0)
            return [t for t in range(TILES) if slot_of(t * TILE_PIECES, mode) == slot + 1] if mode else []

        def pe_stage(pe, n, first=False, mode=None, k_batch=None, z_norm=None, prep=None):
            def up(ht):
                if ht == 0:
                    pe.wait_ge(y_split, 4 * (n + 1))
                if not (first and ht < 4):
                    pe.wait_ge(gelu_done, 2 * (n * HID_TILES + ht - 3))
                cols = slice(ht * P, (ht + 1) * P)
                for k in range(KD):
                    last = split_matmul(pe, hid[:, ht % 4, :], w1_hi[:, k, cols], w1_lo[:, k, cols],
                                        y_hi[:, k, :], y_lo[:, k, :], k == 0, k == KD - 1)
                last.then_inc(up_done, 1)

            def down(ht):
                if ht == 0 and not first:
                    pe.wait_ge(acc_out, 2 * n)
                pe.wait_ge(tail_done, n * HID_TILES + ht + 1)
                for k in range(KD):
                    cols = slice(k * P, (k + 1) * P)
                    last = split_matmul(pe, acc[:, k, :], w2_hi[:, ht, cols], w2_lo[:, ht, cols],
                                        g_hi[:, ht % GBUF, :], g_lo[:, ht % GBUF, :],
                                        ht == 0, ht == HID_TILES - 1)
                last.then_inc(down_done, 1)

            up(0)
            up(1)
            for ht in range(HID_TILES):
                if ht + 2 < HID_TILES:
                    up(ht + 2)
                if ht == 3:
                    pe.wait_ge(gate_step, n * GATE_STEPS + 1)
                down(ht)
                if ht == 0 and not first:
                    turn_acc(pe, n)
                if ht == 2:
                    if not first:
                        pe.wait_ge(x_added, 4 * n)
                    for k in range(KD):
                        last = split_matmul(pe, turn[0:EXPERTS, 0, :], gate_hi[:, k, :], gate_lo[:, k, :],
                                            y_hi[:, k, :], y_lo[:, k, :], k == 0, k == KD - 1)
                    last.then_inc(logit_done, 1)
                if ht == 3:
                    for t in range(TILES):
                        last = pe.transpose(turn[:, 1, t * EXPERTS:(t + 1) * EXPERTS],
                                            logit_rows[:, t * P:(t + 1) * P], ident[0:EXPERTS, 0:EXPERTS])
                    last.then_inc(logit_turned, 1)
                if mode in (DENSE, FRONT) and ht == 5:
                    pe.wait_ge(norm_step, LN_STEPS * (z_norm + 1))
                    pe.wait_ge(gate_step, n * GATE_STEPS + 2)
                    transpose_tiles(pe, y, turn, ident[:, :]).then_inc(z_turned, 1)
                for t in qkv_at(ht, mode):
                    pe.wait_ge(z_split, 4 * (k_batch + 1))
                    if t > 0:
                        pe.wait_ge(head_step, HEAD_STEPS * k_batch + 16 * (t - 1) + 2)
                    for lo, hi, out in ((0, 2 * D, turn[:, 0, :]), (2 * D, QKV, turn[:, 1, 0:D])):
                        for k in range(KD):
                            for a, (zz, ww) in enumerate(((z_hi, wqkv_hi), (z_hi, wqkv_lo), (z_lo, wqkv_hi))):
                                last = pe.matmul(out, zz[:, k, t * P:(t + 1) * P], ww[:, k, lo:hi],
                                                 start=(k == 0 and a == 0), stop=(k == KD - 1 and a == 2))
                    last.then_inc(qkv_done, 1)
            if prep is not None:
                pe.wait_ge(norm_step, LN_STEPS * (prep + 1))
                if mode in (DENSE, FRONT):
                    pe.wait_ge(head_step, HEAD_STEPS * k_batch + 16 * (TILES - 1) + 2)
                else:
                    pe.wait_ge(gate_step, n * GATE_STEPS + 2)
                transpose_tiles(pe, y, turn, ident[:, :]).then_inc(y_turned, 1)

        def turn_acc(pe, n):
            pe.wait_ge(acc_out, 2 * n)
            for t in range(TILES):
                for k in range(KD):
                    last = pe.transpose(turn_rows[:, t, k * P:(k + 1) * P],
                                        acc_sb[:, k, t * P:(t + 1) * P], ident[:, :])
            last.then_inc(acc_turned, 1)

        def copy_acc(act, n):
            act.wait_ge(down_done, n * HID_TILES)
            for k in range(KD):
                act.activation(acc_sb[:, k, :], acc[:, k, :], ACT.Identity, bias=b2_sum[:, k:k + 1],
                               scale=1.0 / WS).then_inc(acc_out, 1)

        def add_stage(dve, n, batch):
            dve.wait_ge(acc_turned, n)
            dve.wait_ge(gate_step, n * GATE_STEPS)
            for t in range(TILES):
                xt = x[:, batch, t, :]
                dve.scalar_tensor_tensor(xt, turn_rows[:, t, :], half_gain[:, t:t + 1], xt,
                                         ALU.mult, ALU.add).then_inc(x_added, 1)

        def gate_logits(dve, n):
            dve.wait_ge(logit_done, n + 1)
            dve.tensor_scalar(logit_rows[:, :], turn[0:EXPERTS, 0, :], 1.0 / WS, gate_bias[:, 0:1],
                              ALU.mult, ALU.add).then_inc(gate_step, 1)

        def gate_norm(dve, n):
            at = n * GATE_STEPS
            ms, r, t4, mx = (gate_c[:, i, :] for i in range(4))
            wide = [P, TILES, EXPERTS]
            dve.wait_ge(logit_turned, n + 1)
            dve.tensor_copy(logit[:, :, :], turn[:, 1, 0:TILES * EXPERTS].rearrange("p (t e) -> p t e", t=TILES)
                            ).then_inc(gate_step, 1)
            dve.wait_ge(gate_step, at + 2)
            dve.tensor_tensor(logit_sq[:, :, :], logit[:, :, :], logit[:, :, :], ALU.mult).then_inc(gate_step, 1)
            dve.wait_ge(gate_step, at + 3)
            dve.tensor_reduce(ms, logit_sq[:, :, :], AX.X, ALU.add).then_inc(gate_step, 1)
            dve.wait_ge(gate_step, at + 4)
            dve.tensor_scalar(ms, ms, 1.0 / EXPERTS, F32_EPS, ALU.mult, ALU.add).then_inc(gate_step, 1)
            rsqrt_newton(dve, gate_step, at + 5, ms, r, t4)
            dve.wait_ge(gate_step, at + 16)
            dve.tensor_tensor(logit[:, :, :], logit[:, :, :], r.unsqueeze(2).to_broadcast(wide),
                              ALU.mult).then_inc(gate_step, 1)
            dve.wait_ge(gate_step, at + 17)
            dve.tensor_tensor(logit[:, :, :], logit[:, :, :], rms_w[:, :].unsqueeze(1).to_broadcast(wide),
                              ALU.mult).then_inc(gate_step, 1)
            dve.wait_ge(gate_step, at + 18)
            dve.tensor_reduce(mx, logit[:, :, :], AX.X, ALU.max).then_inc(gate_step, 1)
            dve.wait_ge(gate_step, at + 19)
            dve.tensor_tensor(logit[:, :, :], logit[:, :, :], mx.unsqueeze(2).to_broadcast(wide),
                              ALU.subtract).then_inc(gate_step, 1)

        def gate_gain(dve, n):
            at = n * GATE_STEPS + 20
            s = gate_c[:, 4, :]
            dve.wait_ge(gate_exp, n + 1)
            dve.tensor_reduce(s, logit[:, :, :], AX.X, ALU.add).then_inc(gate_step, 1)
            dve.wait_ge(gate_step, at + 1)
            dve.tensor_scalar(s, s, 1e-6, 1.0, ALU.mult, ALU.add).then_inc(gate_step, 1)
            dve.wait_ge(gate_step, at + 2)
            dve.reciprocal(s, s).then_inc(gate_step, 1)
            dve.wait_ge(gate_step, at + 3)
            dve.tensor_scalar(half_gain[:, :], s, 0.5, None, ALU.mult).then_inc(gate_step, 1)

        def split_turned(dve, hi, lo, turned, count, split, at):
            dve.wait_ge(turned, count)
            for k in range(KD):
                dve.tensor_copy(hi[:, k, :], turn[:, k, :]).then_inc(split, 1)
            dve.wait_ge(split, at + KD)
            for k in range(KD):
                dve.tensor_tensor(lo[:, k, :], turn[:, k, :], hi[:, k, :], ALU.subtract).then_inc(split, 1)

        def rows_qkv(dve, j, t):
            at = HEAD_STEPS * j + 16 * t
            dve.wait_ge(qkv_done, TILES * j + t + 1)
            dve.scalar_tensor_tensor(qk[:, :], turn[:, 0, :], 1.0 / WS, qkv_bias[:, 0:2 * D],
                                     ALU.mult, ALU.add).then_inc(head_step, 1)
            dve.scalar_tensor_tensor(v_rows[:, t, :], turn[:, 1, 0:D], 1.0 / WS, qkv_bias[:, 2 * D:QKV],
                                     ALU.mult, ALU.add).then_inc(head_step, 1)
            pairs = qk[:, :].rearrange("p (h i two) -> p h i two", i=HEAD_DIM // 2, two=2)
            out = qk_rot[:, :].rearrange("p (h i two) -> p h i two", i=HEAD_DIM // 2, two=2)
            wide = [P, 2 * HEADS, HEAD_DIM // 2]
            cos = rope[:, t, 0, :].unsqueeze(1).to_broadcast(wide)
            sin = rope[:, t, 1, :].unsqueeze(1).to_broadcast(wide)
            r = [rot[:, i, :].rearrange("p (h i) -> p h i", i=HEAD_DIM // 2) for i in range(4)]
            dve.wait_ge(head_step, at + 1)
            for i, (half, table) in enumerate(((0, cos), (1, sin), (0, sin), (1, cos))):
                dve.tensor_tensor(r[i], pairs[:, :, :, half], table, ALU.mult).then_inc(head_step, 1)
            dve.wait_ge(head_step, at + 6)
            dve.tensor_tensor(out[:, :, :, 0], r[0], r[1], ALU.subtract).then_inc(head_step, 1)
            dve.tensor_tensor(out[:, :, :, 1], r[2], r[3], ALU.add).then_inc(head_step, 1)

        
        def rows_score(dve, j, t, g):
            at = HEAD_STEPS * j + 16 * t + 8 + 2 * g
            wide = [P, GROUP, HEADS, HEAD_DIM]
            q4 = qk_rot[:, g * GROUP * HEAD_DIM:(g + 1) * GROUP * HEAD_DIM].rearrange(
                "p (i d) -> p i d", d=HEAD_DIM).unsqueeze(2).to_broadcast(wide)
            k4 = qk_rot[:, D:2 * D].rearrange("p (j d) -> p j d", d=HEAD_DIM).unsqueeze(1).to_broadcast(wide)
            pr = prod[:, :].rearrange("p (i j d) -> p i j d", i=GROUP, j=HEADS)
            dve.wait_ge(head_step, at)
            dve.tensor_tensor(pr, q4, k4, ALU.mult).then_inc(head_step, 1)
            dve.wait_ge(head_step, at + 1)
            row = t * HEADS + g * GROUP
            dve.tensor_reduce(score[:, row:row + GROUP, :], pr, AX.X, ALU.add).then_inc(head_step, 1)

        def score_shift(dve, j):
            at = HEAD_STEPS * j + 64
            dve.wait_ge(head_step, at)
            dve.tensor_reduce(s_col[:, 0, :], score[:, :, :], AX.X, ALU.max).then_inc(head_step, 1)
            dve.wait_ge(head_step, at + 1)
            dve.tensor_tensor(score[:, :, :], score[:, :, :],
                              s_col[:, 0, :].unsqueeze(2).to_broadcast([P, TILES * HEADS, HEADS]),
                              ALU.subtract).then_inc(head_step, 1)

        def score_sum(dve, j):
            at = HEAD_STEPS * j + 66
            dve.wait_ge(head_exp, j + 1)
            dve.tensor_reduce(s_col[:, 1, :], score[:, :, :], AX.X, ALU.add).then_inc(head_step, 1)
            dve.wait_ge(head_step, at + 1)
            dve.reciprocal(s_col[:, 2, :], s_col[:, 1, :]).then_inc(head_step, 1)

        def rows_values(dve, j, t, g):
            at = HEAD_STEPS * j + 68 + 8 * t + 2 * g
            wide = [P, GROUP, HEAD_DIM, HEADS]
            row = t * HEADS + g * GROUP
            e4 = score[:, row:row + GROUP, :].unsqueeze(2).to_broadcast(wide)
            v4 = v_rows[:, t, :].rearrange("p (j d) -> p d j", d=HEAD_DIM).unsqueeze(1).to_broadcast(wide)
            pr = prod[:, :].rearrange("p (i d j) -> p i d j", i=GROUP, d=HEAD_DIM)
            dve.wait_ge(head_step, at)
            dve.tensor_tensor(pr, e4, v4, ALU.mult).then_inc(head_step, 1)
            dve.wait_ge(head_step, at + 1)
            dve.tensor_reduce(o_rows[:, t, g * GROUP * HEAD_DIM:(g + 1) * GROUP * HEAD_DIM].rearrange(
                "p (i d) -> p i d", d=HEAD_DIM), pr, AX.X, ALU.add).then_inc(head_step, 1)

        def add_attention(dve, j):
            at = HEAD_STEPS * j + 100
            heads = o_rows[:, :, :].rearrange("p t (i d) -> p (t i) d", d=HEAD_DIM)
            dve.wait_ge(head_step, at)
            dve.tensor_tensor(heads, heads, s_col[:, 2, :].unsqueeze(2).to_broadcast([P, TILES * HEADS, HEAD_DIM]),
                              ALU.mult).then_inc(head_step, 1)
            dve.wait_ge(head_step, at + 1)
            dve.tensor_tensor(x[:, j, :, :], x[:, j, :, :], o_rows[:, :, :], ALU.add).then_inc(head_step, 1)

        def normalise(dve, q, batch):
            layernorm_batch(dve, norm_step, LN_STEPS * q, x[:, batch, :, :], y, stats, ln_col,
                            var[:, :], rstd[:, :], newton[:, :])

        def head_piece(dve, j, i):
            if i < SHIFT:
                t, part = i // TILE_PIECES, i % TILE_PIECES
                if part == 0:
                    rows_qkv(dve, j, t)
                else:
                    rows_score(dve, j, t, part - 1)
            elif i == SHIFT:
                score_shift(dve, j)
            elif i == SHIFT + 1:
                score_sum(dve, j)
            elif i < PIECES - 1:
                rows_values(dve, j, (i - SHIFT - 2) // GROUPS, (i - SHIFT - 2) % GROUPS)
            else:
                add_attention(dve, j)

        def dve_stage(dve, n, first=False, prev=None, mode=None, k_batch=None, z_norm=None, prep=None):
            if not first:
                dve.wait_ge(up_done, n * HID_TILES)
            split_turned(dve, y_hi, y_lo, y_turned, n + 1, y_split, 4 * n)
            for ht in range(HID_TILES):
                g = ht % GBUF
                if mode in (DENSE, FRONT) and ht == 3:
                    dve.wait_ge(x_added, 4 * n)
                if mode in (DENSE, BACK) and prep is not None and ht == prep[0]:
                    dve.wait_ge(head_step, HEAD_STEPS * (k_batch + 1))
                dve.wait_ge(gelu_done, 2 * (n * HID_TILES + ht + 1))
                if not (first and ht < GBUF):
                    dve.wait_ge(down_done, n * HID_TILES + ht - GBUF + 1)
                dve.tensor_tensor(g_lo[:, g, :], g_full[:, g, :], g_hi[:, g, :],
                                  ALU.subtract).then_inc(tail_done, 1)
                if ht == 1 and not first:
                    add_stage(dve, n, prev)
                if ht == 2:
                    gate_logits(dve, n)
                if ht == 4:
                    gate_norm(dve, n)
                if ht == GAIN_AT[mode]:
                    gate_gain(dve, n)
                if mode in (DENSE, FRONT) and ht == 3:
                    normalise(dve, z_norm, k_batch)
                if mode in (DENSE, FRONT) and ht == 6:
                    split_turned(dve, z_hi, z_lo, z_turned, k_batch + 1, z_split, 4 * k_batch)
                for i in pieces_at(ht, mode):
                    head_piece(dve, k_batch, i)
                if prep is not None and ht == prep[0]:
                    normalise(dve, prep[1], prep[2])

        def act_stage(act, n, first=False, mode=None, k_batch=None):
            if not first:
                copy_acc(act, n)
            for ht in range(HID_TILES):
                g = ht % GBUF
                act.wait_ge(up_done, n * HID_TILES + ht + 1)
                if not (first and ht < GBUF):
                    act.wait_ge(down_done, n * HID_TILES + ht - GBUF + 1)
                for out in (g_full, g_hi):
                    act.activation(out[:, g, :], hid[:, ht % 4, :], ACT.Gelu, bias=b1_col[:, ht:ht + 1],
                                   scale=1.0 / WS).then_inc(gelu_done, 1)
                if ht == EXP_AT.get(mode, 7):
                    act.wait_ge(gate_step, n * GATE_STEPS + 20)
                    act.activation(logit[:, :, :], logit[:, :, :], ACT.Exp, scale=2.0).then_inc(gate_exp, 1)
                    if mode in EXP_AT:
                        act.wait_ge(head_step, HEAD_STEPS * k_batch + 66)
                        act.activation(score[:, :, :], score[:, :, :], ACT.Exp,
                                       scale=float(HEAD_DIM) ** -0.5).then_inc(head_exp, 1)

        LAST = BATCH - 1

        with nc.Block() as block:
            @block.tensor
            def _(pe):
                pe.wait_ge(norm_step, LN_STEPS)
                transpose_tiles(pe, y, turn, ident[:, :]).then_inc(y_turned, 1)
                pe_stage(pe, 0, first=True, prep=1)
                pe_stage(pe, 1, mode=DENSE, k_batch=0, z_norm=2, prep=3)
                with pe.Fori(1, LAST) as k:
                    pe_stage(pe, 2 * k, mode=FRONT, k_batch=k, z_norm=3 * k + 1, prep=3 * k + 2)
                    pe_stage(pe, 2 * k + 1, mode=BACK, k_batch=k, prep=3 * k + 3)
                pe_stage(pe, 2 * LAST, mode=DENSE, k_batch=LAST, z_norm=3 * LAST + 1, prep=3 * LAST + 2)
                pe_stage(pe, 2 * LAST + 1)
                turn_acc(pe, STAGES)

            @block.vector
            def _(dve):
                normalise(dve, 0, 0)
                dve_stage(dve, 0, first=True, prep=(26, 1, 1))
                dve_stage(dve, 1, prev=0, mode=DENSE, k_batch=0, z_norm=2, prep=(HID_TILES - 1, 3, 0))
                with dve.Fori(1, LAST) as k:
                    dve_stage(dve, 2 * k, prev=k, mode=FRONT, k_batch=k, z_norm=3 * k + 1,
                              prep=(28, 3 * k + 2, k + 1))
                    dve_stage(dve, 2 * k + 1, prev=k - 1, mode=BACK, k_batch=k,
                              prep=(29, 3 * k + 3, k))
                dve_stage(dve, 2 * LAST, prev=LAST, mode=DENSE, k_batch=LAST, z_norm=3 * LAST + 1,
                          prep=(HID_TILES - 1, 3 * LAST + 2, LAST))
                dve_stage(dve, 2 * LAST + 1, prev=LAST - 1)
                add_stage(dve, STAGES, LAST)

            @block.scalar
            def _(act):
                act_stage(act, 0, first=True)
                act_stage(act, 1, mode=DENSE, k_batch=0)
                with act.Fori(1, LAST) as k:
                    act_stage(act, 2 * k, mode=FRONT, k_batch=k)
                    act_stage(act, 2 * k + 1, mode=BACK, k_batch=k)
                act_stage(act, 2 * LAST, mode=DENSE, k_batch=LAST)
                act_stage(act, 2 * LAST + 1)
                copy_acc(act, STAGES)


ROWS = 64
TAKEN = ROWS - 1
PAIRS = BATCH // 2
FFN = 1024
ROUTED_EXT = D + 4
SENTINEL = -3.0e38
MASK_FLOOR = -1.0e38
RMS_EPS = 1e-6
TWO_PI_PARTS = (6.28125, 0.0019350051879882812, 3.019916050561733e-07)
ROUND = 1.5 * 2.0 ** 23


def routed_layer(nc, keep, tag, x, ident, io):
    with ExitStack() as ctx:
        def sb(name, shape, dt=F32):
            return ctx.enter_context(nc.sbuf_tensor(f"{tag}_{name}", shape, dt))

        def sem(name):
            return keep.enter_context(nc.semaphore(f"{tag}_{name}"))

        ps = ctx.enter_context(nc.psum_tensor(f"{tag}_ps", [P, 8, 512], F32))
        y = sb("y", [P, BATCH, TILES, ROUTED_EXT])
        one_hot = sb("one_hot", [P, PAIRS, TILES, 2, ROWS])
        slot_hot = sb("slot_hot", [P, PAIRS, TILES, P])
        stay = sb("stay", [P, TILES, BATCH])
        xs = sb("xs", [P, PAIRS, ROUTED_EXT])
        mask_sel = sb("mask_sel", [P, PAIRS, ROWS])
        wqkv = sb("wqkv", [P, KD, QKV])
        wo = sb("wo", [P, KD, D])
        w1 = sb("w1", [P, KD, FFN])
        w2 = sb("w2", [P, FFN // P, D])
        ln1 = sb("ln1", [P, D])
        ln2 = sb("ln2", [P, D])
        inv_freq = sb("inv_freq", [P, HEAD_DIM // 2])
        iota_row = sb("iota_row", [P, ROWS])
        head_block = sb("head_block", [P, 8])
        pair_block = sb("pair_block", [P, 2])

        with ExitStack() as part:
            def tmp(name, shape, dt=F32):
                return part.enter_context(nc.sbuf_tensor(f"{tag}_{name}", shape, dt))

            def tsem(name):
                return keep.enter_context(nc.semaphore(f"{tag}_{name}"))

            router = tmp("router", [P, D])
            router_bias = tmp("router_bias", [P, 1])
            weighed = tmp("weighed", [P, TILES, D])
            w_col = tmp("w_col", [P, BATCH, TILES])
            w_row = tmp("w_row", [BATCH, SEQ])
            work = tmp("work", [BATCH, SEQ])
            best = tmp("best", [BATCH, 8])
            row = tmp("row", [BATCH, 6, SEQ])
            last_at = tmp("last_at", [BATCH, 1])
            slot_col = tmp("slot_col", [P, TILES, BATCH])
            pos_rows = tmp("pos_rows", [16, P], I32)
            pos_rows_f = tmp("pos_rows_f", [16, P])
            mask_idx = tmp("mask_idx", [P, PAIRS], I32)
            mask_rows = tmp("mask_rows", [P, PAIRS, SEQ])
            mask_t = tmp("mask_t", [P, TILES, P])
            stats = tmp("stats", [P, TILES, 6])
            ln_col = tmp("ln_col", [P, 4, TILES])
            var = tmp("var", [P, TILES])
            rstd = tmp("rstd", [P, TILES])
            newton = tmp("newton", [P, TILES])

            small_in = tsem("small_in")
            weights_in = sem("weights_in")
            made = tsem("made")
            norm_step = tsem("norm_step")
            rows_turned = tsem("rows_turned")
            pick_step = tsem("pick_step")
            cols_turned = tsem("cols_turned")
            hot_step = tsem("hot_step")
            gathered = tsem("gathered")
            sel_out = tsem("sel_out")
            hot_turned = tsem("hot_turned")
            hot_out = tsem("hot_out")
            mask_in = [tsem(f"mask_in{i}") for i in range(PAIRS)]
            mask_turned = tsem("mask_turned")
            mask_out = tsem("mask_out")
            mask_picked = tsem("mask_picked")
            mask_done = tsem("mask_done")

            BATCH_STEPS = LN_STEPS + 2
            MASK_BATCHES = 4
            idx_row = row[:, 0, :]
            ones_row = row[:, 1, :]

            with nc.Block() as block:
                @block.sync
                def _(sp):
                    for name in ("router_w",):
                        sp.dma_start(router[:, :], io["router_w"].rearrange("d o -> (d o)").partition_broadcast(P)).then_inc(small_in, 16)
                    sp.dma_start(router_bias[:, :], io["router_b"].partition_broadcast(P)).then_inc(small_in, 16)
                    sp.dma_start(pos_rows[:, :], io["position_ids"][:, 0:SEQ].rearrange("b (t p) -> b t p", p=P)
                                 ).then_inc(small_in, 16)
                    for i, name in enumerate(("wq", "wk", "wv")):
                        sp.dma_start(wqkv[:, :, i * D:(i + 1) * D], io[name].rearrange("(k p) n -> p k n", p=P)).then_inc(weights_in, 16)
                    sp.dma_start(wo[:, :, :], io["wo"].rearrange("(k p) n -> p k n", p=P)).then_inc(weights_in, 16)
                    sp.dma_start(w1[:, :, :], io["w1"].rearrange("(k p) n -> p k n", p=P)).then_inc(weights_in, 16)
                    sp.dma_start(w2[:, :, :], io["w2"].rearrange("(f p) n -> p f n", p=P)).then_inc(weights_in, 16)
                    sp.dma_start(ln1[:, :], io["ln1"].partition_broadcast(P)).then_inc(weights_in, 16)
                    sp.dma_start(ln2[:, :], io["ln2"].partition_broadcast(P)).then_inc(weights_in, 16)
                    sp.dma_start(inv_freq[:, :], io["inv_freq"].partition_broadcast(P)).then_inc(weights_in, 16)

                @block.gpsimd
                def _(pool):
                    pool.iota(iota_row[:, :], pattern=[[1, ROWS]], base=0, channel_multiplier=0,
                              allow_small_or_imprecise_dtypes=True).then_inc(made, 1)
                    pool.iota(idx_row, pattern=[[1, SEQ]], base=1, channel_multiplier=0,
                              allow_small_or_imprecise_dtypes=True).then_inc(made, 1)
                    pool.memset(ones_row, 1.0).then_inc(made, 1)
                    for b in range(BATCH):
                        pool.iota(y[:, b, :, D + 2], pattern=[[P, TILES]], base=min(b, MASK_BATCHES - 1) * 1024,
                                  channel_multiplier=1, allow_small_or_imprecise_dtypes=True).then_inc(made, 1)
                    pool.memset(y[:, :, :, D + 3], 0.0).then_inc(made, 1)
                    pool.memset(head_block[:, :], 1.0).then_inc(made, 1)
                    pool.memset(pair_block[:, :], 1.0).then_inc(made, 1)
                    for m, width, n in ((head_block, HEAD_DIM, 8), (pair_block, ROWS, 2)):
                        pool.wait_ge(made, 14 if m is head_block else 16)
                        pool.affine_select(out=m[:, :], in_=m[:, :], compare_op=ALU.is_ge, fill=0.0, base=0,
                                           pattern=[[-width, n]], channel_multiplier=1).then_inc(made, 1)
                        pool.wait_ge(made, 15 if m is head_block else 17)
                        pool.affine_select(out=m[:, :], in_=m[:, :], compare_op=ALU.is_ge, fill=0.0, base=width - 1,
                                           pattern=[[width, n]], channel_multiplier=-1).then_inc(made, 1)
                    mask_view = io["attention_mask"].rearrange("b o q (h k) -> (b o q h) k", k=SEQ)
                    for pr in range(PAIRS):
                        pool.wait_ge(sel_out, 2 * (pr + 1))
                        pool.indirect_dma_start(out=mask_rows[:, pr, :], out_offset=None, in_=mask_view,
                                                in_offset=bass.IndirectOffsetOnAxis(ap=mask_idx[:, pr:pr + 1], axis=0)
                                                ).then_inc(mask_in[pr], 16)

                @block.vector
                def _(dve):
                    dve.wait_ge(small_in, 48)
                    dve.tensor_copy(pos_rows_f[:, :], pos_rows[:, :]).then_inc(hot_step, 1)
                    with dve.Fori(0, BATCH) as b:
                        yb = y[:, b, :, 0:D]
                        layernorm_batch(dve, norm_step, b * BATCH_STEPS, x[:, b, :, :], yb, stats, ln_col,
                                        var[:, :], rstd[:, :], newton[:, :])
                        dve.wait_ge(norm_step, b * BATCH_STEPS + LN_STEPS)
                        dve.tensor_tensor(weighed[:, :, :], yb, router[:, :].unsqueeze(1).to_broadcast([P, TILES, D]),
                                          ALU.mult).then_inc(norm_step, 1)
                        dve.wait_ge(norm_step, b * BATCH_STEPS + LN_STEPS + 1)
                        dve.tensor_reduce(w_col[:, b, :], weighed[:, :, :], AX.X, ALU.add).then_inc(norm_step, 1)
                    dve.wait_ge(norm_step, BATCH * BATCH_STEPS)
                    dve.tensor_scalar(w_col[:, :, :], w_col[:, :, :], router_bias[:, 0:1], None,
                                      ALU.add).then_inc(norm_step, 1)
                    dve.wait_ge(norm_step, BATCH * BATCH_STEPS + 1)
                    dve.wait_ge(made, 18)
                    dve.tensor_copy(y[:, :, :, D], w_col[:, :, :]).then_inc(hot_step, 1)
                    dve.wait_ge(cols_turned, 1)
                    pos_cols = ps[:, 1, 0:16].rearrange("p (b t) -> p b t", t=TILES)
                    dve.tensor_copy(y[:, 0:MASK_BATCHES, :, D + 1], pos_cols).then_inc(hot_step, 1)
                    dve.tensor_copy(y[:, MASK_BATCHES:BATCH, :, D + 1],
                                    pos_cols[:, MASK_BATCHES - 1:MASK_BATCHES, :].to_broadcast(
                                        [P, BATCH - MASK_BATCHES, TILES])).then_inc(hot_step, 1)
                    dve.wait_ge(rows_turned, 1)
                    dve.tensor_copy(w_row[:, :], ps[0:BATCH, 0, :]).then_inc(pick_step, 1)
                    dve.wait_ge(pick_step, 1)
                    dve.tensor_copy(work[:, :], w_row[:, :]).then_inc(pick_step, 1)
                    for r in range(ROWS // 8):
                        dve.wait_ge(pick_step, 2 + 2 * r)
                        dve.max(best[:, :], work[:, :]).then_inc(pick_step, 1)
                        dve.wait_ge(pick_step, 3 + 2 * r)
                        dve.match_replace(out=work[:, :], in_to_replace=best[:, :], in_values=work[:, :],
                                          imm_value=SENTINEL).then_inc(pick_step, 1)
                    at = 2 + 2 * (ROWS // 8)
                    least = best[:, 7:8]
                    taken, tied, cum = row[:, 2, :], row[:, 3, :], row[:, 4, :]
                    slot, pass_row = row[:, 5, :], row[:, 3, :]
                    dve.wait_ge(pick_step, at)
                    dve.tensor_scalar(taken, work[:, :], SENTINEL, None, ALU.is_equal).then_inc(pick_step, 1)
                    dve.wait_ge(pick_step, at + 1)
                    dve.scalar_tensor_tensor(tied, w_row[:, :], least, taken, ALU.is_equal, ALU.mult).then_inc(pick_step, 1)
                    dve.wait_ge(pick_step, at + 2)
                    dve.tensor_tensor(tied, tied, idx_row, ALU.mult).then_inc(pick_step, 1)
                    dve.wait_ge(pick_step, at + 3)
                    dve.tensor_reduce(last_at[:, :], tied, AX.X, ALU.max).then_inc(pick_step, 1)
                    dve.wait_ge(pick_step, at + 4)
                    dve.scalar_tensor_tensor(taken, idx_row, last_at[:, 0:1], taken, ALU.not_equal,
                                             ALU.mult).then_inc(pick_step, 1)
                    dve.wait_ge(pick_step, at + 5)
                    dve.tensor_tensor_scan(cum, ones_row, taken, 0.0, ALU.mult, ALU.add).then_inc(pick_step, 1)
                    dve.wait_ge(pick_step, at + 6)
                    dve.tensor_tensor(slot, cum, taken, ALU.mult).then_inc(pick_step, 1)
                    dve.wait_ge(pick_step, at + 7)
                    dve.tensor_scalar(slot, slot, -1.0, None, ALU.add).then_inc(pick_step, 1)
                    dve.tensor_scalar(pass_row, w_row[:, :], least, 0.5, ALU.is_le, ALU.mult).then_inc(pick_step, 1)
                    dve.wait_ge(cols_turned, 2)
                    dve.tensor_copy(slot_col[:, :, :], ps[:, 2, 0:TILES * BATCH].rearrange("p (t b) -> p t b", b=BATCH)
                                    ).then_inc(hot_step, 1)
                    dve.tensor_copy(stay[:, :, :], ps[:, 2, 64:64 + TILES * BATCH].rearrange("p (t b) -> p t b", b=BATCH)
                                    ).then_inc(hot_step, 1)
                    dve.wait_ge(hot_step, 6)
                    for b in range(BATCH):
                        dve.tensor_tensor(one_hot[:, b // 2, :, b % 2, :],
                                          iota_row[:, :].unsqueeze(1).to_broadcast([P, TILES, ROWS]),
                                          slot_col[:, :, b:b + 1].to_broadcast([P, TILES, ROWS]),
                                          ALU.is_equal).then_inc(hot_step, 1)
                    for pr in range(PAIRS):
                        dve.wait_ge(gathered, pr + 1)
                        dve.tensor_copy(xs[:, pr, :], ps[:, 3 + pr, 0:ROUTED_EXT]).then_inc(sel_out, 1)
                        dve.tensor_scalar(mask_idx[:, pr:pr + 1], ps[:, 3 + pr, D + 2:D + 3], 2.0, None,
                                          ALU.mult).then_inc(sel_out, 1)
                    for pr in range(PAIRS):
                        dve.wait_ge(mask_turned, pr + 1)
                        if pr > 0:
                            dve.wait_ge(mask_picked, pr)
                        dve.tensor_scalar(mask_t[:, :, :], ps[:, 3 + pr % 2, :].rearrange("p (t r) -> p t r", t=TILES),
                                          MASK_FLOOR, None, ALU.max).then_inc(mask_out, 1)
                        dve.wait_ge(mask_picked, pr + 1)
                        dve.tensor_copy(mask_sel[:, pr, :], ps[:, 5 + pr % 2, 0:ROWS]).then_inc(mask_done, 1)
                    dve.wait_ge(mask_done, PAIRS)
                    dve.memset(mask_sel[:, :, TAKEN:ROWS], SENTINEL)

                @block.tensor
                def _(pe):
                    pe.wait_ge(hot_step, 1)
                    pe.transpose(ps[:, 1, 0:16], pos_rows_f[:, :], ident[0:16, 0:16]).then_inc(cols_turned, 1)
                    pe.wait_ge(norm_step, BATCH * BATCH_STEPS + 1)
                    for t in range(TILES):
                        last = pe.transpose(ps[0:BATCH, 0, t * P:(t + 1) * P], w_col[:, :, t], ident[:, :])
                    last.then_inc(rows_turned, 1)
                    pe.wait_ge(pick_step, 2 + 2 * (ROWS // 8) + 9)
                    for i, r in ((0, 5), (1, 3)):
                        for t in range(TILES):
                            at = 64 * i + t * BATCH
                            last = pe.transpose(ps[:, 2, at:at + BATCH], row[:, r, t * P:(t + 1) * P],
                                                ident[0:BATCH, 0:BATCH])
                    last.then_inc(cols_turned, 1)
                    for pr in range(PAIRS):
                        pe.wait_ge(hot_step, 6 + 2 * (pr + 1))
                        for i in range(2):
                            for t in range(TILES):
                                last = pe.matmul(ps[i * ROWS:(i + 1) * ROWS, 3 + pr, 0:ROUTED_EXT],
                                                 one_hot[:, pr, t, i, :], y[:, 2 * pr + i, t, :],
                                                 start=(t == 0), stop=(t == TILES - 1))
                        last.then_inc(gathered, 1)
                    for pr in range(PAIRS):
                        bank = (7, 0)[pr % 2]
                        if pr >= 2:
                            pe.wait_ge(hot_out, pr - 1)
                        for t in range(TILES):
                            last = pe.transpose(ps[:, bank, t * P:(t + 1) * P],
                                                one_hot[:, pr, t, :, :].rearrange("p i r -> p (i r)"), ident[:, :])
                        last.then_inc(hot_turned, 1)
                    for pr in range(PAIRS):
                        pe.wait_ge(mask_in[pr], 16)
                        if pr == 0:
                            pe.wait_ge(sel_out, 2 * PAIRS)
                        if pr >= 2:
                            pe.wait_ge(mask_done, pr - 1)
                        for t in range(TILES):
                            last = pe.transpose(ps[:, 3 + pr % 2, t * P:(t + 1) * P],
                                                mask_rows[:, pr, t * P:(t + 1) * P], ident[:, :])
                        last.then_inc(mask_turned, 1)
                        pe.wait_ge(mask_out, pr + 1)
                        for i in range(2):
                            for t in range(TILES):
                                last = pe.matmul(ps[i * ROWS:(i + 1) * ROWS, 5 + pr % 2, 0:ROWS],
                                                 mask_t[:, t, i * ROWS:(i + 1) * ROWS], one_hot[:, pr, t, i, :],
                                                 start=(t == 0), stop=(t == TILES - 1))
                        last.then_inc(mask_picked, 1)

                @block.scalar
                def _(act):
                    for pr in range(PAIRS):
                        act.wait_ge(hot_turned, pr + 1)
                        act.activation(slot_hot[:, pr, :, :].rearrange("p t n -> p (t n)"),
                                       ps[:, (7, 0)[pr % 2], :], ACT.Copy).then_inc(hot_out, 1)

        h = sb("h", [P, PAIRS, D])
        h_t = sb("h_t", [P, KD, PAIRS * P])
        sq = sb("sq", [P, PAIRS, D])
        col = sb("col", [P, 4, PAIRS])
        ang = sb("ang", [P, 4, PAIRS * HEAD_DIM // 2])
        rope = sb("rope", [P, 2, PAIRS, HEAD_DIM // 2])
        rot = sb("rot", [P, 4, D])
        qk = sb("qk", [P, 2, 2 * D])
        q_t = sb("q_t", [P, 2, KD, P])
        k_blk = sb("k_blk", [P, 2, KD, 2, 8, ROWS])
        v_blk = sb("v_blk", [P, BATCH, 8, 2, HEAD_DIM])
        s = sb("s", [P, 2, HEADS, ROWS])
        s_col = sb("s_col", [P, 2, 3, HEADS])
        p_t = sb("p_t", [P, 2, 8, P])
        o = sb("o", [P, 2, D])
        o_t = sb("o_t", [P, 2, KD, P])
        x1 = sb("x1", [P, PAIRS, D])
        gel = sb("gel", [P, FFN // P, PAIRS * P])
        proc = sb("proc", [P, PAIRS, D])

        rms_step = sem("rms_step")
        h_turned = sem("h_turned")
        h_out = sem("h_out")
        qk_done = sem("qk_done")
        v_done = sem("v_done")
        v_out = sem("v_out")
        ang_step = sem("ang_step")
        sin_done = sem("sin_done")
        rot_step = sem("rot_step")
        qk_turned = sem("qk_turned")
        qt_out = sem("qt_out")
        kb_out = sem("kb_out")
        s_done = sem("s_done")
        s_step = sem("s_step")
        s_exp = sem("s_exp")
        p_turned = sem("p_turned")
        p_out = sem("p_out")
        o_done = sem("o_done")
        o_out = sem("o_out")
        o_turned = sem("o_turned")
        ot_out = sem("ot_out")
        wo_done = sem("wo_done")
        x1_out = sem("x1_out")
        up_done = sem("up_done")
        gel_out = sem("gel_out")
        down_done = sem("down_done")
        proc_step = sem("proc_step")
        put_done = sem("put_done")
        passed = sem("passed")
        put_out = sem("put_out")

        RMS_STEPS = 3 + RSQRT_STEPS + PAIRS

        def rmsnorm(dve, call, src, gain, bank_src=None):
            at = call * RMS_STEPS
            dve.tensor_tensor(sq[:, :, :], src, src, ALU.mult).then_inc(rms_step, 1)
            dve.wait_ge(rms_step, at + 1)
            dve.tensor_reduce(col[:, 0, :], sq[:, :, :], AX.X, ALU.add).then_inc(rms_step, 1)
            dve.wait_ge(rms_step, at + 2)
            dve.tensor_scalar(col[:, 0, :], col[:, 0, :], 1.0 / D, RMS_EPS, ALU.mult, ALU.add).then_inc(rms_step, 1)
            rsqrt_newton(dve, rms_step, at + 3, col[:, 0, :], col[:, 1, :], col[:, 2, :])
            dve.wait_ge(rms_step, at + 3 + RSQRT_STEPS)
            for pr in range(PAIRS):
                dve.scalar_tensor_tensor(h[:, pr, :], src[:, pr, :], col[:, 1, pr:pr + 1], gain[:, :],
                                         ALU.mult, ALU.mult).then_inc(rms_step, 1)

        def angles(dve):
            n = PAIRS * HEAD_DIM // 2
            a, k, r = ang[:, 0, :], ang[:, 1, :], ang[:, 2:4, :]
            dve.tensor_tensor(a.rearrange("p (r i) -> p r i", r=PAIRS),
                              xs[:, :, D + 1:D + 2].to_broadcast([P, PAIRS, HEAD_DIM // 2]),
                              inv_freq[:, :].unsqueeze(1).to_broadcast([P, PAIRS, HEAD_DIM // 2]),
                              ALU.mult).then_inc(ang_step, 1)
            at = 1
            for i, quarter in enumerate((0.0, 0.25)):
                dve.wait_ge(ang_step, at)
                dve.tensor_scalar(k, a, float(1.0 / (2.0 * np.pi)), quarter, ALU.mult, ALU.add).then_inc(ang_step, 1)
                dve.wait_ge(ang_step, at + 1)
                dve.tensor_scalar(k, k, ROUND, None, ALU.add).then_inc(ang_step, 1)
                dve.wait_ge(ang_step, at + 2)
                dve.tensor_scalar(k, k, ROUND, None, ALU.subtract).then_inc(ang_step, 1)
                src = a
                for m, part in enumerate(TWO_PI_PARTS):
                    dve.wait_ge(ang_step, at + 3 + m)
                    dve.scalar_tensor_tensor(r[:, i, :], k, -part, src, ALU.mult, ALU.add).then_inc(ang_step, 1)
                    src = r[:, i, :]
                dve.wait_ge(ang_step, at + 6)
                dve.tensor_scalar(r[:, i, :], r[:, i, :], float(np.pi / 2) * i, float(np.float32(np.pi)) * (1 - 1e-7),
                                  ALU.add, ALU.min).then_inc(ang_step, 1)
                dve.wait_ge(ang_step, at + 7)
                dve.tensor_scalar(r[:, i, :], r[:, i, :], -float(np.float32(np.pi)) * (1 - 1e-7), None,
                                  ALU.max).then_inc(ang_step, 1)
                at += 8

        ANG_STEPS = 1 + 16

        def scores(pe, pr):
            lo = (6, 0)[pr % 2]
            if pr < 2:
                pe.wait_ge(v_out, (4, 8)[pr])
            else:
                pe.wait_ge(s_step, 6 * (pr - 2) + 2)
            pe.wait_ge(qt_out, pr + 1)
            pe.wait_ge(kb_out, 4 * (pr + 1))
            for half in range(KD):
                for i in range(2):
                    last = pe.matmul(ps[i * ROWS:(i + 1) * ROWS, lo + half, :],
                                     q_t[:, pr % 2, half, i * ROWS:(i + 1) * ROWS],
                                     k_blk[:, pr % 2, half, i, :, :].rearrange("p h c -> p (h c)"),
                                     start=True, stop=True)
            last.then_inc(s_done, 1)

        def values(pe, pr):
            lo = 2
            pe.wait_ge(s_exp, pr + 1)
            pe.wait_ge(qt_out, 2)
            if pr >= 1:
                pe.wait_ge(x1_out, pr)
            for m in range(8):
                last = pe.transpose(ps[:, lo + m // 4, (m % 4) * P:(m % 4 + 1) * P],
                                    s[:, pr % 2, 2 * m:2 * m + 2, :].rearrange("p h c -> p (h c)"), ident[:, :])
            last.then_inc(p_turned, 1)
            pe.wait_ge(p_out, 2 * (pr + 1))
            for i in range(2):
                for m in range(8):
                    last = pe.matmul(ps[i * ROWS:(i + 1) * ROWS, lo, m * 32:(m + 1) * 32],
                                     p_t[:, pr % 2, m, i * ROWS:(i + 1) * ROWS],
                                     v_blk[:, 2 * pr + i, m, :, :].rearrange("p h d -> p (h d)"),
                                     start=True, stop=True)
            last.then_inc(o_done, 1)
            pe.wait_ge(o_out, pr + 1)
            for k in range(KD):
                last = pe.transpose(ps[:, lo + 1, k * P:(k + 1) * P], o[:, pr % 2, k * P:(k + 1) * P], ident[:, :])
            last.then_inc(o_turned, 1)
            pe.wait_ge(ot_out, pr + 1)
            for k in range(KD):
                last = pe.matmul(ps[:, lo, D:2 * D], o_t[:, pr % 2, k, :], wo[:, k, :],
                                 start=(k == 0), stop=(k == KD - 1))
            last.then_inc(wo_done, 1)

        def rotate(dve, pr):
            half = HEAD_DIM // 2
            wide = [P, 2 * HEADS, half]
            src = ps[:, 2 + pr, :].rearrange("p (h two i) -> p h two i", two=2, i=half)
            out = qk[:, pr % 2, :].rearrange("p (h two i) -> p h two i", two=2, i=half)
            cos = rope[:, 1, pr, :].unsqueeze(1).to_broadcast(wide)
            sin = rope[:, 0, pr, :].unsqueeze(1).to_broadcast(wide)
            r = [rot[:, m, :].rearrange("p (h i) -> p h i", i=half) for m in range(4)]
            dve.wait_ge(qk_done, pr + 1)
            if pr > 0:
                dve.wait_ge(rot_step, 6 * pr)
            for m, (a, table) in enumerate(((0, cos), (1, sin), (0, sin), (1, cos))):
                dve.tensor_tensor(r[m], src[:, :, a, :], table, ALU.mult).then_inc(rot_step, 1)
            dve.wait_ge(rot_step, 6 * pr + 4)
            if pr >= 2:
                dve.wait_ge(qk_turned, pr - 1)
            dve.tensor_tensor(out[:, :, 0, :], r[0], r[1], ALU.subtract).then_inc(rot_step, 1)
            dve.tensor_tensor(out[:, :, 1, :], r[2], r[3], ALU.add).then_inc(rot_step, 1)

        def key_blocks(dve, pr):
            dve.wait_ge(qk_turned, pr + 1)
            if pr >= 2:
                dve.wait_ge(s_done, pr - 1)
            for half in range(KD):
                for i in range(2):
                    at = (2 + half) * P + i * ROWS
                    dve.tensor_tensor(k_blk[:, pr % 2, half, i, :, :],
                                      ps[:, 2 + pr, at:at + ROWS].unsqueeze(1).to_broadcast([P, 8, ROWS]),
                                      head_block[:, :].unsqueeze(2).to_broadcast([P, 8, ROWS]),
                                      ALU.mult).then_inc(kb_out, 1)

        def softmax_and_out(dve, pr):
            lo = (6, 0)[pr % 2]
            at = 6 * pr
            sv = s[:, pr % 2, :, :]
            mx, total, inv = (s_col[:, pr % 2, m, :] for m in range(3))
            dve.wait_ge(s_done, pr + 1)
            if pr >= 2:
                dve.wait_ge(p_turned, pr - 1)
            for half in range(KD):
                dve.scalar_tensor_tensor(sv[:, half * 8:(half + 1) * 8, :],
                                         ps[:, lo + half, :].rearrange("p (h c) -> p h c", c=ROWS), 0.25,
                                         mask_sel[:, pr, :].unsqueeze(1).to_broadcast([P, 8, ROWS]),
                                         ALU.mult, ALU.add).then_inc(s_step, 1)
            dve.wait_ge(s_step, at + 2)
            dve.tensor_reduce(mx, sv, AX.X, ALU.max).then_inc(s_step, 1)
            dve.wait_ge(s_step, at + 3)
            dve.tensor_tensor(sv, sv, mx.unsqueeze(2).to_broadcast([P, HEADS, ROWS]), ALU.subtract).then_inc(s_step, 1)
            dve.wait_ge(s_exp, pr + 1)
            dve.tensor_reduce(total, sv, AX.X, ALU.add).then_inc(s_step, 1)
            dve.wait_ge(s_step, at + 5)
            dve.reciprocal(inv, total).then_inc(s_step, 1)
            dve.wait_ge(o_done, pr + 1)
            dve.wait_ge(s_step, at + 6)
            bank = 2
            dve.tensor_tensor(o[:, pr % 2, :].rearrange("p (h d) -> p h d", d=HEAD_DIM),
                              ps[:, bank, 0:D].rearrange("p (h d) -> p h d", d=HEAD_DIM),
                              inv.unsqueeze(2).to_broadcast([P, HEADS, HEAD_DIM]), ALU.mult).then_inc(o_out, 1)
            dve.wait_ge(wo_done, pr + 1)
            dve.tensor_tensor(x1[:, pr, :], ps[:, bank, D:2 * D], xs[:, pr, 0:D], ALU.add).then_inc(x1_out, 1)

        with nc.Block() as block:
            @block.tensor
            def _(pe):
                def turn_h(call, count):
                    pe.wait_ge(rms_step, count)
                    for k in range(KD):
                        for pr in range(PAIRS):
                            last = pe.transpose(ps[:, k, pr * P:(pr + 1) * P], h[:, pr, k * P:(k + 1) * P], ident[:, :])
                    last.then_inc(h_turned, 1)

                turn_h(0, RMS_STEPS)
                pe.wait_ge(h_out, 2)
                pe.wait_ge(weights_in, 16 * 9)
                for pr in range(PAIRS):
                    for k in range(KD):
                        last = pe.matmul(ps[:, 2 + pr, :], h_t[:, k, pr * P:(pr + 1) * P], wqkv[:, k, 0:2 * D],
                                         start=(k == 0), stop=(k == KD - 1))
                    last.then_inc(qk_done, 1)
                for pr in range(PAIRS):
                    bank = (6, 7, 0, 1)[pr]
                    for i in range(2):
                        at = (2 * pr + i) * ROWS
                        for c in range(2):
                            for k in range(KD):
                                last = pe.matmul(ps[c * ROWS:(c + 1) * ROWS, bank, i * D:(i + 1) * D],
                                                 h_t[:, k, at:at + ROWS], wqkv[:, k, 2 * D:QKV],
                                                 start=(k == 0), stop=(k == KD - 1))
                    last.then_inc(v_done, 1)
                for pr in range(PAIRS):
                    pe.wait_ge(rot_step, 6 * (pr + 1))
                    for m in range(4):
                        last = pe.transpose(ps[:, 2 + pr, m * P:(m + 1) * P], qk[:, pr % 2, m * P:(m + 1) * P], ident[:, :])
                    last.then_inc(qk_turned, 1)
                    scores(pe, pr)
                    if pr >= 1:
                        values(pe, pr - 1)
                values(pe, PAIRS - 1)
                turn_h(1, 2 * RMS_STEPS)
                pe.wait_ge(h_out, 4)
                for f in range(FFN // P):
                    if f >= 4:
                        pe.wait_ge(gel_out, f - 3)
                    for k in range(KD):
                        last = pe.matmul(ps[:, 2 + f % 4, :], w1[:, k, f * P:(f + 1) * P], h_t[:, k, :],
                                         start=(k == 0), stop=(k == KD - 1))
                    last.then_inc(up_done, 1)
                for pr in range(PAIRS):
                    for f in range(FFN // P):
                        if pr == 0:
                            pe.wait_ge(gel_out, f + 1)
                        last = pe.matmul(ps[:, (6, 7, 0, 1)[pr], 0:D], gel[:, f, pr * P:(pr + 1) * P],
                                         w2[:, f, :], start=(f == 0), stop=(f == FFN // P - 1))
                    last.then_inc(down_done, 1)
                for b in range(BATCH):
                    pr, i = b // 2, b % 2
                    pe.wait_ge(proc_step, 2 * (pr + 1))
                    if b >= 2:
                        pe.wait_ge(put_out, b - 1)
                    for t in range(TILES):
                        last = pe.matmul(ps[:, 2 + 2 * (b % 2) + t // 2, (t % 2) * D:(t % 2 + 1) * D],
                                         slot_hot[i * ROWS:(i + 1) * ROWS, pr, t, :], proc[i * ROWS:(i + 1) * ROWS, pr, :],
                                         start=True, stop=True)
                    last.then_inc(put_done, 1)

            @block.vector
            def _(dve):
                dve.wait_ge(weights_in, 16 * 9)
                rmsnorm(dve, 0, xs[:, :, 0:D], ln1)
                angles(dve)
                for b in range(BATCH):
                    pr, i = b // 2, b % 2
                    dve.wait_ge(v_done, pr + 1)
                    src = ps[:, (6, 7, 0, 1)[pr], i * D:(i + 1) * D].rearrange("p (m h d) -> p m h d", m=8, h=2)
                    dve.tensor_tensor(v_blk[:, b, :, :, :], src,
                                      pair_block[:, :].unsqueeze(1).unsqueeze(3).to_broadcast([P, 8, 2, HEAD_DIM]),
                                      ALU.mult).then_inc(v_out, 1)
                dve.wait_ge(sin_done, 1)
                for pr in range(PAIRS):
                    rotate(dve, pr)
                    key_blocks(dve, pr)
                    if pr >= 1:
                        softmax_and_out(dve, pr - 1)
                softmax_and_out(dve, PAIRS - 1)
                dve.wait_ge(x1_out, PAIRS)
                rmsnorm(dve, 1, x1[:, :, :], ln2)
                for pr in range(PAIRS):
                    dve.wait_ge(down_done, pr + 1)
                    dve.tensor_tensor(proc[:, pr, :], ps[:, (6, 7, 0, 1)[pr], 0:D], x1[:, pr, :],
                                      ALU.add).then_inc(proc_step, 1)
                    dve.wait_ge(proc_step, 2 * pr + 1)
                    dve.tensor_scalar(proc[:, pr, :], proc[:, pr, :], xs[:, pr, D:D + 1], None,
                                      ALU.mult).then_inc(proc_step, 1)
                for b in range(BATCH):
                    for t in range(TILES):
                        xt = x[:, b, t, :]
                        dve.scalar_tensor_tensor(xt, y[:, b, t, 0:D], stay[:, t, b:b + 1], xt,
                                                 ALU.mult, ALU.add).then_inc(passed, 1)
                    dve.wait_ge(put_done, b + 1)
                    dve.wait_ge(passed, TILES * (b + 1))
                    two = 2 + 2 * (b % 2)
                    dve.scalar_tensor_tensor(x[:, b, :, :].rearrange("p t d -> p (t d)"),
                                             ps[:, two:two + 2, :].rearrange("p a n -> p (a n)"), 0.5,
                                             x[:, b, :, :].rearrange("p t d -> p (t d)"),
                                             ALU.mult, ALU.add).then_inc(put_out, 1)

            @block.scalar
            def _(act):
                def h_copy(call):
                    act.wait_ge(h_turned, call + 1)
                    for k in range(KD):
                        act.activation(h_t[:, k, :], ps[:, k, :], ACT.Copy).then_inc(h_out, 1)

                def values_copies(pr):
                    lo = 2
                    act.wait_ge(s_step, 6 * pr + 4)
                    sv = s[:, pr % 2, :, :]
                    act.activation(sv, sv, ACT.Exp).then_inc(s_exp, 1)
                    act.wait_ge(p_turned, pr + 1)
                    for m in range(2):
                        act.activation(p_t[:, pr % 2, 4 * m:4 * m + 4, :].rearrange("p m n -> p (m n)"),
                                       ps[:, lo + m, :], ACT.Copy).then_inc(p_out, 1)
                    act.wait_ge(o_turned, pr + 1)
                    act.activation(o_t[:, pr % 2, :, :].rearrange("p k n -> p (k n)"), ps[:, lo + 1, 0:D],
                                   ACT.Copy).then_inc(ot_out, 1)

                h_copy(0)
                act.wait_ge(ang_step, ANG_STEPS)
                act.activation(rope[:, :, :, :].rearrange("p c r i -> p (c r i)"),
                               ang[:, 2:4, :].rearrange("p c n -> p (c n)"), ACT.Sin).then_inc(sin_done, 1)
                for pr in range(PAIRS):
                    act.wait_ge(kb_out, 4 * (pr + 1))
                    if pr >= 2:
                        act.wait_ge(s_done, pr - 1)
                    act.activation(q_t[:, pr % 2, :, :].rearrange("p k n -> p (k n)"), ps[:, 2 + pr, 0:2 * P],
                                   ACT.Copy).then_inc(qt_out, 1)
                    if pr >= 1:
                        values_copies(pr - 1)
                values_copies(PAIRS - 1)
                h_copy(1)
                for f in range(FFN // P):
                    act.wait_ge(up_done, f + 1)
                    act.activation(gel[:, f, :], ps[:, 2 + f % 4, :], ACT.Gelu_apprx_tanh).then_inc(gel_out, 1)


BF16 = mybir.dt.bfloat16
LATENT = 64
MLA_HEADS, MLA_DIM = 16, 64
MLA_PAIRS = MLA_HEADS // 2
BLOCKED = -1.0e30
KEY_AT = (0, 512, 1024, 896)
KEY_COLS = sum(SEQ - t * P for t in range(TILES))
QUERY_AT = (512 + 384, 1024, 512, 0)


def latent_attention_layer(nc, keep, x, ident, io):
    with ExitStack() as ctx:
        def sb(name, shape, dt=F32):
            return ctx.enter_context(nc.sbuf_tensor(f"mla_{name}", shape, dt))

        def sem(name):
            return keep.enter_context(nc.semaphore(f"mla_{name}"))

        ps = ctx.enter_context(nc.psum_tensor("mla_ps", [P, 8, 512], F32))
        a_hi = sb("a_hi", [P, KD, MLA_HEADS, 2, LATENT], F16)
        a_lo = sb("a_lo", [P, KD, MLA_HEADS, 2, LATENT], F16)
        b_hi = sb("b_hi", [P, MLA_PAIRS, D], F16)
        b_lo = sb("b_lo", [P, MLA_PAIRS, D], F16)
        down_hi = sb("down_hi", [P, KD, 2, LATENT], F16)
        down_lo = sb("down_lo", [P, KD, 2, LATENT], F16)
        ident_b = sb("ident_b", [P, P], BF16)
        block_q = sb("block_q", [P, P], BF16)
        block_k = sb("block_k", [P, P], BF16)
        pick = sb("pick", [P, MLA_HEADS, P], BF16)
        val_hi = sb("val_hi", [P, TILES, P], F16)
        val_lo = sb("val_lo", [P, TILES, P], F16)
        m_t = sb("m_t", [48, SEQ], BF16)

        with ExitStack() as part:
            def tmp(name, shape, dt=F32):
                return part.enter_context(nc.sbuf_tensor(f"mla_{name}", shape, dt))

            def tsem(name):
                return keep.enter_context(nc.semaphore(f"mla_{name}"))

            wq = tmp("wq", [P, KD, MLA_HEADS * MLA_DIM])
            wk = tmp("wk", [LATENT, MLA_HEADS * MLA_DIM])
            wv = tmp("wv", [LATENT, MLA_HEADS * MLA_DIM])
            wout = tmp("wout", [P, MLA_PAIRS, D])
            down = tmp("down", [P, KD, LATENT])
            wq_t = tmp("wq_t", [P, MLA_PAIRS, D])
            wk_t = tmp("wk_t", [P, MLA_PAIRS, LATENT])
            wv_t = tmp("wv_t", [P, MLA_PAIRS, LATENT])
            pick_f = tmp("pick_f", [P, MLA_HEADS, P])
            block_f = tmp("block_f", [P, 2, P])
            loaded = tsem("loaded")
            made = tsem("made")
            turned = tsem("turned")
            turn_out = tsem("turn_out")
            folded = tsem("folded")
            split = tsem("split")
            const_done = tsem("const_done")

            with nc.Block() as block:
                @block.sync
                def _(sp):
                    sp.dma_start(wq[:, :, :], io["Wq"].rearrange("(k p) h n -> p k (h n)", p=P)).then_inc(loaded, 16)
                    sp.dma_start(wk[:, :], io["Wk_up"].rearrange("c h n -> c (h n)")).then_inc(loaded, 16)
                    sp.dma_start(wv[:, :], io["Wv_up"].rearrange("c h n -> c (h n)")).then_inc(loaded, 16)
                    sp.dma_start(wout[:, :, :], io["Wout"].rearrange("(m h) n d -> (h n) m d", h=2)).then_inc(loaded, 16)
                    sp.dma_start(down[:, :, :], io["Wkv_down"].rearrange("(k p) c -> p k c", p=P)).then_inc(loaded, 16)

                @block.gpsimd
                def _(pool):
                    pool.memset(pick_f[:, :, :], 0.0).then_inc(made, 1)
                    pool.memset(block_f[:, :, :], 0.0).then_inc(made, 1)
                    for n, base in enumerate((0, -32)):
                        pool.wait_ge(made, 2 + n)
                        pool.affine_select(out=pick_f[:, :, :], in_=pick_f[:, :, :], compare_op=ALU.not_equal, fill=1.0,
                                           base=base, pattern=[[-1, MLA_HEADS], [0, P]],
                                           channel_multiplier=1).then_inc(made, 1)
                    pool.affine_select(out=block_f[:, 0, :], in_=block_f[:, 0, :], compare_op=ALU.is_ge, fill=BLOCKED,
                                       base=0, pattern=[[-1, P]], channel_multiplier=1).then_inc(made, 1)
                    pool.affine_select(out=block_f[:, 1, :], in_=block_f[:, 1, :], compare_op=ALU.is_ge, fill=BLOCKED,
                                       base=0, pattern=[[1, P]], channel_multiplier=-1).then_inc(made, 1)

                @block.tensor
                def _(pe):
                    pe.wait_ge(loaded, 80)
                    for m in range(MLA_PAIRS):
                        for k in range(KD):
                            last = pe.transpose(ps[:, m // 2, (m % 2) * D + k * P:(m % 2) * D + (k + 1) * P],
                                                wq[:, k, m * P:(m + 1) * P], ident[:, :])
                    last.then_inc(turned, 1)
                    for i, w in enumerate((wk, wv)):
                        for m in range(MLA_PAIRS):
                            last = pe.transpose(ps[:, 4 + i, m * LATENT:(m + 1) * LATENT], w[:, m * P:(m + 1) * P],
                                                ident[0:LATENT, 0:LATENT])
                        last.then_inc(turned, 1)
                    pe.wait_ge(turn_out, 6)
                    for m in range(MLA_PAIRS):
                        if m >= 4:
                            pe.wait_ge(split, 2 * (m - 3))
                        for i in range(2):
                            bank = 4 * i + m % 4
                            rows = slice(i * MLA_DIM, (i + 1) * MLA_DIM)
                            for k in range(KD):
                                last = pe.matmul(ps[:, bank, k * LATENT:(k + 1) * LATENT],
                                                 wq_t[rows, m, k * P:(k + 1) * P], wk_t[rows, m, :],
                                                 start=True, stop=True)
                            last = pe.matmul(ps[i * LATENT:(i + 1) * LATENT, bank, D:2 * D],
                                             wv_t[rows, m, :], wout[rows, m, :], start=True, stop=True)
                        last.then_inc(folded, 1)

                @block.vector
                def _(dve):
                    dve.wait_ge(turned, 3)
                    for n in range(4):
                        dve.tensor_copy(wq_t[:, 2 * n:2 * n + 2, :].rearrange("p m d -> p (m d)"),
                                        ps[:, n, :]).then_inc(turn_out, 1)
                    for w, bank in ((wk_t, 4), (wv_t, 5)):
                        dve.tensor_copy(w[:, :, :].rearrange("p m c -> p (m c)"), ps[:, bank, :]).then_inc(turn_out, 1)
                    dve.wait_ge(made, 6)
                    dve.tensor_copy(pick[:, :, :], pick_f[:, :, :])
                    dve.tensor_copy(block_q[:, :], block_f[:, 0, :])
                    dve.tensor_copy(block_k[:, :], block_f[:, 1, :])
                    dve.tensor_copy(ident_b[:, :], ident[:, :])
                    dve.memset(val_hi[:, :, LATENT:P], 1.0)
                    dve.memset(val_lo[:, :, LATENT:P], 0.0)
                    dve.memset(m_t[:, :], 0.0)
                    wide = [P, KD, 2, LATENT]
                    src = down[:, :, :].unsqueeze(2).to_broadcast(wide)
                    dve.tensor_scalar(down_hi[:, :, :, :], src, WS, None, ALU.mult).then_inc(const_done, 1)
                    dve.wait_ge(const_done, 1)
                    for k in range(KD):
                        dve.scalar_tensor_tensor(down_lo[:, k, :, :], down[:, k, :].unsqueeze(1).to_broadcast([P, 2, LATENT]),
                                                 WS, down_hi[:, k, :, :], ALU.mult, ALU.subtract)
                    for m in range(MLA_PAIRS):
                        dve.wait_ge(folded, m + 1)
                        for i in range(2):
                            bank, rows = 4 * i + m % 4, slice(i * LATENT, (i + 1) * LATENT)
                            dve.tensor_scalar(b_hi[rows, m, :], ps[rows, bank, D:2 * D], WS, None, ALU.mult)
                            for k in range(KD):
                                src = ps[:, bank, k * LATENT:(k + 1) * LATENT].unsqueeze(1).to_broadcast([P, 2, LATENT])
                                last = dve.tensor_scalar(a_hi[:, k, 2 * m + i, :, :], src, WS, None, ALU.mult)
                        last.then_inc(split, 1)
                        dve.wait_ge(split, 2 * m + 1)
                        for i in range(2):
                            bank, rows = 4 * i + m % 4, slice(i * LATENT, (i + 1) * LATENT)
                            dve.scalar_tensor_tensor(b_lo[rows, m, :], ps[rows, bank, D:2 * D], WS, b_hi[rows, m, :],
                                                     ALU.mult, ALU.subtract)
                            for k in range(KD):
                                src = ps[:, bank, k * LATENT:(k + 1) * LATENT].unsqueeze(1).to_broadcast([P, 2, LATENT])
                                last = dve.scalar_tensor_tensor(a_lo[:, k, 2 * m + i, :, :], src, WS,
                                                                a_hi[:, k, 2 * m + i, :, :], ALU.mult, ALU.subtract)
                        last.then_inc(split, 1)

        y = sb("y", [P, TILES, D])
        y_hi = sb("y_hi", [P, KD, SEQ], F16)
        y_lo = sb("y_lo", [P, KD, SEQ], F16)
        stats = sb("stats", [P, TILES, 6])
        ln_col = sb("ln_col", [P, 4, TILES])
        var = sb("var", [P, TILES])
        rstd = sb("rstd", [P, TILES])
        newton = sb("newton", [P, TILES])
        lat = sb("lat", [P, SEQ])
        key_hl = sb("key_hl", [P, SEQ], F16)
        q_hi = sb("q_hi", [P, MLA_HEADS, SEQ], F16)
        q_lo = sb("q_lo", [P, MLA_HEADS, SEQ], F16)
        m_col = sb("m_col", [P, TILES, MLA_HEADS])
        m_neg = sb("m_neg", [MLA_HEADS, SEQ])
        p_full = sb("p_full", [P, 2, KEY_COLS])
        p_hi = sb("p_hi", [P, 2, KEY_COLS], F16)
        p_lo = sb("p_lo", [P, 2, KEY_COLS], F16)
        inv = sb("inv", [LATENT, 2, SEQ])
        o = sb("o", [P, 2, SEQ])
        o_hi = sb("o_hi", [P, MLA_PAIRS, SEQ], F16)
        o_lo = sb("o_lo", [P, MLA_PAIRS, SEQ], F16)

        norm_step = sem("norm_step")
        y_turned = sem("y_turned")
        y_split = sem("y_split")
        lat_done = sem("lat_done")
        lat_step = sem("lat_step")
        lat_turned = sem("lat_turned")
        val_out = sem("val_out")
        q_done = sem("q_done")
        q_head = sem("q_head")
        q_tail = sem("q_tail")
        s_done = sem("s_done")
        s_max = sem("s_max")
        m_turned = sem("m_turned")
        m_step = sem("m_step")
        st_done = sem("st_done")
        exp_done = sem("exp_done")
        p_tail = sem("p_tail")
        pv_done = sem("pv_done")
        o_step = sem("o_step")
        o_head = sem("o_head")
        o_tail = sem("o_tail")
        out_done = sem("out_done")
        x_added = sem("x_added")
        H = MLA_HEADS

        def since(engine, semaphore, base, h, back):
            if h >= back:
                engine.wait_ge(semaphore, base + h - back + 1)

        with nc.Block() as block:
            @block.tensor
            def _(pe):
                with pe.Fori(0, BATCH) as b:
                    heads = b * H
                    pe.wait_ge(norm_step, LN_STEPS * (b + 1))
                    transpose_tiles(pe, y, ps[:, 6:8, :], ident[:, :]).then_inc(y_turned, 1)
                    pe.wait_ge(y_split, 4 * (b + 1))
                    for k in range(KD):
                        last = split_matmul(pe, ps[:, 0, :], down_hi[:, k, :, :].rearrange("p a c -> p (a c)"),
                                            down_lo[:, k, :, :].rearrange("p a c -> p (a c)"),
                                            y_hi[:, k, :], y_lo[:, k, :], k == 0, k == KD - 1)
                    last.then_inc(lat_done, 1)

                    def query(h):
                        since(pe, q_tail, heads, h, 2)
                        for k in range(KD):
                            last = split_matmul(pe, ps[:, 6 + h % 2, :], a_hi[:, k, h, :, :].rearrange("p a c -> p (a c)"),
                                                a_lo[:, k, h, :, :].rearrange("p a c -> p (a c)"),
                                                y_hi[:, k, :], y_lo[:, k, :], k == 0, k == KD - 1)
                        last.then_inc(q_done, 1)

                    def score(h):
                        if h >= 2:
                            pe.wait_ge(s_max, TILES * (heads + h - 1))
                        pe.wait_ge(q_head, heads + h + 1)
                        for t in range(TILES):
                            at = 3 * (h % 2) * 512 + QUERY_AT[t]
                            out = flat[:, at:at + (t + 1) * P]
                            pe.matmul(out, q_hi[:, h, t * P:(t + 1) * P], key_hl[:, 0:(t + 1) * P],
                                      start=True, stop=False)
                            last = pe.matmul(out[:, t * P:(t + 1) * P], ident_b[:, :], block_q[:, :],
                                             start=False, stop=True)
                        last.then_inc(s_done, 1)

                    def score_t(h):
                        if h >= 2:
                            pe.wait_ge(exp_done, 2 * (heads + h - 1))
                        if h == 0:
                            pe.wait_ge(q_tail, heads + H)
                            pe.wait_ge(m_step, 3 * (b + 1))
                        for t in range(TILES):
                            at = 3 * (h % 2) * 512 + KEY_AT[t]
                            n = SEQ - t * P
                            keys = key_hl[:, t * P:(t + 1) * P]
                            pe.matmul(flat[:, at:at + n], keys, q_hi[:, h, t * P:], start=True, stop=False)
                            pe.matmul(flat[:, at:at + n], keys, q_lo[:, h, t * P:], start=False, stop=False)
                            pe.matmul(flat[:, at:at + n], pick[0:48, h, :], m_t[:, t * P:], start=False, stop=False)
                            last = pe.matmul(flat[:, at:at + P], ident_b[:, :], block_k[:, :], start=False, stop=True)
                        last.then_inc(st_done, 1)

                    def values(h):
                        pe.wait_ge(p_tail, heads + h + 1)
                        if h == 0:
                            pe.wait_ge(m_step, 3 * (b + 1))
                        if h >= 2:
                            pe.wait_ge(o_step, 2 * (heads + h - 1))
                        for t in range(TILES):
                            out = ps[:, 6 + h % 2, t * P:]
                            cols = slice(KEY_AT[t], KEY_AT[t] + SEQ - t * P)
                            hi, lo = p_hi[:, h % 2, cols], p_lo[:, h % 2, cols]
                            pe.matmul(out, val_hi[:, t, :], hi, start=(t == 0), stop=False)
                            pe.matmul(out, val_hi[:, t, :], lo, start=False, stop=False)
                            last = pe.matmul(out, val_lo[:, t, :], hi, start=False, stop=(t == TILES - 1))
                        last.then_inc(pv_done, 1)

                    flat = ps[:, :, :].rearrange("p a n -> p (a n)")
                    query(0)
                    pe.wait_ge(lat_step, 3 * b + 1)
                    query(1)
                    for t in range(TILES):
                        last = pe.transpose(ps[:, 1, t * LATENT:(t + 1) * LATENT], lat[0:LATENT, t * P:(t + 1) * P],
                                            ident[0:LATENT, 0:LATENT])
                    last.then_inc(lat_turned, 1)
                    pe.wait_ge(lat_step, 3 * (b + 1))
                    pe.wait_ge(val_out, 2 * (b + 1))
                    for h in range(H):
                        if 1 <= h < H - 1:
                            query(h + 1)
                        score(h)
                    pe.wait_ge(q_tail, heads + H)
                    pe.wait_ge(s_max, TILES * (heads + H))
                    for t in range(TILES):
                        last = pe.transpose(ps[0:H, 6, t * P:(t + 1) * P], m_col[:, t, :], ident[:, :])
                    last.then_inc(m_turned, 1)
                    score_t(0)
                    for h in range(H):
                        if h + 1 < H:
                            score_t(h + 1)
                        values(h)
                    pe.wait_ge(o_tail, MLA_PAIRS * (b + 1))
                    for t in range(TILES):
                        out = ps[:, t // 2, (t % 2) * D:(t % 2 + 1) * D]
                        toks = slice(t * P, (t + 1) * P)
                        for m in range(MLA_PAIRS):
                            pe.matmul(out, o_hi[:, m, toks], b_hi[:, m, :], start=(m == 0), stop=False)
                            pe.matmul(out, o_hi[:, m, toks], b_lo[:, m, :], start=False, stop=False)
                            last = pe.matmul(out, o_lo[:, m, toks], b_hi[:, m, :], start=False,
                                             stop=(m == MLA_PAIRS - 1))
                    last.then_inc(out_done, 1)

            @block.vector
            def _(dve):
                with dve.Fori(0, BATCH) as b:
                    heads = b * H
                    flat = ps[:, :, :].rearrange("p a n -> p (a n)")
                    layernorm_batch(dve, norm_step, LN_STEPS * b, x[:, b, :, :], y, stats, ln_col,
                                    var[:, :], rstd[:, :], newton[:, :])
                    dve.wait_ge(y_turned, b + 1)
                    for k in range(KD):
                        dve.tensor_copy(y_hi[:, k, :], ps[:, 6 + k, :]).then_inc(y_split, 1)
                    dve.wait_ge(y_split, 4 * b + 2)
                    for k in range(KD):
                        dve.tensor_tensor(y_lo[:, k, :], ps[:, 6 + k, :], y_hi[:, k, :], ALU.subtract).then_inc(y_split, 1)
                    dve.wait_ge(lat_done, b + 1)
                    dve.tensor_scalar(lat[:, :], ps[:, 0, :], 1.0 / WS, None, ALU.mult).then_inc(lat_step, 1)
                    dve.wait_ge(lat_step, 3 * b + 1)
                    dve.tensor_copy(key_hl[:, :], lat[:, :]).then_inc(lat_step, 1)
                    dve.wait_ge(lat_step, 3 * b + 2)
                    tails = slice(LATENT, P)
                    dve.tensor_tensor(key_hl[tails, :], lat[tails, :], key_hl[tails, :], ALU.subtract).then_inc(lat_step, 1)
                    dve.wait_ge(lat_turned, b + 1)
                    src = ps[:, 1, 0:TILES * LATENT].rearrange("p (t c) -> p t c", c=LATENT)
                    dve.tensor_copy(val_hi[:, :, 0:LATENT], src).then_inc(val_out, 1)
                    dve.wait_ge(val_out, 2 * b + 1)
                    dve.tensor_tensor(val_lo[:, :, 0:LATENT], src, val_hi[:, :, 0:LATENT], ALU.subtract).then_inc(val_out, 1)

                    for h in range(H):
                        dve.wait_ge(q_head, heads + h + 1)
                        dve.scalar_tensor_tensor(q_lo[:, h, :], ps[:, 6 + h % 2, :], 1.0 / WS, q_hi[:, h, :],
                                                 ALU.mult, ALU.subtract).then_inc(q_tail, 1)
                        dve.wait_ge(s_done, heads + h + 1)
                        for t in range(TILES):
                            at = 3 * (h % 2) * 512 + QUERY_AT[t]
                            dve.tensor_reduce(m_col[:, t, h:h + 1], flat[:, at:at + (t + 1) * P], AX.X,
                                              ALU.max).then_inc(s_max, 1)
                    dve.wait_ge(m_turned, b + 1)
                    dve.tensor_scalar(m_neg[:, :], ps[0:H, 6, :], -1.0, None, ALU.mult).then_inc(m_step, 1)
                    dve.wait_ge(m_step, 3 * b + 1)
                    dve.tensor_copy(m_t[0:H, :], m_neg[:, :]).then_inc(m_step, 1)
                    dve.wait_ge(m_step, 3 * b + 2)
                    dve.tensor_tensor(m_t[32:32 + H, :], m_neg[:, :], m_t[0:H, :], ALU.subtract).then_inc(m_step, 1)

                    def normalise(h):
                        pair, at = h // 2, 2 * (heads + h)
                        bank = ps[:, 6 + h % 2, :]
                        dve.wait_ge(pv_done, heads + h + 1)
                        dve.reciprocal(inv[:, h % 2, :], bank[LATENT:P, :]).then_inc(o_step, 1)
                        dve.wait_ge(o_step, at + 1)
                        if pair >= 2:
                            dve.wait_ge(o_head, MLA_PAIRS * b + pair - 1)
                            dve.wait_ge(o_tail, MLA_PAIRS * b + pair - 1)
                        rows = slice((h % 2) * LATENT, (h % 2 + 1) * LATENT)
                        dve.tensor_tensor(o[rows, pair % 2, :], bank[0:LATENT, :], inv[:, h % 2, :],
                                          ALU.mult).then_inc(o_step, 1)

                    def out_tail(pair):
                        dve.wait_ge(o_head, MLA_PAIRS * b + pair + 1)
                        dve.tensor_tensor(o_lo[:, pair, :], o[:, pair % 2, :], o_hi[:, pair, :],
                                          ALU.subtract).then_inc(o_tail, 1)

                    for h in range(H):
                        dve.wait_ge(exp_done, 2 * (heads + h + 1))
                        since(dve, pv_done, heads, h, 2)
                        dve.tensor_tensor(p_lo[:, h % 2, :], p_full[:, h % 2, :], p_hi[:, h % 2, :],
                                          ALU.subtract).then_inc(p_tail, 1)
                        if h >= 1:
                            normalise(h - 1)
                        if h >= 3 and h % 2 == 1:
                            out_tail(h // 2 - 1)
                    normalise(H - 1)
                    out_tail(MLA_PAIRS - 1)
                    dve.wait_ge(out_done, b + 1)
                    xb = x[:, b, :, :].rearrange("p t d -> p (t d)")
                    dve.scalar_tensor_tensor(xb, flat[:, 0:TILES * D], 1.0 / WS, xb, ALU.mult,
                                             ALU.add).then_inc(x_added, 1)

            @block.scalar
            def _(act):
                with act.Fori(0, BATCH) as b:
                    heads = b * H
                    flat = ps[:, :, :].rearrange("p a n -> p (a n)")
                    for h in range(H):
                        act.wait_ge(q_done, heads + h + 1)
                        act.activation(q_hi[:, h, :], ps[:, 6 + h % 2, :], ACT.Copy, scale=1.0 / WS).then_inc(q_head, 1)

                    def out_head(pair):
                        act.wait_ge(o_step, 4 * (MLA_PAIRS * b + pair + 1))
                        act.activation(o_hi[:, pair, :], o[:, pair % 2, :], ACT.Copy).then_inc(o_head, 1)

                    for h in range(H):
                        at = 3 * (h % 2) * 512
                        act.wait_ge(st_done, heads + h + 1)
                        since(act, p_tail, heads, h, 2)
                        since(act, pv_done, heads, h, 2)
                        for out in (p_full, p_hi):
                            act.activation(out[:, h % 2, :], flat[:, at:at + KEY_COLS], ACT.Exp,
                                           scale=float(MLA_DIM) ** -0.5).then_inc(exp_done, 1)
                        if h >= 3 and h % 2 == 1:
                            out_head(h // 2 - 1)
                    out_head(MLA_PAIRS - 1)


class Kept:

    def __init__(self, stack):
        self.stack, self.semaphores = stack, []

    def enter_context(self, semaphore):
        self.semaphores.append(self.stack.enter_context(semaphore))
        return self.semaphores[-1]


def macaron_kernel(nc, io, out):
    with ExitStack() as ctx:
        x = ctx.enter_context(nc.sbuf_tensor("x", [P, BATCH, TILES, D], F32))
        ident = ctx.enter_context(nc.sbuf_tensor("ident", [P, P], F32))
        x_in = ctx.enter_context(nc.semaphore("x_in"))
        x_out = ctx.enter_context(nc.semaphore("x_out"))
        ident_set = ctx.enter_context(nc.semaphore("ident_set"))

        with nc.Block() as block:
            @block.sync
            def _(sp):
                for b in range(BATCH):
                    sp.dma_start(x[:, b], io["x"][b].rearrange("(t p) d -> p t d", p=P)).then_inc(x_in, 16)
                sp.wait_ge(x_in, 16 * BATCH)

            @block.gpsimd
            def _(pool):
                pool.memset(ident[:, :], 0.0).then_inc(ident_set, 1)
                pool.wait_ge(ident_set, 1)
                pool.affine_select(out=ident[:, :], in_=ident[:, :], compare_op=ALU.not_equal, fill=1.0,
                                   base=0, pattern=[[-1, P]], channel_multiplier=1).then_inc(ident_set, 1)

        experts = {n: io["L0_attn_" + n] for n in ("Wq", "bq", "Wk", "bk", "Wv", "bv")}
        experts |= {n: io["L0_ffn_" + n] for n in ("gate_w", "gate_b", "rms_w", "w1", "b1", "w2", "b2")}
        experts["rope_tab"] = io["rope_tab"]
        routed = {n: io["L1_ffn_" + n] for n in ("attention_mask", "position_ids", "router_w", "router_b", "wq", "wk",
                                                 "wv", "wo", "w1", "w2", "ln1", "ln2")}
        routed["inv_freq"] = io["inv_freq"]
        latent = {n: io["L1_attn_" + n] for n in ("Wq", "Wkv_down", "Wk_up", "Wv_up", "Wout")}

        def layer(build, *args):
            with ExitStack() as kept:
                held = Kept(kept)
                build(nc, held, *args)
                with nc.Block() as block:
                    @block.sync
                    def _(sp):
                        for semaphore in held.semaphores:
                            sp.sem_clear(semaphore)

        layer(expert_and_head_layers, x, ident, experts)
        layer(routed_layer, "routed1", x, ident, routed)
        layer(latent_attention_layer, x, ident, latent)
        layer(routed_layer, "routed2", x, ident, routed)

        with nc.Block() as block:
            @block.sync
            def _(sp):
                for b in range(BATCH):
                    sp.dma_start(out[b].rearrange("(t p) d -> p t d", p=P), x[:, b]).then_inc(x_out, 16)
                sp.wait_ge(x_out, 16 * BATCH)


def kernel(**inputs):
    import numpy as _np
    import concourse.bacc as _bacc
    from concourse import mybir as _mybir
    from concourse.bass_utils import run_bass_kernel_spmd as _run

    even = _np.arange(0, HEAD_DIM, 2, dtype=_np.float32)
    freqs = (_np.float32(10000.0) ** (-(even / _np.float32(D)))).astype(_np.float32)
    angles = _np.arange(SEQ, dtype=_np.float32)[:, None] * freqs[None, :]
    tables = {
        "rope_tab": _np.stack([_np.cos(angles.astype(_np.float64)), _np.sin(angles.astype(_np.float64))],
                              axis=1).astype(_np.float32),
        "inv_freq": (_np.float32(1.0) / _np.float32(10000.0) ** (even / _np.float32(HEAD_DIM))).astype(_np.float32),
    }
    nc = _bacc.Bacc("TRN2", target_bir_lowering=False, num_devices=1)
    arrays, io = {}, {}
    for name, value in {**inputs, **tables}.items():
        a = _np.ascontiguousarray(value)
        arrays[f"in_{name}_dram"] = a
        key = "x" if name == "L0_attn_x" else name
        io[key] = nc.dram_tensor(f"in_{name}_dram", a.shape, _mybir.dt.from_np(a.dtype), kind="ExternalInput").ap()
    out = nc.dram_tensor("out_0_dram", (BATCH, SEQ, D), F32, kind="ExternalOutput").ap()
    macaron_kernel(nc, io, out)
    r = _run(nc, [arrays], core_ids=[0])
    return r.results[0]["out_0_dram"]
```

```python
from contextlib import ExitStack

import numpy as np

import concourse.bass as bass
from concourse import mybir

F32 = mybir.dt.float32
F16 = mybir.dt.float16
I32 = mybir.dt.int32
U32 = mybir.dt.uint32
ALU = mybir.AluOpType
ACT = mybir.ActivationFunctionType
AX = mybir.AxisListType

P = 128
BATCH, SEQ, D = 8, 512, 256
TILES = SEQ // P
KD = D // P
EXPERTS, EXPERT_HID = 8, 512
HID_TILES = EXPERTS * EXPERT_HID // P
HEADS, HEAD_DIM = 16, 16
QKV = 3 * D
LN_EPS = 1e-5
F32_EPS = float(np.finfo(np.float32).eps)

WS = 16.0

RSQRT_STEPS = 11
LN_COLUMN_STEPS = 7 + RSQRT_STEPS
LN_STEPS = TILES + LN_COLUMN_STEPS + TILES
GATE_STEPS = 24
HEAD_STEPS = 102
STAGES = 2 * BATCH


def rsqrt_newton(dve, step, at, v, y, t):
    yi = y.bitcast(I32)
    dve.wait_ge(step, at)
    dve.tensor_scalar(yi, v.bitcast(I32), 1, None, ALU.logical_shift_right).then_inc(step, 1)
    dve.wait_ge(step, at + 1)
    dve.tensor_scalar(yi, yi, -1.0, float(0x5F3759DF), ALU.mult, ALU.add).then_inc(step, 1)
    for n in range(3):
        dve.wait_ge(step, at + 2 + 3 * n)
        dve.tensor_tensor(t, y, y, ALU.mult).then_inc(step, 1)
        dve.wait_ge(step, at + 3 + 3 * n)
        dve.scalar_tensor_tensor(t, t, -0.5, v, ALU.mult, ALU.mult).then_inc(step, 1)
        dve.wait_ge(step, at + 4 + 3 * n)
        dve.scalar_tensor_tensor(y, t, 1.5, y, ALU.add, ALU.mult).then_inc(step, 1)


def layernorm_stats(dve, step, x4, stats):
    for t in range(TILES):
        dve.bn_stats(stats[:, t, :], x4[:, t, :]).then_inc(step, 1)


def layernorm_columns(dve, step, at, stats, col, var, rstd, tmp):
    twice_mean, gap, squares, mean = (col[:, i, :] for i in range(4))
    dve.wait_ge(step, at)
    dve.tensor_tensor(twice_mean, stats[:, :, 1], stats[:, :, 4], ALU.add).then_inc(step, 1)
    dve.tensor_tensor(gap, stats[:, :, 1], stats[:, :, 4], ALU.subtract).then_inc(step, 1)
    dve.tensor_tensor(squares, stats[:, :, 2], stats[:, :, 5], ALU.add).then_inc(step, 1)
    dve.wait_ge(step, at + 3)
    dve.tensor_scalar(mean, twice_mean, 0.5, None, ALU.mult).then_inc(step, 1)
    dve.tensor_tensor(gap, gap, gap, ALU.mult).then_inc(step, 1)
    dve.tensor_scalar(squares, squares, 1.0 / D, LN_EPS, ALU.mult, ALU.add).then_inc(step, 1)
    dve.wait_ge(step, at + 6)
    dve.scalar_tensor_tensor(var, gap, 0.25, squares, ALU.mult, ALU.add).then_inc(step, 1)
    rsqrt_newton(dve, step, at + 7, var, rstd, tmp)


def layernorm_apply(dve, step, at, x4, y4, col, rstd):
    mean = col[:, 3, :]
    dve.wait_ge(step, at)
    for t in range(TILES):
        dve.tensor_scalar(y4[:, t, :], x4[:, t, :], mean[:, t:t + 1], rstd[:, t:t + 1],
                          ALU.subtract, ALU.mult).then_inc(step, 1)


def layernorm_batch(dve, step, at, x4, y4, stats, col, var, rstd, tmp):
    layernorm_stats(dve, step, x4, stats)
    layernorm_columns(dve, step, at + TILES, stats, col, var, rstd, tmp)
    layernorm_apply(dve, step, at + TILES + LN_COLUMN_STEPS, x4, y4, col, rstd)


def transpose_tiles(pe, y4, out2, ident):
    for k in range(KD):
        for t in range(TILES):
            last = pe.transpose(out2[:, k, t * P:(t + 1) * P], y4[:, t, k * P:(k + 1) * P], ident)
    return last


def split_matmul(pe, out, w_hi, w_lo, v_hi, v_lo, first, final):
    pe.matmul(out, w_hi, v_hi, start=first, stop=False)
    pe.matmul(out, w_hi, v_lo, start=False, stop=False)
    return pe.matmul(out, w_lo, v_hi, start=False, stop=final)


def expert_and_head_layers(nc, keep, x, ident, io):
    with ExitStack() as ctx:
        def sb(name, shape, dt=F32):
            return ctx.enter_context(nc.sbuf_tensor(name, shape, dt))

        def sem(name):
            return keep.enter_context(nc.semaphore(name))

        w1_hi = sb("w1_hi", [P, KD, HID_TILES * P], F16)
        w1_lo = sb("w1_lo", [P, KD, HID_TILES * P], F16)
        w2_hi = sb("w2_hi", [P, HID_TILES, D], F16)
        w2_lo = sb("w2_lo", [P, HID_TILES, D], F16)
        wqkv_hi = sb("wqkv_hi", [P, KD, QKV], F16)
        wqkv_lo = sb("wqkv_lo", [P, KD, QKV], F16)
        gate_hi = sb("gate_hi", [P, KD, EXPERTS], F16)
        gate_lo = sb("gate_lo", [P, KD, EXPERTS], F16)
        gate_bias = sb("gate_bias", [EXPERTS, 1])
        rms_w = sb("rms_w", [P, EXPERTS])
        b1_col = sb("b1_col", [P, HID_TILES])
        b2_sum = sb("b2_sum", [P, KD])
        qkv_bias = sb("qkv_bias", [P, QKV])
        rope = sb("rope", [P, TILES, 2, HEAD_DIM // 2])

        with ExitStack() as setup:
            def tmp(name, shape, dt=F32):
                return setup.enter_context(nc.sbuf_tensor(name, shape, dt))

            def tsem(name):
                return keep.enter_context(nc.semaphore(name))

            SLOTS = 4
            CHUNK = KD * EXPERT_HID
            stage = tmp("stage", [P, SLOTS, CHUNK])
            b1_rows = tmp("b1_rows", [HID_TILES, P])
            gate_rows = tmp("gate_rows", [EXPERTS, D])
            b2_rows = tmp("b2_rows", [EXPERTS, D])
            ones = tmp("ones", [EXPERTS, 1])
            gate_t = tmp("gate_t", [P, KD, EXPERTS])
            small = setup.enter_context(nc.psum_tensor("small", [P, 3, 512], F32))
            slot_in = [tsem(f"slot_in{i}") for i in range(SLOTS)]
            small_in = tsem("small_in")
            head_done = tsem("head_done")
            tail_done = tsem("tail_done")
            small_t = tsem("small_t")
            ones_set = tsem("ones_set")
            gate_step = tsem("gate_split_step")

            chunks = []
            for w, lo, hi in ((io["Wq"], 0, D), (io["Wk"], D, 2 * D), (io["Wv"], 2 * D, QKV)):
                chunks.append((w.rearrange("(k p) n -> p k n", p=P), (KD, D),
                               wqkv_hi[:, :, lo:hi], wqkv_lo[:, :, lo:hi]))
            for e in range(EXPERTS):
                cols = slice(e * EXPERT_HID, (e + 1) * EXPERT_HID)
                chunks.append((io["w1"][e].rearrange("(k p) h -> p k h", p=P), (KD, EXPERT_HID),
                               w1_hi[:, :, cols], w1_lo[:, :, cols]))
                rows = slice(e * EXPERT_HID // P, (e + 1) * EXPERT_HID // P)
                chunks.append((io["w2"][e].rearrange("(j p) d -> p j d", p=P), (EXPERT_HID // P, D),
                               w2_hi[:, rows, :], w2_lo[:, rows, :]))

            def staged(c):
                a, b = chunks[c][1]
                return stage[:, c % SLOTS, 0:a * b].rearrange("p (a b) -> p a b", a=a)

            SMALL_LOADS = 8
            with nc.Block() as block:
                @block.sync
                def _(sp):
                    for c, (src, _, _, _) in enumerate(chunks):
                        if c >= SLOTS:
                            sp.wait_ge(tail_done, c - SLOTS + 1)
                        sp.dma_start(staged(c), src).then_inc(slot_in[c % SLOTS], 16)

                @block.gpsimd
                def _(pool):
                    pool.memset(ones[:, :], 1.0).then_inc(ones_set, 1)
                    pool.dma_start(b1_rows[:, :], io["b1"].rearrange("e (j p) -> (e j) p", p=P)).then_inc(small_in, 16)
                    pool.dma_start(gate_rows[:, :], io["gate_w"]).then_inc(small_in, 16)
                    pool.dma_start(b2_rows[:, :], io["b2"]).then_inc(small_in, 16)
                    pool.dma_start(gate_bias[:, :], io["gate_b"].rearrange("(e o) -> e o", o=1)).then_inc(small_in, 16)
                    pool.dma_start(rms_w[:, :], io["rms_w"].partition_broadcast(P)).then_inc(small_in, 16)
                    for i, name in enumerate(("bq", "bk", "bv")):
                        pool.dma_start(qkv_bias[:, i * D:(i + 1) * D],
                                       io[name].partition_broadcast(P)).then_inc(small_in, 16)
                    pool.dma_start(rope[:, :, :, :],
                                   io["rope_tab"].rearrange("(t p) c i -> p t c i", p=P)).then_inc(small_in, 16)

                @block.scalar
                def _(act):
                    for c, (_, _, hi, _) in enumerate(chunks):
                        act.wait_ge(slot_in[c % SLOTS], 16 * (c // SLOTS + 1))
                        act.activation(hi, staged(c), ACT.Copy, scale=WS).then_inc(head_done, 1)

                @block.vector
                def _(dve):
                    for c, (_, _, hi, lo) in enumerate(chunks):
                        dve.wait_ge(head_done, c + 1)
                        dve.scalar_tensor_tensor(lo, staged(c), WS, hi, ALU.mult,
                                                 ALU.subtract).then_inc(tail_done, 1)
                    dve.wait_ge(small_t, 3)
                    dve.tensor_copy(b1_col[:, :], small[:, 0, 0:HID_TILES])
                    dve.tensor_copy(b2_sum[:, :], small[:, 1, 0:KD])
                    dve.tensor_scalar(gate_t[:, :, :], small[:, 2, 0:KD * EXPERTS].rearrange("p (k e) -> p k e", k=KD),
                                      WS, None, ALU.mult).then_inc(gate_step, 1)
                    dve.wait_ge(gate_step, 1)
                    dve.tensor_copy(gate_hi[:, :, :], gate_t[:, :, :]).then_inc(gate_step, 1)
                    dve.wait_ge(gate_step, 2)
                    dve.tensor_tensor(gate_lo[:, :, :], gate_t[:, :, :], gate_hi[:, :, :], ALU.subtract)

                @block.tensor
                def _(pe):
                    pe.wait_ge(small_in, 16 * (SMALL_LOADS + 1))
                    pe.wait_ge(ones_set, 1)
                    pe.transpose(small[:, 0, 0:HID_TILES], b1_rows[:, :],
                                 ident[0:HID_TILES, 0:HID_TILES]).then_inc(small_t, 1)
                    for k in range(KD):
                        last = pe.matmul(small[:, 1, k:k + 1], b2_rows[:, k * P:(k + 1) * P], ones[:, :],
                                         start=True, stop=True)
                    last.then_inc(small_t, 1)
                    for k in range(KD):
                        last = pe.transpose(small[:, 2, k * EXPERTS:(k + 1) * EXPERTS],
                                            gate_rows[:, k * P:(k + 1) * P], ident[0:EXPERTS, 0:EXPERTS])
                    last.then_inc(small_t, 1)

        GBUF = 4
        AHEAD = 2
        GROUP = 4
        y = sb("y", [P, TILES, D])
        y_hi = sb("y_hi", [P, KD, SEQ], F16)
        y_lo = sb("y_lo", [P, KD, SEQ], F16)
        z_hi = sb("z_hi", [P, KD, SEQ], F16)
        z_lo = sb("z_lo", [P, KD, SEQ], F16)
        g_full = sb("g_full", [P, GBUF, SEQ])
        g_hi = sb("g_hi", [P, GBUF, SEQ], F16)
        g_lo = sb("g_lo", [P, GBUF, SEQ], F16)
        acc_sb = sb("acc_sb", [P, KD, SEQ])
        stats = sb("stats", [P, TILES, 6])
        ln_col = sb("ln_col", [P, 4, TILES])
        var = sb("var", [P, TILES])
        rstd = sb("rstd", [P, TILES])
        newton = sb("newton", [P, TILES])
        logit_rows = sb("logit_rows", [EXPERTS, SEQ])
        logit = sb("logit", [P, TILES, EXPERTS])
        logit_sq = sb("logit_sq", [P, TILES, EXPERTS])
        gate_c = sb("gate_c", [P, 5, TILES])
        half_gain = sb("half_gain", [P, TILES])
        qk = sb("qk", [P, 2 * D])
        qk_rot = sb("qk_rot", [P, 2 * D])
        rot = sb("rot", [P, 4, D])
        v_rows = sb("v_rows", [P, TILES, D])
        prod = sb("prod", [P, GROUP * HEADS * HEAD_DIM])
        score = sb("score", [P, TILES * HEADS, HEADS])
        s_col = sb("s_col", [P, 3, TILES * HEADS])
        o_rows = sb("o_rows", [P, TILES, D])
        hid = ctx.enter_context(nc.psum_tensor("hid", [P, 4, SEQ], F32))
        acc = ctx.enter_context(nc.psum_tensor("acc", [P, KD, SEQ], F32))
        turn = ctx.enter_context(nc.psum_tensor("turn", [P, 2, 512], F32))
        turn_rows = turn[:, :, :].rearrange("p a (b d) -> p (a b) d", d=D)

        norm_step = sem("norm_step")
        y_turned = sem("y_turned")
        y_split = sem("y_split")
        up_done = sem("up_done")
        gelu_done = sem("gelu_done")
        tail_done = sem("g_tail_done")
        down_done = sem("down_done")
        acc_out = sem("acc_out")
        acc_turned = sem("acc_turned")
        x_added = sem("x_added")
        logit_done = sem("logit_done")
        logit_turned = sem("logit_turned")
        gate_step = sem("gate_step")
        gate_exp = sem("gate_exp")
        z_turned = sem("z_turned")
        z_split = sem("z_split")
        qkv_done = sem("qkv_done")
        head_step = sem("head_step")
        head_exp = sem("head_exp")

        DENSE, FRONT, BACK = "dense", "front", "back"
        GROUPS = HEADS // GROUP
        TILE_PIECES = 1 + GROUPS
        SHIFT = TILES * TILE_PIECES
        PIECES = SHIFT + 2 + TILES * GROUPS + 1
        EXP_AT = {DENSE: 20, BACK: 6}
        GAIN_AT = {DENSE: 22, BACK: 8, FRONT: 9, None: 9}

        def slot_of(piece, mode):
            if mode == DENSE:
                return 8 + piece // 2 + (3 if piece > SHIFT else 0)
            return 8 + 5 * piece // 4 + (5 if piece > SHIFT else 0)

        def pieces_at(ht, mode):
            slot = ht + (HID_TILES if mode == BACK else 0)
            return [i for i in range(PIECES) if slot_of(i, mode) == slot] if mode else []

        def qkv_at(ht, mode):
            slot = ht + (HID_TILES if mode == BACK else 0)
            return [t for t in range(TILES) if slot_of(t * TILE_PIECES, mode) == slot + 1] if mode else []

        def pe_stage(pe, n, first=False, mode=None, k_batch=None, z_norm=None, prep=None):
            def up(ht):
                if ht == 0:
                    pe.wait_ge(y_split, 4 * (n + 1))
                if not (first and ht < 4):
                    pe.wait_ge(gelu_done, 2 * (n * HID_TILES + ht - 3))
                cols = slice(ht * P, (ht + 1) * P)
                for k in range(KD):
                    last = split_matmul(pe, hid[:, ht % 4, :], w1_hi[:, k, cols], w1_lo[:, k, cols],
                                        y_hi[:, k, :], y_lo[:, k, :], k == 0, k == KD - 1)
                last.then_inc(up_done, 1)

            def down(ht):
                if ht == 0 and not first:
                    pe.wait_ge(acc_out, 2 * n)
                pe.wait_ge(tail_done, n * HID_TILES + ht + 1)
                for k in range(KD):
                    cols = slice(k * P, (k + 1) * P)
                    last = split_matmul(pe, acc[:, k, :], w2_hi[:, ht, cols], w2_lo[:, ht, cols],
                                        g_hi[:, ht % GBUF, :], g_lo[:, ht % GBUF, :],
                                        ht == 0, ht == HID_TILES - 1)
                last.then_inc(down_done, 1)

            for ht in range(AHEAD):
                up(ht)
            for ht in range(HID_TILES):
                if ht + AHEAD < HID_TILES:
                    up(ht + AHEAD)
                if ht == 3:
                    pe.wait_ge(gate_step, n * GATE_STEPS + 1)
                down(ht)
                if ht == 0 and not first:
                    turn_acc(pe, n)
                if ht == 2:
                    if not first:
                        pe.wait_ge(x_added, 4 * n)
                    for k in range(KD):
                        last = split_matmul(pe, turn[0:EXPERTS, 0, :], gate_hi[:, k, :], gate_lo[:, k, :],
                                            y_hi[:, k, :], y_lo[:, k, :], k == 0, k == KD - 1)
                    last.then_inc(logit_done, 1)
                if ht == 3:
                    for t in range(TILES):
                        last = pe.transpose(turn[:, 1, t * EXPERTS:(t + 1) * EXPERTS],
                                            logit_rows[:, t * P:(t + 1) * P], ident[0:EXPERTS, 0:EXPERTS])
                    last.then_inc(logit_turned, 1)
                if mode in (DENSE, FRONT) and ht == 5:
                    pe.wait_ge(norm_step, LN_STEPS * (z_norm + 1))
                    pe.wait_ge(gate_step, n * GATE_STEPS + 2)
                    transpose_tiles(pe, y, turn, ident[:, :]).then_inc(z_turned, 1)
                for t in qkv_at(ht, mode):
                    pe.wait_ge(z_split, 4 * (k_batch + 1))
                    if t > 0:
                        pe.wait_ge(head_step, HEAD_STEPS * k_batch + 16 * (t - 1) + 2)
                    for lo, hi, out in ((0, 2 * D, turn[:, 0, :]), (2 * D, QKV, turn[:, 1, 0:D])):
                        for k in range(KD):
                            for a, (zz, ww) in enumerate(((z_hi, wqkv_hi), (z_hi, wqkv_lo), (z_lo, wqkv_hi))):
                                last = pe.matmul(out, zz[:, k, t * P:(t + 1) * P], ww[:, k, lo:hi],
                                                 start=(k == 0 and a == 0), stop=(k == KD - 1 and a == 2))
                    last.then_inc(qkv_done, 1)
            if prep is not None:
                pe.wait_ge(norm_step, LN_STEPS * (prep + 1))
                if mode in (DENSE, FRONT):
                    pe.wait_ge(head_step, HEAD_STEPS * k_batch + 16 * (TILES - 1) + 2)
                else:
                    pe.wait_ge(gate_step, n * GATE_STEPS + 2)
                transpose_tiles(pe, y, turn, ident[:, :]).then_inc(y_turned, 1)

        def turn_acc(pe, n):
            pe.wait_ge(acc_out, 2 * n)
            for t in range(TILES):
                for k in range(KD):
                    last = pe.transpose(turn_rows[:, t, k * P:(k + 1) * P],
                                        acc_sb[:, k, t * P:(t + 1) * P], ident[:, :])
            last.then_inc(acc_turned, 1)

        def copy_acc(act, n):
            act.wait_ge(down_done, n * HID_TILES)
            for k in range(KD):
                act.activation(acc_sb[:, k, :], acc[:, k, :], ACT.Identity, bias=b2_sum[:, k:k + 1],
                               scale=1.0 / WS).then_inc(acc_out, 1)

        def add_stage(dve, n, batch):
            dve.wait_ge(acc_turned, n)
            dve.wait_ge(gate_step, n * GATE_STEPS)
            for t in range(TILES):
                xt = x[:, batch, t, :]
                dve.scalar_tensor_tensor(xt, turn_rows[:, t, :], half_gain[:, t:t + 1], xt,
                                         ALU.mult, ALU.add).then_inc(x_added, 1)

        def gate_logits(dve, n):
            dve.wait_ge(logit_done, n + 1)
            dve.tensor_scalar(logit_rows[:, :], turn[0:EXPERTS, 0, :], 1.0 / WS, gate_bias[:, 0:1],
                              ALU.mult, ALU.add).then_inc(gate_step, 1)

        def gate_norm(dve, n):
            at = n * GATE_STEPS
            ms, r, t4, mx = (gate_c[:, i, :] for i in range(4))
            wide = [P, TILES, EXPERTS]
            dve.wait_ge(logit_turned, n + 1)
            dve.tensor_copy(logit[:, :, :], turn[:, 1, 0:TILES * EXPERTS].rearrange("p (t e) -> p t e", t=TILES)
                            ).then_inc(gate_step, 1)
            dve.wait_ge(gate_step, at + 2)
            dve.tensor_tensor(logit_sq[:, :, :], logit[:, :, :], logit[:, :, :], ALU.mult).then_inc(gate_step, 1)
            dve.wait_ge(gate_step, at + 3)
            dve.tensor_reduce(ms, logit_sq[:, :, :], AX.X, ALU.add).then_inc(gate_step, 1)
            dve.wait_ge(gate_step, at + 4)
            dve.tensor_scalar(ms, ms, 1.0 / EXPERTS, F32_EPS, ALU.mult, ALU.add).then_inc(gate_step, 1)
            rsqrt_newton(dve, gate_step, at + 5, ms, r, t4)
            dve.wait_ge(gate_step, at + 16)
            dve.tensor_tensor(logit[:, :, :], logit[:, :, :], r.unsqueeze(2).to_broadcast(wide),
                              ALU.mult).then_inc(gate_step, 1)
            dve.wait_ge(gate_step, at + 17)
            dve.tensor_tensor(logit[:, :, :], logit[:, :, :], rms_w[:, :].unsqueeze(1).to_broadcast(wide),
                              ALU.mult).then_inc(gate_step, 1)
            dve.wait_ge(gate_step, at + 18)
            dve.tensor_reduce(mx, logit[:, :, :], AX.X, ALU.max).then_inc(gate_step, 1)
            dve.wait_ge(gate_step, at + 19)
            dve.tensor_tensor(logit[:, :, :], logit[:, :, :], mx.unsqueeze(2).to_broadcast(wide),
                              ALU.subtract).then_inc(gate_step, 1)

        def gate_gain(dve, n):
            at = n * GATE_STEPS + 20
            s = gate_c[:, 4, :]
            dve.wait_ge(gate_exp, n + 1)
            dve.tensor_reduce(s, logit[:, :, :], AX.X, ALU.add).then_inc(gate_step, 1)
            dve.wait_ge(gate_step, at + 1)
            dve.tensor_scalar(s, s, 1e-6, 1.0, ALU.mult, ALU.add).then_inc(gate_step, 1)
            dve.wait_ge(gate_step, at + 2)
            dve.reciprocal(s, s).then_inc(gate_step, 1)
            dve.wait_ge(gate_step, at + 3)
            dve.tensor_scalar(half_gain[:, :], s, 0.5, None, ALU.mult).then_inc(gate_step, 1)

        def split_turned(dve, hi, lo, turned, count, split, at):
            dve.wait_ge(turned, count)
            for k in range(KD):
                dve.tensor_copy(hi[:, k, :], turn[:, k, :]).then_inc(split, 1)
            dve.wait_ge(split, at + KD)
            for k in range(KD):
                dve.tensor_tensor(lo[:, k, :], turn[:, k, :], hi[:, k, :], ALU.subtract).then_inc(split, 1)

        def rows_qkv(dve, j, t):
            at = HEAD_STEPS * j + 16 * t
            dve.wait_ge(qkv_done, TILES * j + t + 1)
            dve.scalar_tensor_tensor(qk[:, :], turn[:, 0, :], 1.0 / WS, qkv_bias[:, 0:2 * D],
                                     ALU.mult, ALU.add).then_inc(head_step, 1)
            dve.scalar_tensor_tensor(v_rows[:, t, :], turn[:, 1, 0:D], 1.0 / WS, qkv_bias[:, 2 * D:QKV],
                                     ALU.mult, ALU.add).then_inc(head_step, 1)
            pairs = qk[:, :].rearrange("p (h i two) -> p h i two", i=HEAD_DIM // 2, two=2)
            out = qk_rot[:, :].rearrange("p (h i two) -> p h i two", i=HEAD_DIM // 2, two=2)
            wide = [P, 2 * HEADS, HEAD_DIM // 2]
            cos = rope[:, t, 0, :].unsqueeze(1).to_broadcast(wide)
            sin = rope[:, t, 1, :].unsqueeze(1).to_broadcast(wide)
            r = [rot[:, i, :].rearrange("p (h i) -> p h i", i=HEAD_DIM // 2) for i in range(4)]
            dve.wait_ge(head_step, at + 1)
            for i, (half, table) in enumerate(((0, cos), (1, sin), (0, sin), (1, cos))):
                dve.tensor_tensor(r[i], pairs[:, :, :, half], table, ALU.mult).then_inc(head_step, 1)
            dve.wait_ge(head_step, at + 6)
            dve.tensor_tensor(out[:, :, :, 0], r[0], r[1], ALU.subtract).then_inc(head_step, 1)
            dve.tensor_tensor(out[:, :, :, 1], r[2], r[3], ALU.add).then_inc(head_step, 1)

        
        def rows_score(dve, j, t, g):
            at = HEAD_STEPS * j + 16 * t + 8 + 2 * g
            wide = [P, GROUP, HEADS, HEAD_DIM]
            q4 = qk_rot[:, g * GROUP * HEAD_DIM:(g + 1) * GROUP * HEAD_DIM].rearrange(
                "p (i d) -> p i d", d=HEAD_DIM).unsqueeze(2).to_broadcast(wide)
            k4 = qk_rot[:, D:2 * D].rearrange("p (j d) -> p j d", d=HEAD_DIM).unsqueeze(1).to_broadcast(wide)
            pr = prod[:, :].rearrange("p (i j d) -> p i j d", i=GROUP, j=HEADS)
            dve.wait_ge(head_step, at)
            dve.tensor_tensor(pr, q4, k4, ALU.mult).then_inc(head_step, 1)
            dve.wait_ge(head_step, at + 1)
            row = t * HEADS + g * GROUP
            dve.tensor_reduce(score[:, row:row + GROUP, :], pr, AX.X, ALU.add).then_inc(head_step, 1)

        def score_shift(dve, j):
            at = HEAD_STEPS * j + 64
            dve.wait_ge(head_step, at)
            dve.tensor_reduce(s_col[:, 0, :], score[:, :, :], AX.X, ALU.max).then_inc(head_step, 1)
            dve.wait_ge(head_step, at + 1)
            dve.tensor_tensor(score[:, :, :], score[:, :, :],
                              s_col[:, 0, :].unsqueeze(2).to_broadcast([P, TILES * HEADS, HEADS]),
                              ALU.subtract).then_inc(head_step, 1)

        def score_sum(dve, j):
            at = HEAD_STEPS * j + 66
            dve.wait_ge(head_exp, j + 1)
            dve.tensor_reduce(s_col[:, 1, :], score[:, :, :], AX.X, ALU.add).then_inc(head_step, 1)
            dve.wait_ge(head_step, at + 1)
            dve.reciprocal(s_col[:, 2, :], s_col[:, 1, :]).then_inc(head_step, 1)

        def rows_values(dve, j, t, g):
            at = HEAD_STEPS * j + 68 + 8 * t + 2 * g
            wide = [P, GROUP, HEAD_DIM, HEADS]
            row = t * HEADS + g * GROUP
            e4 = score[:, row:row + GROUP, :].unsqueeze(2).to_broadcast(wide)
            v4 = v_rows[:, t, :].rearrange("p (j d) -> p d j", d=HEAD_DIM).unsqueeze(1).to_broadcast(wide)
            pr = prod[:, :].rearrange("p (i d j) -> p i d j", i=GROUP, d=HEAD_DIM)
            dve.wait_ge(head_step, at)
            dve.tensor_tensor(pr, e4, v4, ALU.mult).then_inc(head_step, 1)
            dve.wait_ge(head_step, at + 1)
            dve.tensor_reduce(o_rows[:, t, g * GROUP * HEAD_DIM:(g + 1) * GROUP * HEAD_DIM].rearrange(
                "p (i d) -> p i d", d=HEAD_DIM), pr, AX.X, ALU.add).then_inc(head_step, 1)

        def add_attention(dve, j):
            at = HEAD_STEPS * j + 100
            heads = o_rows[:, :, :].rearrange("p t (i d) -> p (t i) d", d=HEAD_DIM)
            dve.wait_ge(head_step, at)
            dve.tensor_tensor(heads, heads, s_col[:, 2, :].unsqueeze(2).to_broadcast([P, TILES * HEADS, HEAD_DIM]),
                              ALU.mult).then_inc(head_step, 1)
            dve.wait_ge(head_step, at + 1)
            dve.tensor_tensor(x[:, j, :, :], x[:, j, :, :], o_rows[:, :, :], ALU.add).then_inc(head_step, 1)

        def normalise(dve, q, batch):
            layernorm_batch(dve, norm_step, LN_STEPS * q, x[:, batch, :, :], y, stats, ln_col,
                            var[:, :], rstd[:, :], newton[:, :])

        def head_piece(dve, j, i):
            if i < SHIFT:
                t, part = i // TILE_PIECES, i % TILE_PIECES
                if part == 0:
                    rows_qkv(dve, j, t)
                else:
                    rows_score(dve, j, t, part - 1)
            elif i == SHIFT:
                score_shift(dve, j)
            elif i == SHIFT + 1:
                score_sum(dve, j)
            elif i < PIECES - 1:
                rows_values(dve, j, (i - SHIFT - 2) // GROUPS, (i - SHIFT - 2) % GROUPS)
            else:
                add_attention(dve, j)

        def dve_stage(dve, n, first=False, prev=None, mode=None, k_batch=None, z_norm=None, prep=None):
            if not first:
                dve.wait_ge(up_done, n * HID_TILES)
            split_turned(dve, y_hi, y_lo, y_turned, n + 1, y_split, 4 * n)
            for ht in range(HID_TILES):
                g = ht % GBUF
                if mode in (DENSE, FRONT) and ht == 3:
                    dve.wait_ge(x_added, 4 * n)
                if mode in (DENSE, BACK) and prep is not None and ht == prep[0]:
                    dve.wait_ge(head_step, HEAD_STEPS * (k_batch + 1))
                dve.wait_ge(gelu_done, 2 * (n * HID_TILES + ht + 1))
                if not (first and ht < GBUF):
                    dve.wait_ge(down_done, n * HID_TILES + ht - GBUF + 1)
                dve.tensor_tensor(g_lo[:, g, :], g_full[:, g, :], g_hi[:, g, :],
                                  ALU.subtract).then_inc(tail_done, 1)
                if ht == 1 and not first:
                    add_stage(dve, n, prev)
                if ht == 2:
                    gate_logits(dve, n)
                if ht == 4:
                    gate_norm(dve, n)
                if ht == GAIN_AT[mode]:
                    gate_gain(dve, n)
                if mode in (DENSE, FRONT) and ht == 3:
                    normalise(dve, z_norm, k_batch)
                if mode in (DENSE, FRONT) and ht == 6:
                    split_turned(dve, z_hi, z_lo, z_turned, k_batch + 1, z_split, 4 * k_batch)
                for i in pieces_at(ht, mode):
                    head_piece(dve, k_batch, i)
                if prep is not None and ht == prep[0]:
                    normalise(dve, prep[1], prep[2])

        def act_stage(act, n, first=False, mode=None, k_batch=None):
            if not first:
                copy_acc(act, n)
            for ht in range(HID_TILES):
                g = ht % GBUF
                act.wait_ge(up_done, n * HID_TILES + ht + 1)
                if not (first and ht < GBUF):
                    act.wait_ge(down_done, n * HID_TILES + ht - GBUF + 1)
                for out in (g_full, g_hi):
                    act.activation(out[:, g, :], hid[:, ht % 4, :], ACT.Gelu, bias=b1_col[:, ht:ht + 1],
                                   scale=1.0 / WS).then_inc(gelu_done, 1)
                if ht == EXP_AT.get(mode, 7):
                    act.wait_ge(gate_step, n * GATE_STEPS + 20)
                    act.activation(logit[:, :, :], logit[:, :, :], ACT.Exp, scale=2.0).then_inc(gate_exp, 1)
                    if mode in EXP_AT:
                        act.wait_ge(head_step, HEAD_STEPS * k_batch + 66)
                        act.activation(score[:, :, :], score[:, :, :], ACT.Exp,
                                       scale=float(HEAD_DIM) ** -0.5).then_inc(head_exp, 1)

        LAST = BATCH - 1

        with nc.Block() as block:
            @block.tensor
            def _(pe):
                pe.wait_ge(norm_step, LN_STEPS)
                transpose_tiles(pe, y, turn, ident[:, :]).then_inc(y_turned, 1)
                pe_stage(pe, 0, first=True, prep=1)
                pe_stage(pe, 1, mode=DENSE, k_batch=0, z_norm=2, prep=3)
                with pe.Fori(1, LAST) as k:
                    pe_stage(pe, 2 * k, mode=FRONT, k_batch=k, z_norm=3 * k + 1, prep=3 * k + 2)
                    pe_stage(pe, 2 * k + 1, mode=BACK, k_batch=k, prep=3 * k + 3)
                pe_stage(pe, 2 * LAST, mode=DENSE, k_batch=LAST, z_norm=3 * LAST + 1, prep=3 * LAST + 2)
                pe_stage(pe, 2 * LAST + 1)
                turn_acc(pe, STAGES)

            @block.vector
            def _(dve):
                normalise(dve, 0, 0)
                dve_stage(dve, 0, first=True, prep=(26, 1, 1))
                dve_stage(dve, 1, prev=0, mode=DENSE, k_batch=0, z_norm=2, prep=(HID_TILES - 1, 3, 0))
                with dve.Fori(1, LAST) as k:
                    dve_stage(dve, 2 * k, prev=k, mode=FRONT, k_batch=k, z_norm=3 * k + 1,
                              prep=(28, 3 * k + 2, k + 1))
                    dve_stage(dve, 2 * k + 1, prev=k - 1, mode=BACK, k_batch=k,
                              prep=(29, 3 * k + 3, k))
                dve_stage(dve, 2 * LAST, prev=LAST, mode=DENSE, k_batch=LAST, z_norm=3 * LAST + 1,
                          prep=(HID_TILES - 1, 3 * LAST + 2, LAST))
                dve_stage(dve, 2 * LAST + 1, prev=LAST - 1)
                add_stage(dve, STAGES, LAST)

            @block.scalar
            def _(act):
                act_stage(act, 0, first=True)
                act_stage(act, 1, mode=DENSE, k_batch=0)
                with act.Fori(1, LAST) as k:
                    act_stage(act, 2 * k, mode=FRONT, k_batch=k)
                    act_stage(act, 2 * k + 1, mode=BACK, k_batch=k)
                act_stage(act, 2 * LAST, mode=DENSE, k_batch=LAST)
                act_stage(act, 2 * LAST + 1)
                copy_acc(act, STAGES)


ROWS = 64
TAKEN = ROWS - 1
PAIRS = BATCH // 2
ALL_TILES = BATCH * TILES
FFN = 1024
ROUTED_EXT = D + 4
SENTINEL = -3.0e38
MASK_FLOOR = -1.0e38
RMS_EPS = 1e-6
TWO_PI_PARTS = (6.28125, 0.0019350051879882812, 3.019916050561733e-07)
ROUND = 1.5 * 2.0 ** 23


def routed_layer(nc, keep, tag, x, ident, io):
    with ExitStack() as ctx:
        def sb(name, shape, dt=F32):
            return ctx.enter_context(nc.sbuf_tensor(f"{tag}_{name}", shape, dt))

        def sem(name):
            return keep.enter_context(nc.semaphore(f"{tag}_{name}"))

        ps = ctx.enter_context(nc.psum_tensor(f"{tag}_ps", [P, 8, 512], F32))
        y = sb("y", [P, BATCH, TILES, ROUTED_EXT])
        one_hot = sb("one_hot", [P, PAIRS, TILES, 2, ROWS])
        slot_hot = sb("slot_hot", [P, PAIRS, TILES, P], F16)
        stay = sb("stay", [P, TILES, BATCH])
        xs = sb("xs", [P, PAIRS, ROUTED_EXT])
        mask_sel = sb("mask_sel", [P, PAIRS, ROWS])
        wqkv = sb("wqkv", [P, KD, QKV])
        wo = sb("wo", [P, KD, D])
        w1 = sb("w1", [P, KD, FFN])
        w2 = sb("w2", [P, FFN // P, D])
        ln1 = sb("ln1", [P, D])
        ln2 = sb("ln2", [P, D])
        inv_freq = sb("inv_freq", [P, HEAD_DIM // 2])
        iota_row = sb("iota_row", [P, ROWS])
        head_block = sb("head_block", [P, 8])
        pair_block = sb("pair_block", [P, 2])

        with ExitStack() as part:
            def tmp(name, shape, dt=F32):
                return part.enter_context(nc.sbuf_tensor(f"{tag}_{name}", shape, dt))

            def tsem(name):
                return keep.enter_context(nc.semaphore(f"{tag}_{name}"))

            router = tmp("router", [P, D])
            router_bias = tmp("router_bias", [P, 1])
            weighed = tmp("weighed", [P, 2, TILES, D])
            w_col = tmp("w_col", [P, BATCH, TILES])
            w_row = tmp("w_row", [BATCH, SEQ])
            work = tmp("work", [BATCH, SEQ])
            best = tmp("best", [BATCH, 8])
            row = tmp("row", [BATCH, 6, SEQ])
            last_at = tmp("last_at", [BATCH, 1])
            slot_col = tmp("slot_col", [P, TILES, BATCH])
            pos_rows = tmp("pos_rows", [16, P], I32)
            pos_rows_f = tmp("pos_rows_f", [16, P])
            mask_idx = tmp("mask_idx", [P, PAIRS], I32)
            mask_rows = tmp("mask_rows", [P, PAIRS, SEQ])
            mask_t = tmp("mask_t", [P, TILES, P])
            stats = tmp("stats", [P, ALL_TILES, 6])
            ln_col = tmp("ln_col", [P, 4, ALL_TILES])
            var = tmp("var", [P, ALL_TILES])
            rstd = tmp("rstd", [P, ALL_TILES])
            shift = tmp("shift", [P, ALL_TILES])
            newton = tmp("newton", [P, ALL_TILES])

            small_in = tsem("small_in")
            weights_in = sem("weights_in")
            made = tsem("made")
            norm_step = tsem("norm_step")
            normed = tsem("normed")
            weigh_step = tsem("weigh_step")
            rows_turned = tsem("rows_turned")
            pick_step = tsem("pick_step")
            cols_turned = tsem("cols_turned")
            hot_step = tsem("hot_step")
            gathered = tsem("gathered")
            sel_out = tsem("sel_out")
            hot_turned = tsem("hot_turned")
            hot_out = tsem("hot_out")
            mask_in = [tsem(f"mask_in{i}") for i in range(PAIRS)]
            mask_turned = tsem("mask_turned")
            mask_out = tsem("mask_out")
            mask_picked = tsem("mask_picked")
            mask_done = tsem("mask_done")

            COLUMNS_AT = ALL_TILES + LN_COLUMN_STEPS
            LN_ON_ACT = TILES - 1
            MASK_BATCHES = 4
            idx_row = row[:, 0, :]
            ones_row = row[:, 1, :]

            with nc.Block() as block:
                @block.sync
                def _(sp):
                    for name in ("router_w",):
                        sp.dma_start(router[:, :], io["router_w"].rearrange("d o -> (d o)").partition_broadcast(P)).then_inc(small_in, 16)
                    sp.dma_start(router_bias[:, :], io["router_b"].partition_broadcast(P)).then_inc(small_in, 16)
                    sp.dma_start(pos_rows[:, :], io["position_ids"][:, 0:SEQ].rearrange("b (t p) -> b t p", p=P)
                                 ).then_inc(small_in, 16)
                    for i, name in enumerate(("wq", "wk", "wv")):
                        sp.dma_start(wqkv[:, :, i * D:(i + 1) * D], io[name].rearrange("(k p) n -> p k n", p=P)).then_inc(weights_in, 16)
                    sp.dma_start(wo[:, :, :], io["wo"].rearrange("(k p) n -> p k n", p=P)).then_inc(weights_in, 16)
                    sp.dma_start(w1[:, :, :], io["w1"].rearrange("(k p) n -> p k n", p=P)).then_inc(weights_in, 16)
                    sp.dma_start(w2[:, :, :], io["w2"].rearrange("(f p) n -> p f n", p=P)).then_inc(weights_in, 16)
                    sp.dma_start(ln1[:, :], io["ln1"].partition_broadcast(P)).then_inc(weights_in, 16)
                    sp.dma_start(ln2[:, :], io["ln2"].partition_broadcast(P)).then_inc(weights_in, 16)
                    sp.dma_start(inv_freq[:, :], io["inv_freq"].partition_broadcast(P)).then_inc(weights_in, 16)

                @block.gpsimd
                def _(pool):
                    pool.iota(iota_row[:, :], pattern=[[1, ROWS]], base=0, channel_multiplier=0,
                              allow_small_or_imprecise_dtypes=True).then_inc(made, 1)
                    pool.iota(idx_row, pattern=[[1, SEQ]], base=1, channel_multiplier=0,
                              allow_small_or_imprecise_dtypes=True).then_inc(made, 1)
                    pool.memset(ones_row, 1.0).then_inc(made, 1)
                    for b in range(BATCH):
                        pool.iota(y[:, b, :, D + 2], pattern=[[P, TILES]], base=min(b, MASK_BATCHES - 1) * 1024,
                                  channel_multiplier=1, allow_small_or_imprecise_dtypes=True).then_inc(made, 1)
                    pool.memset(y[:, :, :, D + 3], 0.0).then_inc(made, 1)
                    pool.memset(head_block[:, :], 1.0).then_inc(made, 1)
                    pool.memset(pair_block[:, :], 1.0).then_inc(made, 1)
                    for m, width, n in ((head_block, HEAD_DIM, 8), (pair_block, ROWS, 2)):
                        pool.wait_ge(made, 14 if m is head_block else 16)
                        pool.affine_select(out=m[:, :], in_=m[:, :], compare_op=ALU.is_ge, fill=0.0, base=0,
                                           pattern=[[-width, n]], channel_multiplier=1).then_inc(made, 1)
                        pool.wait_ge(made, 15 if m is head_block else 17)
                        pool.affine_select(out=m[:, :], in_=m[:, :], compare_op=ALU.is_ge, fill=0.0, base=width - 1,
                                           pattern=[[width, n]], channel_multiplier=-1).then_inc(made, 1)
                    mask_view = io["attention_mask"].rearrange("b o q (h k) -> (b o q h) k", k=SEQ)
                    for pr in range(PAIRS):
                        pool.wait_ge(sel_out, 2 * (pr + 1))
                        pool.indirect_dma_start(out=mask_rows[:, pr, :], out_offset=None, in_=mask_view,
                                                in_offset=bass.IndirectOffsetOnAxis(ap=mask_idx[:, pr:pr + 1], axis=0)
                                                ).then_inc(mask_in[pr], 16)

                @block.vector
                def _(dve):
                    dve.wait_ge(small_in, 48)
                    dve.tensor_copy(pos_rows_f[:, :], pos_rows[:, :]).then_inc(hot_step, 1)
                    with dve.Fori(0, BATCH) as b:
                        for t in range(TILES):
                            dve.bn_stats(stats[:, TILES * b + t, :], x[:, b, t, :]).then_inc(norm_step, 1)
                    layernorm_columns(dve, norm_step, ALL_TILES, stats, ln_col, var[:, :], rstd[:, :], newton[:, :])
                    dve.wait_ge(norm_step, COLUMNS_AT)
                    dve.scalar_tensor_tensor(shift[:, :], ln_col[:, 3, :], -1.0, rstd[:, :], ALU.mult,
                                             ALU.mult).then_inc(norm_step, 1)
                    dve.wait_ge(norm_step, COLUMNS_AT + 1)
                    with dve.Fori(0, BATCH // 2) as two:
                        for i in range(2):
                            b = 2 * two + i
                            col = TILES * b + LN_ON_ACT
                            dve.tensor_scalar(y[:, b, LN_ON_ACT, 0:D], x[:, b, LN_ON_ACT, :], rstd[:, bass.ds(col, 1)],
                                              shift[:, bass.ds(col, 1)], ALU.mult, ALU.add).then_inc(weigh_step, 1)
                            dve.wait_ge(normed, LN_ON_ACT * (b + 1))
                            dve.wait_ge(weigh_step, 3 * b + 1)
                            dve.tensor_tensor(weighed[:, i, :, :], y[:, b, :, 0:D],
                                              router[:, :].unsqueeze(1).to_broadcast([P, TILES, D]),
                                              ALU.mult).then_inc(weigh_step, 1)
                            dve.wait_ge(weigh_step, 3 * b + 2)
                            dve.tensor_reduce(w_col[:, b, :], weighed[:, i, :, :], AX.X, ALU.add).then_inc(weigh_step, 1)
                    dve.wait_ge(weigh_step, 3 * BATCH)
                    dve.tensor_scalar(w_col[:, :, :], w_col[:, :, :], router_bias[:, 0:1], None,
                                      ALU.add).then_inc(weigh_step, 1)
                    dve.wait_ge(weigh_step, 3 * BATCH + 1)
                    dve.wait_ge(made, 18)
                    dve.tensor_copy(y[:, :, :, D], w_col[:, :, :]).then_inc(hot_step, 1)
                    dve.wait_ge(cols_turned, 1)
                    pos_cols = ps[:, 1, 0:16].rearrange("p (b t) -> p b t", t=TILES)
                    dve.tensor_copy(y[:, 0:MASK_BATCHES, :, D + 1], pos_cols).then_inc(hot_step, 1)
                    dve.tensor_copy(y[:, MASK_BATCHES:BATCH, :, D + 1],
                                    pos_cols[:, MASK_BATCHES - 1:MASK_BATCHES, :].to_broadcast(
                                        [P, BATCH - MASK_BATCHES, TILES])).then_inc(hot_step, 1)
                    dve.wait_ge(rows_turned, 1)
                    dve.tensor_copy(w_row[:, :], ps[0:BATCH, 0, :]).then_inc(pick_step, 1)
                    dve.wait_ge(pick_step, 1)
                    dve.tensor_copy(work[:, :], w_row[:, :]).then_inc(pick_step, 1)
                    for r in range(ROWS // 8):
                        dve.wait_ge(pick_step, 2 + 2 * r)
                        dve.max(best[:, :], work[:, :]).then_inc(pick_step, 1)
                        dve.wait_ge(pick_step, 3 + 2 * r)
                        dve.match_replace(out=work[:, :], in_to_replace=best[:, :], in_values=work[:, :],
                                          imm_value=SENTINEL).then_inc(pick_step, 1)
                    at = 2 + 2 * (ROWS // 8)
                    least = best[:, 7:8]
                    taken, tied, cum = row[:, 2, :], row[:, 3, :], row[:, 4, :]
                    slot, pass_row = row[:, 5, :], row[:, 3, :]
                    dve.wait_ge(pick_step, at)
                    dve.tensor_scalar(taken, work[:, :], SENTINEL, None, ALU.is_equal).then_inc(pick_step, 1)
                    dve.wait_ge(pick_step, at + 1)
                    dve.scalar_tensor_tensor(tied, w_row[:, :], least, taken, ALU.is_equal, ALU.mult).then_inc(pick_step, 1)
                    dve.wait_ge(pick_step, at + 2)
                    dve.tensor_tensor(tied, tied, idx_row, ALU.mult).then_inc(pick_step, 1)
                    dve.wait_ge(pick_step, at + 3)
                    dve.tensor_reduce(last_at[:, :], tied, AX.X, ALU.max).then_inc(pick_step, 1)
                    dve.wait_ge(pick_step, at + 4)
                    dve.scalar_tensor_tensor(taken, idx_row, last_at[:, 0:1], taken, ALU.not_equal,
                                             ALU.mult).then_inc(pick_step, 1)
                    dve.wait_ge(pick_step, at + 5)
                    dve.tensor_tensor_scan(cum, ones_row, taken, 0.0, ALU.mult, ALU.add).then_inc(pick_step, 1)
                    dve.wait_ge(pick_step, at + 6)
                    dve.tensor_tensor(slot, cum, taken, ALU.mult).then_inc(pick_step, 1)
                    dve.wait_ge(pick_step, at + 7)
                    dve.tensor_scalar(slot, slot, -1.0, None, ALU.add).then_inc(pick_step, 1)
                    dve.tensor_scalar(pass_row, w_row[:, :], least, 0.5, ALU.is_le, ALU.mult).then_inc(pick_step, 1)
                    dve.wait_ge(cols_turned, 2)
                    dve.tensor_copy(slot_col[:, :, :], ps[:, 2, 0:TILES * BATCH].rearrange("p (t b) -> p t b", b=BATCH)
                                    ).then_inc(hot_step, 1)
                    dve.tensor_copy(stay[:, :, :], ps[:, 2, 64:64 + TILES * BATCH].rearrange("p (t b) -> p t b", b=BATCH)
                                    ).then_inc(hot_step, 1)
                    dve.wait_ge(hot_step, 6)
                    for b in range(BATCH):
                        dve.tensor_tensor(one_hot[:, b // 2, :, b % 2, :],
                                          iota_row[:, :].unsqueeze(1).to_broadcast([P, TILES, ROWS]),
                                          slot_col[:, :, b:b + 1].to_broadcast([P, TILES, ROWS]),
                                          ALU.is_equal).then_inc(hot_step, 1)
                    for pr in range(PAIRS):
                        dve.wait_ge(gathered, pr + 1)
                        dve.tensor_copy(xs[:, pr, :], ps[:, 3 + pr, 0:ROUTED_EXT]).then_inc(sel_out, 1)
                        dve.tensor_scalar(mask_idx[:, pr:pr + 1], ps[:, 3 + pr, D + 2:D + 3], 2.0, None,
                                          ALU.mult).then_inc(sel_out, 1)
                    for pr in range(PAIRS):
                        dve.wait_ge(mask_turned, pr + 1)
                        if pr > 0:
                            dve.wait_ge(mask_picked, pr)
                        dve.tensor_scalar(mask_t[:, :, :], ps[:, 3 + pr % 2, :].rearrange("p (t r) -> p t r", t=TILES),
                                          MASK_FLOOR, None, ALU.max).then_inc(mask_out, 1)
                        dve.wait_ge(mask_picked, pr + 1)
                        for i in range(2):
                            own = slice(i * ROWS, (i + 1) * ROWS)
                            dve.tensor_copy(mask_sel[own, pr, :], ps[own, 5 + pr % 2, own]).then_inc(mask_done, 1)
                    dve.wait_ge(mask_done, 2 * PAIRS)
                    dve.memset(mask_sel[:, :, TAKEN:ROWS], SENTINEL)

                @block.tensor
                def _(pe):
                    pe.wait_ge(hot_step, 1)
                    pe.transpose(ps[:, 1, 0:16], pos_rows_f[:, :], ident[0:16, 0:16]).then_inc(cols_turned, 1)
                    pe.wait_ge(weigh_step, 3 * BATCH + 1)
                    for t in range(TILES):
                        last = pe.transpose(ps[0:BATCH, 0, t * P:(t + 1) * P], w_col[:, :, t], ident[:, :])
                    last.then_inc(rows_turned, 1)
                    pe.wait_ge(pick_step, 2 + 2 * (ROWS // 8) + 9)
                    for i, r in ((0, 5), (1, 3)):
                        for t in range(TILES):
                            at = 64 * i + t * BATCH
                            last = pe.transpose(ps[:, 2, at:at + BATCH], row[:, r, t * P:(t + 1) * P],
                                                ident[0:BATCH, 0:BATCH])
                    last.then_inc(cols_turned, 1)
                    for pr in range(PAIRS):
                        pe.wait_ge(hot_step, 6 + 2 * (pr + 1))
                        for i in range(2):
                            for t in range(TILES):
                                last = pe.matmul(ps[i * ROWS:(i + 1) * ROWS, 3 + pr, 0:ROUTED_EXT],
                                                 one_hot[:, pr, t, i, :], y[:, 2 * pr + i, t, :],
                                                 start=(t == 0), stop=(t == TILES - 1))
                        last.then_inc(gathered, 1)
                    for pr in range(PAIRS):
                        bank = (7, 0)[pr % 2]
                        if pr >= 2:
                            pe.wait_ge(hot_out, pr - 1)
                        for t in range(TILES):
                            last = pe.transpose(ps[:, bank, t * P:(t + 1) * P],
                                                one_hot[:, pr, t, :, :].rearrange("p i r -> p (i r)"), ident[:, :])
                        last.then_inc(hot_turned, 1)
                    for pr in range(PAIRS):
                        pe.wait_ge(mask_in[pr], 16)
                        if pr == 0:
                            pe.wait_ge(sel_out, 2 * PAIRS)
                        if pr >= 2:
                            pe.wait_ge(mask_done, 2 * (pr - 1))
                        for t in range(TILES):
                            last = pe.transpose(ps[:, 3 + pr % 2, t * P:(t + 1) * P],
                                                mask_rows[:, pr, t * P:(t + 1) * P], ident[:, :])
                        last.then_inc(mask_turned, 1)
                        pe.wait_ge(mask_out, pr + 1)
                        for t in range(TILES):
                            last = pe.matmul(ps[:, 5 + pr % 2, 0:P], mask_t[:, t, :],
                                             one_hot[:, pr, t, :, :].rearrange("p i r -> p (i r)"),
                                             start=(t == 0), stop=(t == TILES - 1))
                        last.then_inc(mask_picked, 1)

                @block.scalar
                def _(act):
                    act.wait_ge(norm_step, COLUMNS_AT + 1)
                    with act.Fori(0, BATCH) as b:
                        for t in range(LN_ON_ACT):
                            col = TILES * b + t
                            act.activation(y[:, b, t, 0:D], x[:, b, t, :], ACT.Identity, bias=shift[:, bass.ds(col, 1)],
                                           scale=rstd[:, bass.ds(col, 1)]).then_inc(normed, 1)
                    for pr in range(PAIRS):
                        act.wait_ge(hot_turned, pr + 1)
                        act.activation(slot_hot[:, pr, :, :].rearrange("p t n -> p (t n)"),
                                       ps[:, (7, 0)[pr % 2], :], ACT.Copy).then_inc(hot_out, 1)

        h = sb("h", [P, PAIRS, D])
        h_t = sb("h_t", [P, KD, PAIRS * P])
        sq = sb("sq", [P, PAIRS, D])
        col = sb("col", [P, 4, PAIRS])
        ang = sb("ang", [P, 4, PAIRS * HEAD_DIM // 2])
        rope = sb("rope", [P, 2, PAIRS, HEAD_DIM // 2])
        rot = sb("rot", [P, 4, D])
        qk = sb("qk", [P, 2, 2 * D])
        q_t = sb("q_t", [P, PAIRS, KD, P])
        k_blk = sb("k_blk", [P, PAIRS, KD, 2, 8, ROWS])
        v_blk = sb("v_blk", [P, BATCH, 8, 2, HEAD_DIM])
        s = sb("s", [P, 2, HEADS, ROWS])
        s_col = sb("s_col", [P, 2, 3, HEADS])
        p_t = sb("p_t", [P, 2, 8, P])
        o = sb("o", [P, 2, D])
        o_t = sb("o_t", [P, 2, KD, P])
        x1 = sb("x1", [P, PAIRS, D])
        gel = k_blk[:, :, :, :, :, :].rearrange("p r a i h c -> p (r a i) (h c)")[:, 0:FFN // P, :]
        proc = sb("proc", [P, PAIRS, D])
        proc_hi = sb("proc_hi", [P, PAIRS, D], F16)
        proc_lo = sb("proc_lo", [P, PAIRS, D], F16)

        rms_step = sem("rms_step")
        h_turned = sem("h_turned")
        h_out = sem("h_out")
        qk_done = sem("qk_done")
        v_done = sem("v_done")
        v_out = sem("v_out")
        ang_step = sem("ang_step")
        sin_done = sem("sin_done")
        rot_step = sem("rot_step")
        qk_turned = sem("qk_turned")
        qt_out = sem("qt_out")
        kb_out = sem("kb_out")
        s_done = sem("s_done")
        s_step = sem("s_step")
        sum_step = sem("sum_step")
        s_exp = sem("s_exp")
        p_turned = sem("p_turned")
        p_out = sem("p_out")
        o_done = sem("o_done")
        o_out = sem("o_out")
        o_turned = sem("o_turned")
        ot_out = sem("ot_out")
        wo_done = sem("wo_done")
        x1_out = sem("x1_out")
        up_done = sem("up_done")
        gel_out = sem("gel_out")
        down_done = sem("down_done")
        proc_step = sem("proc_step")
        put_done = sem("put_done")
        passed = sem("passed")
        put_out = sem("put_out")

        RMS_STEPS = 3 + RSQRT_STEPS + PAIRS

        def rmsnorm(dve, call, src, gain, bank_src=None):
            at = call * RMS_STEPS
            dve.tensor_tensor(sq[:, :, :], src, src, ALU.mult).then_inc(rms_step, 1)
            dve.wait_ge(rms_step, at + 1)
            dve.tensor_reduce(col[:, 0, :], sq[:, :, :], AX.X, ALU.add).then_inc(rms_step, 1)
            dve.wait_ge(rms_step, at + 2)
            dve.tensor_scalar(col[:, 0, :], col[:, 0, :], 1.0 / D, RMS_EPS, ALU.mult, ALU.add).then_inc(rms_step, 1)
            rsqrt_newton(dve, rms_step, at + 3, col[:, 0, :], col[:, 1, :], col[:, 2, :])
            dve.wait_ge(rms_step, at + 3 + RSQRT_STEPS)
            for pr in range(PAIRS):
                dve.scalar_tensor_tensor(h[:, pr, :], src[:, pr, :], col[:, 1, pr:pr + 1], gain[:, :],
                                         ALU.mult, ALU.mult).then_inc(rms_step, 1)

        def angles(dve):
            n = PAIRS * HEAD_DIM // 2
            a, k, r = ang[:, 0, :], ang[:, 1, :], ang[:, 2:4, :]
            dve.tensor_tensor(a.rearrange("p (r i) -> p r i", r=PAIRS),
                              xs[:, :, D + 1:D + 2].to_broadcast([P, PAIRS, HEAD_DIM // 2]),
                              inv_freq[:, :].unsqueeze(1).to_broadcast([P, PAIRS, HEAD_DIM // 2]),
                              ALU.mult).then_inc(ang_step, 1)
            at = 1
            for i, quarter in enumerate((0.0, 0.25)):
                dve.wait_ge(ang_step, at)
                dve.tensor_scalar(k, a, float(1.0 / (2.0 * np.pi)), quarter, ALU.mult, ALU.add).then_inc(ang_step, 1)
                dve.wait_ge(ang_step, at + 1)
                dve.tensor_scalar(k, k, ROUND, None, ALU.add).then_inc(ang_step, 1)
                dve.wait_ge(ang_step, at + 2)
                dve.tensor_scalar(k, k, ROUND, None, ALU.subtract).then_inc(ang_step, 1)
                src = a
                for m, part in enumerate(TWO_PI_PARTS):
                    dve.wait_ge(ang_step, at + 3 + m)
                    dve.scalar_tensor_tensor(r[:, i, :], k, -part, src, ALU.mult, ALU.add).then_inc(ang_step, 1)
                    src = r[:, i, :]
                dve.wait_ge(ang_step, at + 6)
                dve.tensor_scalar(r[:, i, :], r[:, i, :], float(np.pi / 2) * i, float(np.float32(np.pi)) * (1 - 1e-7),
                                  ALU.add, ALU.min).then_inc(ang_step, 1)
                dve.wait_ge(ang_step, at + 7)
                dve.tensor_scalar(r[:, i, :], r[:, i, :], -float(np.float32(np.pi)) * (1 - 1e-7), None,
                                  ALU.max).then_inc(ang_step, 1)
                at += 8

        ANG_STEPS = 1 + 16

        S_BANK, W_BANK = (6, 0, 6, 0), (2, 4, 2, 4)
        PUT_BANK = (2, 4, 6, 0)

        def turn_qk(pe, pr):
            pe.wait_ge(rot_step, 6 * (pr + 1))
            for m in range(4):
                last = pe.transpose(ps[:, 2 + pr, m * P:(m + 1) * P], qk[:, pr % 2, m * P:(m + 1) * P], ident[:, :])
            last.then_inc(qk_turned, 1)

        def scores(pe, pr):
            lo = S_BANK[pr]
            if pr < 2:
                pe.wait_ge(v_out, (4, 8)[pr])
            else:
                pe.wait_ge(s_step, 4 * (pr - 2) + 2)
            pe.wait_ge(qt_out, pr + 1)
            pe.wait_ge(kb_out, 4 * (pr + 1))
            for half in range(KD):
                for i in range(2):
                    last = pe.matmul(ps[i * ROWS:(i + 1) * ROWS, lo + half, :],
                                     q_t[:, pr, half, i * ROWS:(i + 1) * ROWS],
                                     k_blk[:, pr, half, i, :, :].rearrange("p h c -> p (h c)"),
                                     start=True, stop=True)
            last.then_inc(s_done, 1)

        def turn_p(pe, pr):
            lo = W_BANK[pr]
            pe.wait_ge(s_exp, pr + 1)
            pe.wait_ge(qt_out, lo)
            if pr >= 2:
                pe.wait_ge(x1_out, pr - 1)
            for m in range(8):
                last = pe.transpose(ps[:, lo + m // 4, (m % 4) * P:(m % 4 + 1) * P],
                                    s[:, pr % 2, 2 * m:2 * m + 2, :].rearrange("p h c -> p (h c)"), ident[:, :])
            last.then_inc(p_turned, 1)

        def values(pe, pr):
            pe.wait_ge(p_out, 2 * (pr + 1))
            for i in range(2):
                for m in range(8):
                    last = pe.matmul(ps[i * ROWS:(i + 1) * ROWS, W_BANK[pr], m * 32:(m + 1) * 32],
                                     p_t[:, pr % 2, m, i * ROWS:(i + 1) * ROWS],
                                     v_blk[:, 2 * pr + i, m, :, :].rearrange("p h d -> p (h d)"),
                                     start=True, stop=True)
            last.then_inc(o_done, 1)

        def turn_o(pe, pr):
            pe.wait_ge(o_out, pr + 1)
            for k in range(KD):
                last = pe.transpose(ps[:, W_BANK[pr] + 1, k * P:(k + 1) * P], o[:, pr % 2, k * P:(k + 1) * P], ident[:, :])
            last.then_inc(o_turned, 1)

        def project(pe, pr):
            pe.wait_ge(ot_out, pr + 1)
            for k in range(KD):
                last = pe.matmul(ps[:, W_BANK[pr], D:2 * D], o_t[:, pr % 2, k, :], wo[:, k, :],
                                 start=(k == 0), stop=(k == KD - 1))
            last.then_inc(wo_done, 1)

        def rotate(dve, pr):
            half = HEAD_DIM // 2
            wide = [P, 2 * HEADS, half]
            src = ps[:, 2 + pr, :].rearrange("p (h two i) -> p h two i", two=2, i=half)
            out = qk[:, pr % 2, :].rearrange("p (h two i) -> p h two i", two=2, i=half)
            cos = rope[:, 1, pr, :].unsqueeze(1).to_broadcast(wide)
            sin = rope[:, 0, pr, :].unsqueeze(1).to_broadcast(wide)
            r = [rot[:, m, :].rearrange("p (h i) -> p h i", i=half) for m in range(4)]
            dve.wait_ge(qk_done, pr + 1)
            if pr > 0:
                dve.wait_ge(rot_step, 6 * pr)
            for m, (a, table) in enumerate(((0, cos), (1, sin), (0, sin), (1, cos))):
                dve.tensor_tensor(r[m], src[:, :, a, :], table, ALU.mult).then_inc(rot_step, 1)
            dve.wait_ge(rot_step, 6 * pr + 4)
            dve.tensor_tensor(out[:, :, 0, :], r[0], r[1], ALU.subtract).then_inc(rot_step, 1)
            dve.tensor_tensor(out[:, :, 1, :], r[2], r[3], ALU.add).then_inc(rot_step, 1)

        def key_blocks(dve, pr):
            dve.wait_ge(qk_turned, pr + 1)
            for half in range(KD):
                for i in range(2):
                    at = (2 + half) * P + i * ROWS
                    dve.tensor_tensor(k_blk[:, pr, half, i, :, :],
                                      ps[:, 2 + pr, at:at + ROWS].unsqueeze(1).to_broadcast([P, 8, ROWS]),
                                      head_block[:, :].unsqueeze(2).to_broadcast([P, 8, ROWS]),
                                      ALU.mult).then_inc(kb_out, 1)

        def softmax_shift(dve, pr):
            lo = S_BANK[pr]
            at = 4 * pr
            sv, mx = s[:, pr % 2, :, :], s_col[:, pr % 2, 0, :]
            dve.wait_ge(s_done, pr + 1)
            if pr >= 2:
                dve.wait_ge(p_turned, pr - 1)
            for half in range(KD):
                dve.scalar_tensor_tensor(sv[:, half * 8:(half + 1) * 8, :],
                                         ps[:, lo + half, :].rearrange("p (h c) -> p h c", c=ROWS), 0.25,
                                         mask_sel[:, pr, :].unsqueeze(1).to_broadcast([P, 8, ROWS]),
                                         ALU.mult, ALU.add).then_inc(s_step, 1)
            dve.wait_ge(s_step, at + 2)
            dve.tensor_reduce(mx, sv, AX.X, ALU.max).then_inc(s_step, 1)
            dve.wait_ge(s_step, at + 3)
            dve.tensor_tensor(sv, sv, mx.unsqueeze(2).to_broadcast([P, HEADS, ROWS]), ALU.subtract).then_inc(s_step, 1)

        def softmax_sum(dve, pr):
            total, inv = (s_col[:, pr % 2, m, :] for m in (1, 2))
            dve.wait_ge(s_exp, pr + 1)
            dve.tensor_reduce(total, s[:, pr % 2, :, :], AX.X, ALU.add).then_inc(sum_step, 1)
            dve.wait_ge(sum_step, 2 * pr + 1)
            dve.reciprocal(inv, total).then_inc(sum_step, 1)

        def divide(dve, pr):
            dve.wait_ge(o_done, pr + 1)
            dve.wait_ge(sum_step, 2 * (pr + 1))
            dve.tensor_tensor(o[:, pr % 2, :].rearrange("p (h d) -> p h d", d=HEAD_DIM),
                              ps[:, W_BANK[pr], 0:D].rearrange("p (h d) -> p h d", d=HEAD_DIM),
                              s_col[:, pr % 2, 2, :].unsqueeze(2).to_broadcast([P, HEADS, HEAD_DIM]),
                              ALU.mult).then_inc(o_out, 1)

        def add_selected(dve, pr):
            dve.wait_ge(wo_done, pr + 1)
            dve.tensor_tensor(x1[:, pr, :], ps[:, W_BANK[pr], D:2 * D], xs[:, pr, 0:D], ALU.add).then_inc(x1_out, 1)

        with nc.Block() as block:
            @block.tensor
            def _(pe):
                def turn_h(call, count):
                    pe.wait_ge(rms_step, count)
                    for k in range(KD):
                        for pr in range(PAIRS):
                            last = pe.transpose(ps[:, k, pr * P:(pr + 1) * P], h[:, pr, k * P:(k + 1) * P], ident[:, :])
                    last.then_inc(h_turned, 1)

                turn_h(0, RMS_STEPS)
                pe.wait_ge(h_out, 2)
                pe.wait_ge(weights_in, 16 * 9)
                for pr in range(PAIRS):
                    for k in range(KD):
                        last = pe.matmul(ps[:, 2 + pr, :], h_t[:, k, pr * P:(pr + 1) * P], wqkv[:, k, 0:2 * D],
                                         start=(k == 0), stop=(k == KD - 1))
                    last.then_inc(qk_done, 1)
                for pr in range(PAIRS):
                    bank = (6, 7, 0, 1)[pr]
                    for i in range(2):
                        at = (2 * pr + i) * ROWS
                        for c in range(2):
                            for k in range(KD):
                                last = pe.matmul(ps[c * ROWS:(c + 1) * ROWS, bank, i * D:(i + 1) * D],
                                                 h_t[:, k, at:at + ROWS], wqkv[:, k, 2 * D:QKV],
                                                 start=(k == 0), stop=(k == KD - 1))
                    last.then_inc(v_done, 1)
                for piece, pr in ((turn_qk, 0), (scores, 0), (turn_qk, 1), (scores, 1), (turn_qk, 2), (turn_p, 0),
                                  (scores, 2), (values, 0), (turn_qk, 3), (turn_o, 0), (scores, 3), (project, 0),
                                  (turn_p, 1), (values, 1), (turn_p, 2), (turn_o, 1), (values, 2), (project, 1),
                                  (turn_p, 3), (turn_o, 2), (values, 3), (project, 2), (turn_o, 3), (project, 3)):
                    piece(pe, pr)
                turn_h(1, 2 * RMS_STEPS)
                pe.wait_ge(h_out, 4)
                for f in range(FFN // P):
                    if f >= 4:
                        pe.wait_ge(gel_out, f - 3)
                    for k in range(KD):
                        last = pe.matmul(ps[:, 2 + f % 4, :], w1[:, k, f * P:(f + 1) * P], h_t[:, k, :],
                                         start=(k == 0), stop=(k == KD - 1))
                    last.then_inc(up_done, 1)
                for pr in range(PAIRS):
                    for f in range(FFN // P):
                        if pr == 0:
                            pe.wait_ge(gel_out, f + 1)
                        last = pe.matmul(ps[:, (6, 7, 0, 1)[pr], 0:D], gel[:, f, pr * P:(pr + 1) * P],
                                         w2[:, f, :], start=(f == 0), stop=(f == FFN // P - 1))
                    last.then_inc(down_done, 1)
                for b in range(BATCH):
                    pr, i = b // 2, b % 2
                    pe.wait_ge(proc_step, 4 * max(pr + 1, 2 if b == 2 else 0))
                    if b == 3:
                        pe.wait_ge(proc_step, 4 * PAIRS)
                    if b >= 4:
                        pe.wait_ge(put_out, b - 3)
                    rows = slice(i * ROWS, (i + 1) * ROWS)
                    for t in range(TILES):
                        out = ps[:, PUT_BANK[b % 4] + t // 2, (t % 2) * D:(t % 2 + 1) * D]
                        pe.matmul(out, slot_hot[rows, pr, t, :], proc_hi[rows, pr, :], start=True, stop=False)
                        last = pe.matmul(out, slot_hot[rows, pr, t, :], proc_lo[rows, pr, :], start=False, stop=True)
                    last.then_inc(put_done, 1)

            @block.vector
            def _(dve):
                dve.wait_ge(weights_in, 16 * 9)
                rmsnorm(dve, 0, xs[:, :, 0:D], ln1)
                angles(dve)
                for b in range(BATCH):
                    pr, i = b // 2, b % 2
                    dve.wait_ge(v_done, pr + 1)
                    src = ps[:, (6, 7, 0, 1)[pr], i * D:(i + 1) * D].rearrange("p (m h d) -> p m h d", m=8, h=2)
                    dve.tensor_tensor(v_blk[:, b, :, :, :], src,
                                      pair_block[:, :].unsqueeze(1).unsqueeze(3).to_broadcast([P, 8, 2, HEAD_DIM]),
                                      ALU.mult).then_inc(v_out, 1)
                dve.wait_ge(sin_done, 1)
                for piece, pr in ((rotate, 0), (key_blocks, 0), (rotate, 1), (key_blocks, 1), (softmax_shift, 0),
                                  (rotate, 2), (softmax_shift, 1), (key_blocks, 2), (softmax_sum, 0), (rotate, 3),
                                  (divide, 0), (key_blocks, 3), (softmax_sum, 1), (softmax_shift, 2),
                                  (add_selected, 0), (divide, 1), (softmax_shift, 3), (softmax_sum, 2),
                                  (add_selected, 1), (divide, 2), (softmax_sum, 3), (add_selected, 2),
                                  (divide, 3), (add_selected, 3)):
                    piece(dve, pr)
                dve.wait_ge(x1_out, PAIRS)
                rmsnorm(dve, 1, x1[:, :, :], ln2)
                for b in range(BATCH):
                    for t in range(TILES):
                        xt = x[:, b, t, :]
                        dve.scalar_tensor_tensor(xt, y[:, b, t, 0:D], stay[:, t, b:b + 1], xt,
                                                 ALU.mult, ALU.add).then_inc(passed, 1)
                for pr in range(PAIRS):
                    dve.wait_ge(down_done, pr + 1)
                    dve.tensor_tensor(proc[:, pr, :], ps[:, (6, 7, 0, 1)[pr], 0:D], x1[:, pr, :],
                                      ALU.add).then_inc(proc_step, 1)
                    dve.wait_ge(proc_step, 4 * pr + 1)
                    dve.tensor_scalar(proc[:, pr, :], proc[:, pr, :], xs[:, pr, D:D + 1], None,
                                      ALU.mult).then_inc(proc_step, 1)
                    dve.wait_ge(proc_step, 4 * pr + 2)
                    dve.tensor_copy(proc_hi[:, pr, :], proc[:, pr, :]).then_inc(proc_step, 1)
                    dve.wait_ge(proc_step, 4 * pr + 3)
                    dve.tensor_tensor(proc_lo[:, pr, :], proc[:, pr, :], proc_hi[:, pr, :],
                                      ALU.subtract).then_inc(proc_step, 1)
                for b in range(BATCH):
                    dve.wait_ge(put_done, b + 1)
                    dve.wait_ge(passed, TILES * (b + 1))
                    two = PUT_BANK[b % 4]
                    dve.scalar_tensor_tensor(x[:, b, :, :].rearrange("p t d -> p (t d)"),
                                             ps[:, two:two + 2, :].rearrange("p a n -> p (a n)"), 0.5,
                                             x[:, b, :, :].rearrange("p t d -> p (t d)"),
                                             ALU.mult, ALU.add).then_inc(put_out, 1)

            @block.scalar
            def _(act):
                def h_copy(call):
                    act.wait_ge(h_turned, call + 1)
                    for k in range(KD):
                        act.activation(h_t[:, k, :], ps[:, k, :], ACT.Copy).then_inc(h_out, 1)

                def queries_copy(pr):
                    act.wait_ge(kb_out, 4 * (pr + 1))
                    act.activation(q_t[:, pr, :, :].rearrange("p k n -> p (k n)"), ps[:, 2 + pr, 0:2 * P],
                                   ACT.Copy).then_inc(qt_out, 1)

                def exponential(pr):
                    act.wait_ge(s_step, 4 * (pr + 1))
                    act.activation(s[:, pr % 2, :, :], s[:, pr % 2, :, :], ACT.Exp).then_inc(s_exp, 1)

                def p_copy(pr):
                    act.wait_ge(p_turned, pr + 1)
                    for m in range(2):
                        act.activation(p_t[:, pr % 2, 4 * m:4 * m + 4, :].rearrange("p m n -> p (m n)"),
                                       ps[:, W_BANK[pr] + m, :], ACT.Copy).then_inc(p_out, 1)

                def o_copy(pr):
                    act.wait_ge(o_turned, pr + 1)
                    act.activation(o_t[:, pr % 2, :, :].rearrange("p k n -> p (k n)"), ps[:, W_BANK[pr] + 1, 0:D],
                                   ACT.Copy).then_inc(ot_out, 1)

                h_copy(0)
                act.wait_ge(ang_step, ANG_STEPS)
                act.activation(rope[:, :, :, :].rearrange("p c r i -> p (c r i)"),
                               ang[:, 2:4, :].rearrange("p c n -> p (c n)"), ACT.Sin).then_inc(sin_done, 1)
                for piece, pr in ((queries_copy, 0), (queries_copy, 1), (exponential, 0), (queries_copy, 2),
                                  (p_copy, 0), (exponential, 1), (queries_copy, 3), (o_copy, 0), (p_copy, 1),
                                  (exponential, 2), (p_copy, 2), (o_copy, 1), (exponential, 3), (p_copy, 3),
                                  (o_copy, 2), (o_copy, 3)):
                    piece(pr)
                h_copy(1)
                for f in range(FFN // P):
                    act.wait_ge(up_done, f + 1)
                    act.activation(gel[:, f, :], ps[:, 2 + f % 4, :], ACT.Gelu_apprx_tanh).then_inc(gel_out, 1)


BF16 = mybir.dt.bfloat16
LATENT = 64
MLA_HEADS, MLA_DIM = 16, 64
MLA_PAIRS = MLA_HEADS // 2
BLOCKED = -1.0e30
M_SCALE, INV_SCALE = 64.0, 256.0
GROUP_HEADS = 4
LEAD = 8
RING = LEAD
SUM_SLOTS = 4
KEY_AT = (0, 512, 1024, 896)
KEY_COLS = sum(SEQ - t * P for t in range(TILES))
QUERY_AT = (512 + 384, 1024, 512, 0)


def latent_attention_layer(nc, keep, x, ident, io):
    with ExitStack() as ctx:
        def sb(name, shape, dt=F32):
            return ctx.enter_context(nc.sbuf_tensor(f"mla_{name}", shape, dt))

        def sem(name):
            return keep.enter_context(nc.semaphore(f"mla_{name}"))

        ps = ctx.enter_context(nc.psum_tensor("mla_ps", [P, 8, 512], F32))
        a_hi = sb("a_hi", [P, KD, MLA_HEADS, 2, LATENT], F16)
        a_lo = sb("a_lo", [P, KD, MLA_HEADS, 2, LATENT], F16)
        b_hi = sb("b_hi", [P, MLA_PAIRS, D], F16)
        b_lo = sb("b_lo", [P, MLA_PAIRS, D], F16)
        down_hi = sb("down_hi", [P, KD, 2, LATENT], F16)
        down_lo = sb("down_lo", [P, KD, 2, LATENT], F16)
        ident_b = sb("ident_b", [P, P], BF16)
        block_q = sb("block_q", [P, P], BF16)
        block_k = sb("block_k", [P, P], BF16)
        spread = sb("spread", [P, MLA_HEADS, LATENT], F16)
        val_hi = sb("val_hi", [P, 2, TILES, P], F16)
        val_lo = sb("val_lo", [P, 2, TILES, P], F16)
        key_top = sb("key_top", [P, 2, SEQ], F16)
        q_lo = sb("q_lo", [P, RING, SEQ], F16)
        inv_hl = sb("inv_hl", [P, SEQ], F16)

        with ExitStack() as part:
            def tmp(name, shape, dt=F32):
                return part.enter_context(nc.sbuf_tensor(f"mla_{name}", shape, dt))

            def tsem(name):
                return keep.enter_context(nc.semaphore(f"mla_{name}"))

            wq = tmp("wq", [P, KD, MLA_HEADS * MLA_DIM])
            wk = tmp("wk", [LATENT, MLA_HEADS * MLA_DIM])
            wv = tmp("wv", [LATENT, MLA_HEADS * MLA_DIM])
            wout = tmp("wout", [P, MLA_PAIRS, D])
            down = tmp("down", [P, KD, LATENT])
            wq_t = tmp("wq_t", [P, MLA_PAIRS, D])
            wk_t = tmp("wk_t", [P, MLA_PAIRS, LATENT])
            wv_t = tmp("wv_t", [P, MLA_PAIRS, LATENT])
            spread_f = tmp("spread_f", [P, MLA_HEADS, LATENT])
            block_f = tmp("block_f", [P, 2, P])
            loaded = tsem("loaded")
            made = tsem("made")
            turned = tsem("turned")
            turn_out = tsem("turn_out")
            folded = tsem("folded")
            split = tsem("split")
            const_done = tsem("const_done")
            zeroed = tsem("zeroed")

            with nc.Block() as block:
                @block.sync
                def _(sp):
                    sp.dma_start(wq[:, :, :], io["Wq"].rearrange("(k p) h n -> p k (h n)", p=P)).then_inc(loaded, 16)
                    sp.dma_start(wk[:, :], io["Wk_up"].rearrange("c h n -> c (h n)")).then_inc(loaded, 16)
                    sp.dma_start(wv[:, :], io["Wv_up"].rearrange("c h n -> c (h n)")).then_inc(loaded, 16)
                    sp.dma_start(wout[:, :, :], io["Wout"].rearrange("(m h) n d -> (h n) m d", h=2)).then_inc(loaded, 16)
                    sp.dma_start(down[:, :, :], io["Wkv_down"].rearrange("(k p) c -> p k c", p=P)).then_inc(loaded, 16)

                @block.gpsimd
                def _(pool):
                    pool.memset(spread_f[:, :, :], 0.0).then_inc(made, 1)
                    pool.memset(block_f[:, :, :], 0.0).then_inc(made, 1)
                    for n, base in enumerate((0, -32)):
                        pool.wait_ge(made, 2 + n)
                        pool.affine_select(out=spread_f[:, :, :], in_=spread_f[:, :, :], compare_op=ALU.not_equal,
                                           fill=1.0 / INV_SCALE, base=base, pattern=[[-1, MLA_HEADS], [0, LATENT]],
                                           channel_multiplier=1).then_inc(made, 1)
                    pool.affine_select(out=block_f[:, 0, :], in_=block_f[:, 0, :], compare_op=ALU.is_ge, fill=BLOCKED,
                                       base=0, pattern=[[-1, P]], channel_multiplier=1).then_inc(made, 1)
                    pool.affine_select(out=block_f[:, 1, :], in_=block_f[:, 1, :], compare_op=ALU.is_ge, fill=BLOCKED,
                                       base=0, pattern=[[1, P]], channel_multiplier=-1).then_inc(made, 1)

                @block.tensor
                def _(pe):
                    pe.wait_ge(loaded, 80)
                    for m in range(MLA_PAIRS):
                        for k in range(KD):
                            last = pe.transpose(ps[:, m // 2, (m % 2) * D + k * P:(m % 2) * D + (k + 1) * P],
                                                wq[:, k, m * P:(m + 1) * P], ident[:, :])
                    last.then_inc(turned, 1)
                    for i, w in enumerate((wk, wv)):
                        for m in range(MLA_PAIRS):
                            last = pe.transpose(ps[:, 4 + i, m * LATENT:(m + 1) * LATENT], w[:, m * P:(m + 1) * P],
                                                ident[0:LATENT, 0:LATENT])
                        last.then_inc(turned, 1)
                    pe.wait_ge(turn_out, 6)
                    for m in range(MLA_PAIRS):
                        if m >= 4:
                            pe.wait_ge(split, 2 * (m - 3))
                        for i in range(2):
                            bank = 4 * i + m % 4
                            rows = slice(i * MLA_DIM, (i + 1) * MLA_DIM)
                            for k in range(KD):
                                last = pe.matmul(ps[:, bank, k * LATENT:(k + 1) * LATENT],
                                                 wq_t[rows, m, k * P:(k + 1) * P], wk_t[rows, m, :],
                                                 start=True, stop=True)
                            last = pe.matmul(ps[i * LATENT:(i + 1) * LATENT, bank, D:2 * D],
                                             wv_t[rows, m, :], wout[rows, m, :], start=True, stop=True)
                        last.then_inc(folded, 1)

                @block.vector
                def _(dve):
                    dve.wait_ge(turned, 3)
                    for n in range(4):
                        dve.tensor_copy(wq_t[:, 2 * n:2 * n + 2, :].rearrange("p m d -> p (m d)"),
                                        ps[:, n, :]).then_inc(turn_out, 1)
                    for w, bank in ((wk_t, 4), (wv_t, 5)):
                        dve.tensor_copy(w[:, :, :].rearrange("p m c -> p (m c)"), ps[:, bank, :]).then_inc(turn_out, 1)
                    dve.wait_ge(made, 6)
                    dve.tensor_copy(spread[:, :, :], spread_f[:, :, :])
                    dve.tensor_copy(block_q[:, :], block_f[:, 0, :])
                    dve.tensor_copy(block_k[:, :], block_f[:, 1, :])
                    dve.tensor_copy(ident_b[:, :], ident[:, :])
                    for slot in range(2):
                        dve.memset(val_hi[:, slot, :, LATENT:P], 1.0)
                        dve.memset(val_lo[:, slot, :, LATENT:P], 0.0)
                    dve.memset(inv_hl[:, :], 0.0)
                    dve.memset(q_lo[LATENT:P, :, :], 0.0)
                    dve.memset(key_top[LATENT:P, :, :], 0.0).then_inc(zeroed, 1)
                    dve.wait_ge(zeroed, 1)
                    dve.memset(key_top[LATENT:LATENT + 1, :, :], M_SCALE)
                    wide = [P, KD, 2, LATENT]
                    src = down[:, :, :].unsqueeze(2).to_broadcast(wide)
                    dve.tensor_scalar(down_hi[:, :, :, :], src, WS, None, ALU.mult).then_inc(const_done, 1)
                    dve.wait_ge(const_done, 1)
                    for k in range(KD):
                        dve.scalar_tensor_tensor(down_lo[:, k, :, :], down[:, k, :].unsqueeze(1).to_broadcast([P, 2, LATENT]),
                                                 WS, down_hi[:, k, :, :], ALU.mult, ALU.subtract)
                    for m in range(MLA_PAIRS):
                        dve.wait_ge(folded, m + 1)
                        for i in range(2):
                            bank, rows = 4 * i + m % 4, slice(i * LATENT, (i + 1) * LATENT)
                            dve.tensor_scalar(b_hi[rows, m, :], ps[rows, bank, D:2 * D], WS, None, ALU.mult)
                            for k in range(KD):
                                src = ps[:, bank, k * LATENT:(k + 1) * LATENT].unsqueeze(1).to_broadcast([P, 2, LATENT])
                                last = dve.tensor_scalar(a_hi[:, k, 2 * m + i, :, :], src, WS, None, ALU.mult)
                        last.then_inc(split, 1)
                        dve.wait_ge(split, 2 * m + 1)
                        for i in range(2):
                            bank, rows = 4 * i + m % 4, slice(i * LATENT, (i + 1) * LATENT)
                            dve.scalar_tensor_tensor(b_lo[rows, m, :], ps[rows, bank, D:2 * D], WS, b_hi[rows, m, :],
                                                     ALU.mult, ALU.subtract)
                            for k in range(KD):
                                src = ps[:, bank, k * LATENT:(k + 1) * LATENT].unsqueeze(1).to_broadcast([P, 2, LATENT])
                                last = dve.scalar_tensor_tensor(a_lo[:, k, 2 * m + i, :, :], src, WS,
                                                                a_hi[:, k, 2 * m + i, :, :], ALU.mult, ALU.subtract)
                        last.then_inc(split, 1)

        y = sb("y", [P, TILES, D])
        y_hi = sb("y_hi", [P, 2, KD, SEQ], F16)
        y_lo = sb("y_lo", [P, 2, KD, SEQ], F16)
        stats = sb("stats", [P, TILES, 6])
        ln_col = sb("ln_col", [P, 4, TILES])
        var = sb("var", [P, TILES])
        rstd = sb("rstd", [P, TILES])
        newton = sb("newton", [P, TILES])
        lat = sb("lat", [P, SEQ])
        key_hl = sb("key_hl", [P, 2, SEQ], F16)
        q_hi = sb("q_hi", [P, RING, SEQ], F16)
        m_col = sb("m_col", [P, 2, TILES, GROUP_HEADS])
        m_neg = sb("m_neg", [GROUP_HEADS, 2, SEQ], F16)
        p_full = sb("p_full", [P, 2, KEY_COLS])
        p_hi = sb("p_hi", [P, 2, KEY_COLS], F16)
        p_lo = sb("p_lo", [P, 2, KEY_COLS], F16)
        o = sb("o", [P, 2, MLA_PAIRS, SEQ])
        o_hi = sb("o_hi", [P, MLA_PAIRS, SEQ], F16)
        o_lo = sb("o_lo", [P, MLA_PAIRS, SEQ], F16)
        sum_row = sb("sum_row", [1, SUM_SLOTS, SEQ])
        sums = sb("sums", [MLA_HEADS, 2, SEQ])
        inv = sb("inv", [MLA_HEADS, SEQ])

        norm_step = sem("norm_step")
        y_turned = sem("y_turned")
        y_split = sem("y_split")
        lat_done = sem("lat_done")
        lat_step = sem("lat_step")
        lat_turned = sem("lat_turned")
        val_out = sem("val_out")
        q_done = sem("q_done")
        q_head = sem("q_head")
        q_tail = sem("q_tail")
        s_done = sem("s_done")
        s_max = sem("s_max")
        m_turned = sem("m_turned")
        m_out = sem("m_out")
        m_put = [sem(f"m_put{i}") for i in range(2)]
        st_done = sem("st_done")
        exp_done = sem("exp_done")
        p_tail = sem("p_tail")
        pv_done = sem("pv_done")
        pv_out = sem("pv_out")
        sum_put = [sem(f"sum_put{i}") for i in range(SUM_SLOTS)]
        inv_step = sem("inv_step")
        spread_done = sem("spread_done")
        scaled = sem("scaled")
        o_head = sem("o_head")
        o_tail = sem("o_tail")
        out_done = sem("out_done")
        x_added = sem("x_added")

        H = MLA_HEADS
        NORM_AT, TURN_AT, LATENT_AT, VALUE_AT = 0, 3, 5, 6
        INVERT_AT, SPREAD_AT, OUTPUT_AT = 1, 3, H - TILES

        def exists(b):
            return not isinstance(b, int) or 0 <= b < BATCH

        def head_of(b, h):
            return (b + h // H, h % H, b * H + h)

        def group_of(b, h):
            if (h + LEAD - 2) % GROUP_HEADS != GROUP_HEADS - 1:
                return None
            last_b, last_h, _ = head_of(b, h + LEAD - 2)
            return (last_b, last_h // GROUP_HEADS) if exists(last_b) else None

        GROUPS = H // GROUP_HEADS

        def stream(engine, step):
            for b in (-1, 0):
                for h in range(H):
                    step(engine, b, b % 2, h)
            with engine.Fori(0, (BATCH - 2) // 2) as two:
                for i in range(2):
                    for h in range(H):
                        step(engine, 2 * two + (1 + i), (1 + i) % 2, h)
            for b in (BATCH - 1, BATCH):
                for h in range(H):
                    step(engine, b, b % 2, h)

        flat = ps[:, :, :].rearrange("p a n -> p (a n)")

        def tensor_step(pe, b, slot, h):
            before, after, n = b - 1, b + 1, b * H + h

            if exists(before) and SPREAD_AT <= h < SPREAD_AT + MLA_PAIRS:
                m = h - SPREAD_AT
                if exists(b):
                    pe.wait_ge(pv_out, 2 * n)
                pe.wait_ge(inv_step, 3 * b)
                if m > 0:
                    pe.wait_ge(scaled, MLA_PAIRS * before + m)
                pe.matmul(ps[:, 7, :], spread[:, 2 * m:2 * m + 2, :].rearrange("p a c -> p (a c)"), inv_hl[:, :],
                          start=True, stop=True).then_inc(spread_done, 1)
            if exists(before) and h >= OUTPUT_AT:
                t = h - OUTPUT_AT
                if exists(b):
                    pe.wait_ge(pv_out, 2 * n)
                pe.wait_ge(o_tail, MLA_PAIRS * b)
                if t > 0:
                    pe.wait_ge(x_added, TILES * before + t)
                toks = slice(t * P, (t + 1) * P)
                for m in range(MLA_PAIRS):
                    pe.matmul(ps[:, 7, 0:D], o_hi[:, m, toks], b_hi[:, m, :], start=(m == 0), stop=False)
                    pe.matmul(ps[:, 7, 0:D], o_hi[:, m, toks], b_lo[:, m, :], start=False, stop=False)
                    last = pe.matmul(ps[:, 7, 0:D], o_lo[:, m, toks], b_hi[:, m, :], start=False,
                                     stop=(m == MLA_PAIRS - 1))
                last.then_inc(out_done, 1)

            hb, hh, hn = head_of(b, h + 1)
            if exists(hb):
                if not isinstance(hn, int) or hn > 0:
                    pe.wait_ge(exp_done, 2 * hn)
                if hh % GROUP_HEADS == 0:
                    g = hh // GROUP_HEADS
                    pe.wait_ge(q_tail, hn + GROUP_HEADS)
                    pe.wait_ge(m_put[g % 2], 16 * (hb * (GROUPS // 2) + g // 2 + 1))
                for t in range(TILES):
                    at = 3 * 512 + KEY_AT[t]
                    cols, toks = SEQ - t * P, slice(t * P, (t + 1) * P)
                    pe.matmul(flat[:, at:at + cols], key_hl[:, (slot + (h + 1) // H) % 2, toks],
                              q_hi[:, hh % RING, t * P:], start=True, stop=False)
                    pe.matmul(flat[:, at:at + cols], key_top[:, (slot + (h + 1) // H) % 2, toks],
                              q_lo[:, hh % RING, t * P:], start=False, stop=False)
                    last = pe.matmul(flat[:, at:at + P], ident_b[:, :], block_k[:, :], start=False, stop=True)
                last.then_inc(st_done, 1)

            if exists(after) and TURN_AT <= h <= VALUE_AT and exists(b):
                pe.wait_ge(q_tail, n + LEAD)
            if exists(after) and TURN_AT <= h < TURN_AT + KD:
                k = h - TURN_AT
                if k == 0:
                    pe.wait_ge(norm_step, LN_STEPS * (after + 1))
                else:
                    pe.wait_ge(y_split, 2 * KD * after + 2 * k)
                for t in range(TILES):
                    last = pe.transpose(ps[:, 6, t * P:(t + 1) * P], y[:, t, k * P:(k + 1) * P], ident[:, :])
                last.then_inc(y_turned, 1)
            if exists(after) and h == LATENT_AT:
                pe.wait_ge(y_split, 2 * KD * (after + 1))
                for k in range(KD):
                    last = split_matmul(pe, ps[:, 6, :], down_hi[:, k, :, :].rearrange("p a c -> p (a c)"),
                                        down_lo[:, k, :, :].rearrange("p a c -> p (a c)"),
                                        y_hi[:, 1 - slot, k, :], y_lo[:, 1 - slot, k, :], k == 0, k == KD - 1)
                last.then_inc(lat_done, 1)
            if exists(after) and h == VALUE_AT:
                pe.wait_ge(lat_step, 4 * after + 1)
                for t in range(TILES):
                    last = pe.transpose(ps[:, 6, t * P:(t + 1) * P], lat[:, t * P:(t + 1) * P], ident[:, :])
                last.then_inc(lat_turned, 1)

            if exists(b):
                pe.wait_ge(p_tail, n + 1)
                if h == 0:
                    pe.wait_ge(val_out, 2 * (b + 1))
                if not isinstance(n, int) or n > 0:
                    pe.wait_ge(pv_out, 2 * n)
                if exists(before) and SPREAD_AT <= h < SPREAD_AT + MLA_PAIRS:
                    pe.wait_ge(scaled, MLA_PAIRS * before + h - SPREAD_AT + 1)
                if exists(before) and h >= OUTPUT_AT:
                    pe.wait_ge(x_added, TILES * before + h - OUTPUT_AT + 1)
                for t in range(TILES):
                    out = ps[:, 7, t * P:]
                    cols = slice(KEY_AT[t], KEY_AT[t] + SEQ - t * P)
                    hi, lo = p_hi[:, h % 2, cols], p_lo[:, h % 2, cols]
                    pe.matmul(out, val_hi[:, slot, t, :], hi, start=(t == 0), stop=False)
                    pe.matmul(out, val_hi[:, slot, t, :], lo, start=False, stop=False)
                    last = pe.matmul(out, val_lo[:, slot, t, :], hi, start=False, stop=(t == TILES - 1))
                last.then_inc(pv_done, 1)

            group = group_of(b, h)
            if group is not None:
                gb, g = group
                pe.wait_ge(s_max, TILES * (gb * H + (g + 1) * GROUP_HEADS))
                for t in range(TILES):
                    last = pe.transpose(ps[0:GROUP_HEADS, 0, t * P:(t + 1) * P], m_col[:, g % 2, t, :], ident[:, :])
                last.then_inc(m_turned, 1)

            hb, hh, hn = head_of(b, h + LEAD)
            qslot = (slot + (h + LEAD) // H) % 2
            if exists(hb):
                if not isinstance(hn, int) or hn > 0:
                    pe.wait_ge(q_tail, hn)
                if hh == 0:
                    pe.wait_ge(val_out, 2 * (hb + 1))
                for k in range(KD):
                    if exists(after) and k == 0 and h == TURN_AT:
                        pe.wait_ge(y_split, 2 * KD * after + 2)
                    if exists(after) and k == 0 and h == TURN_AT + 1:
                        pe.wait_ge(y_split, 2 * KD * after + 4)
                    if exists(after) and k == 0 and h == LATENT_AT:
                        pe.wait_ge(lat_step, 4 * after + 1)
                    if exists(after) and k == 0 and h == VALUE_AT:
                        pe.wait_ge(val_out, 2 * (after + 1))
                    last = split_matmul(pe, ps[:, 6, :], a_hi[:, k, hh, :, :].rearrange("p a c -> p (a c)"),
                                        a_lo[:, k, hh, :, :].rearrange("p a c -> p (a c)"),
                                        y_hi[:, qslot, k, :], y_lo[:, qslot, k, :], k == 0, k == KD - 1)
                last.then_inc(q_done, 1)

            hb, hh, hn = head_of(b, h + LEAD - 1)
            if exists(hb):
                pe.wait_ge(q_head, hn + 1)
                if not isinstance(hn, int) or hn > 0:
                    pe.wait_ge(s_max, TILES * hn)
                if hh == 0:
                    pe.wait_ge(lat_step, 4 * (hb + 1))
                for t in range(TILES):
                    out = flat[:, QUERY_AT[t]:QUERY_AT[t] + (t + 1) * P]
                    if t == TILES - 1 and group is not None:
                        pe.wait_ge(m_out, gb * GROUPS + g + 1)
                    pe.matmul(out, q_hi[:, hh % RING, t * P:(t + 1) * P],
                              key_hl[:, (slot + (h + LEAD - 1) // H) % 2, 0:(t + 1) * P], start=True, stop=False)
                    last = pe.matmul(out[:, t * P:(t + 1) * P], ident_b[:, :], block_q[:, :],
                                     start=False, stop=True)
                last.then_inc(s_done, 1)

        def vector_step(dve, b, slot, h):
            before, after, n = b - 1, b + 1, b * H + h

            if exists(before) and SPREAD_AT <= h < SPREAD_AT + MLA_PAIRS:
                m = h - SPREAD_AT
                dve.wait_ge(spread_done, MLA_PAIRS * before + m + 1)
                dve.tensor_tensor(o[:, 1 - slot, m, :], o[:, 1 - slot, m, :], ps[:, 7, :], ALU.mult).then_inc(scaled, 1)
            if exists(before) and h >= OUTPUT_AT:
                t = h - OUTPUT_AT
                dve.wait_ge(out_done, TILES * before + t + 1)
                xt = x[:, before, t, :]
                dve.scalar_tensor_tensor(xt, ps[:, 7, 0:D], 1.0 / WS, xt, ALU.mult, ALU.add).then_inc(x_added, 1)

            hb, hh, hn = head_of(b, h + LEAD - 2)
            if exists(hb):
                dve.wait_ge(s_done, hn + 1)
                for t in range(TILES):
                    j, g = hh % GROUP_HEADS, hh // GROUP_HEADS
                    dve.tensor_reduce(m_col[:, g % 2, t, j:j + 1], flat[:, QUERY_AT[t]:QUERY_AT[t] + (t + 1) * P],
                                      AX.X, ALU.max).then_inc(s_max, 1)

            if exists(after) and TURN_AT <= h < TURN_AT + KD:
                k = h - TURN_AT
                at = 2 * (KD * after + k)
                dve.wait_ge(y_turned, KD * after + k + 1)
                dve.tensor_copy(y_hi[:, 1 - slot, k, :], ps[:, 6, :]).then_inc(y_split, 1)
                dve.wait_ge(y_split, at + 1)
                dve.tensor_tensor(y_lo[:, 1 - slot, k, :], ps[:, 6, :], y_hi[:, 1 - slot, k, :],
                                  ALU.subtract).then_inc(y_split, 1)
            if exists(after) and h == LATENT_AT:
                dve.wait_ge(lat_done, after + 1)
                dve.tensor_scalar(lat[:, :], ps[:, 6, :], 1.0 / WS, None, ALU.mult).then_inc(lat_step, 1)
                dve.wait_ge(lat_step, 4 * after + 1)
                dve.tensor_copy(key_hl[:, 1 - slot, :], lat[:, :]).then_inc(lat_step, 1)
                dve.tensor_copy(key_top[0:LATENT, 1 - slot, :], lat[0:LATENT, :]).then_inc(lat_step, 1)
                dve.wait_ge(lat_step, 4 * after + 2)
                tails = slice(LATENT, P)
                dve.tensor_tensor(key_hl[tails, 1 - slot, :], lat[tails, :], key_hl[tails, 1 - slot, :],
                                  ALU.subtract).then_inc(lat_step, 1)
            if exists(after) and h == VALUE_AT:
                dve.wait_ge(lat_turned, after + 1)
                src = ps[:, 6, :].rearrange("p (t c) -> p t c", t=TILES)[:, :, 0:LATENT]
                dve.tensor_copy(val_hi[:, 1 - slot, :, 0:LATENT], src).then_inc(val_out, 1)
                dve.wait_ge(val_out, 2 * after + 1)
                dve.tensor_tensor(val_lo[:, 1 - slot, :, 0:LATENT], src, val_hi[:, 1 - slot, :, 0:LATENT],
                                  ALU.subtract).then_inc(val_out, 1)

            hb, hh, hn = head_of(b, h + 1)
            if exists(hb):
                dve.wait_ge(exp_done, 2 * (hn + 1))
                dve.tensor_tensor(p_lo[:, hh % 2, :], p_full[:, hh % 2, :], p_hi[:, hh % 2, :],
                                  ALU.subtract).then_inc(p_tail, 1)

            hb, hh, hn = head_of(b, h + LEAD)
            if exists(hb):
                dve.wait_ge(q_head, hn + 1)
                rows = slice(0, LATENT)
                dve.scalar_tensor_tensor(q_lo[rows, hh % RING, :], ps[rows, 6, :], 1.0 / WS, q_hi[rows, hh % RING, :],
                                         ALU.mult, ALU.subtract).then_inc(q_tail, 1)

            if exists(before) and h == INVERT_AT:
                for i in range(SUM_SLOTS):
                    dve.wait_ge(sum_put[i], 16 * (H // SUM_SLOTS) * b)
                dve.reciprocal(inv[:, :], sums[:, 1 - slot, :]).then_inc(inv_step, 1)
                dve.wait_ge(inv_step, 3 * before + 1)
                dve.tensor_scalar(inv_hl[0:H, :], inv[:, :], INV_SCALE, None, ALU.mult).then_inc(inv_step, 1)
                dve.wait_ge(inv_step, 3 * before + 2)
                dve.scalar_tensor_tensor(inv_hl[32:32 + H, :], inv[:, :], INV_SCALE, inv_hl[0:H, :],
                                         ALU.mult, ALU.subtract).then_inc(inv_step, 1)
            if exists(before) and SPREAD_AT <= h < SPREAD_AT + MLA_PAIRS:
                m = h - SPREAD_AT
                dve.wait_ge(o_head, MLA_PAIRS * before + m + 1)
                dve.tensor_tensor(o_lo[:, m, :], o[:, 1 - slot, m, :], o_hi[:, m, :], ALU.subtract).then_inc(o_tail, 1)
            if exists(after) and h == NORM_AT:
                layernorm_stats(dve, norm_step, x[:, after, :, :], stats)
            if exists(after) and h == NORM_AT + 1:
                layernorm_columns(dve, norm_step, LN_STEPS * after + TILES, stats, ln_col, var[:, :], rstd[:, :], newton[:, :])
            if exists(after) and h == NORM_AT + 2:
                layernorm_apply(dve, norm_step, LN_STEPS * after + TILES + LN_COLUMN_STEPS, x[:, after, :, :], y,
                                ln_col, rstd[:, :])

        def scalar_step(act, b, slot, h):
            before, n = b - 1, b * H + h
            hb, hh, hn = head_of(b, h + 1)
            if exists(hb):
                act.wait_ge(st_done, hn + 1)
                for out in (p_full, p_hi):
                    act.activation(out[:, hh % 2, :], flat[:, 3 * 512:3 * 512 + KEY_COLS], ACT.Exp,
                                   scale=float(MLA_DIM) ** -0.5).then_inc(exp_done, 1)
            if exists(before) and SPREAD_AT <= h < SPREAD_AT + MLA_PAIRS:
                m = h - SPREAD_AT
                act.wait_ge(scaled, MLA_PAIRS * before + m + 1)
                act.activation(o_hi[:, m, :], o[:, 1 - slot, m, :], ACT.Copy).then_inc(o_head, 1)
            group = group_of(b, h)
            if group is not None:
                gb, g = group
                act.wait_ge(m_turned, gb * GROUPS + g + 1)
                act.activation(m_neg[:, g % 2, :], ps[0:GROUP_HEADS, 0, :], ACT.Copy,
                               scale=-1.0 / M_SCALE).then_inc(m_out, 1)
            if exists(b):
                i = h % SUM_SLOTS
                if not isinstance(b, int) or b > 0 or h >= SUM_SLOTS:
                    act.wait_ge(sum_put[i], 16 * (b * (H // SUM_SLOTS) + h // SUM_SLOTS))
                act.wait_ge(pv_done, n + 1)
                rows = slice((h % 2) * LATENT, (h % 2 + 1) * LATENT)
                act.activation(sum_row[:, i, :], ps[LATENT:LATENT + 1, 7, :], ACT.Copy).then_inc(pv_out, 1)
                act.activation(o[rows, slot, h // 2, :], ps[0:LATENT, 7, :], ACT.Copy).then_inc(pv_out, 1)
            hb, hh, hn = head_of(b, h + LEAD)
            if exists(hb):
                act.wait_ge(q_done, hn + 1)
                act.activation(q_hi[:, hh % RING, :], ps[:, 6, :], ACT.Copy, scale=1.0 / WS).then_inc(q_head, 1)

        def dma_step(sp, b, slot, h):
            group = group_of(b, h)
            if group is not None:
                gb, g = group
                at = (g * GROUP_HEADS) % RING
                sp.wait_ge(m_out, gb * GROUPS + g + 1)
                sp.dma_start(q_lo[LATENT:LATENT + 1, at:at + GROUP_HEADS, :], m_neg[:, g % 2, :]).then_inc(m_put[g % 2], 16)
            if exists(b):
                i = h % SUM_SLOTS
                sp.wait_ge(pv_out, 2 * (b * H + h) + 2)
                sp.dma_start(sums[h:h + 1, slot, :], sum_row[:, i, :]).then_inc(sum_put[i], 16)

        with nc.Block() as block:
            @block.tensor
            def _(pe):
                stream(pe, tensor_step)

            @block.vector
            def _(dve):
                stream(dve, vector_step)

            @block.scalar
            def _(act):
                stream(act, scalar_step)

            @block.sync
            def _(sp):
                stream(sp, dma_step)


class Kept:

    def __init__(self, stack):
        self.stack, self.semaphores = stack, []

    def enter_context(self, semaphore):
        self.semaphores.append(self.stack.enter_context(semaphore))
        return self.semaphores[-1]


def macaron_kernel(nc, io, out):
    with ExitStack() as ctx:
        x = ctx.enter_context(nc.sbuf_tensor("x", [P, BATCH, TILES, D], F32))
        ident = ctx.enter_context(nc.sbuf_tensor("ident", [P, P], F32))
        x_in = ctx.enter_context(nc.semaphore("x_in"))
        x_out = ctx.enter_context(nc.semaphore("x_out"))
        ident_set = ctx.enter_context(nc.semaphore("ident_set"))

        with nc.Block() as block:
            @block.sync
            def _(sp):
                for b in range(BATCH):
                    sp.dma_start(x[:, b], io["x"][b].rearrange("(t p) d -> p t d", p=P)).then_inc(x_in, 16)
                sp.wait_ge(x_in, 16 * BATCH)

            @block.gpsimd
            def _(pool):
                pool.memset(ident[:, :], 0.0).then_inc(ident_set, 1)
                pool.wait_ge(ident_set, 1)
                pool.affine_select(out=ident[:, :], in_=ident[:, :], compare_op=ALU.not_equal, fill=1.0,
                                   base=0, pattern=[[-1, P]], channel_multiplier=1).then_inc(ident_set, 1)

        experts = {n: io["L0_attn_" + n] for n in ("Wq", "bq", "Wk", "bk", "Wv", "bv")}
        experts |= {n: io["L0_ffn_" + n] for n in ("gate_w", "gate_b", "rms_w", "w1", "b1", "w2", "b2")}
        experts["rope_tab"] = io["rope_tab"]
        routed = {n: io["L1_ffn_" + n] for n in ("attention_mask", "position_ids", "router_w", "router_b", "wq", "wk",
                                                 "wv", "wo", "w1", "w2", "ln1", "ln2")}
        routed["inv_freq"] = io["inv_freq"]
        latent = {n: io["L1_attn_" + n] for n in ("Wq", "Wkv_down", "Wk_up", "Wv_up", "Wout")}

        def layer(build, *args):
            with ExitStack() as kept:
                held = Kept(kept)
                build(nc, held, *args)
                with nc.Block() as block:
                    @block.sync
                    def _(sp):
                        for semaphore in held.semaphores:
                            sp.sem_clear(semaphore)

        layer(expert_and_head_layers, x, ident, experts)
        layer(routed_layer, "routed1", x, ident, routed)
        layer(latent_attention_layer, x, ident, latent)
        layer(routed_layer, "routed2", x, ident, routed)

        with nc.Block() as block:
            @block.sync
            def _(sp):
                for b in range(BATCH):
                    sp.dma_start(out[b].rearrange("(t p) d -> p t d", p=P), x[:, b]).then_inc(x_out, 16)
                sp.wait_ge(x_out, 16 * BATCH)


def kernel(**inputs):
    import numpy as _np
    import concourse.bacc as _bacc
    from concourse import mybir as _mybir
    from concourse.bass_utils import run_bass_kernel_spmd as _run

    even = _np.arange(0, HEAD_DIM, 2, dtype=_np.float32)
    freqs = (_np.float32(10000.0) ** (-(even / _np.float32(D)))).astype(_np.float32)
    angles = _np.arange(SEQ, dtype=_np.float32)[:, None] * freqs[None, :]
    tables = {
        "rope_tab": _np.stack([_np.cos(angles.astype(_np.float64)), _np.sin(angles.astype(_np.float64))],
                              axis=1).astype(_np.float32),
        "inv_freq": (_np.float32(1.0) / _np.float32(10000.0) ** (even / _np.float32(HEAD_DIM))).astype(_np.float32),
    }
    nc = _bacc.Bacc("TRN2", target_bir_lowering=False, num_devices=1)
    arrays, io = {}, {}
    for name, value in {**inputs, **tables}.items():
        a = _np.ascontiguousarray(value)
        arrays[f"in_{name}_dram"] = a
        key = "x" if name == "L0_attn_x" else name
        io[key] = nc.dram_tensor(f"in_{name}_dram", a.shape, _mybir.dt.from_np(a.dtype), kind="ExternalInput").ap()
    out = nc.dram_tensor("out_0_dram", (BATCH, SEQ, D), F32, kind="ExternalOutput").ap()
    macaron_kernel(nc, io, out)
    r = _run(nc, [arrays], core_ids=[0])
    return r.results[0]["out_0_dram"]
```

```python
from contextlib import ExitStack

import numpy as np

import concourse.bass as bass
from concourse import mybir

F32 = mybir.dt.float32
F16 = mybir.dt.float16
I32 = mybir.dt.int32
U32 = mybir.dt.uint32
ALU = mybir.AluOpType
ACT = mybir.ActivationFunctionType
AX = mybir.AxisListType

P = 128
BATCH, SEQ, D = 8, 512, 256
TILES = SEQ // P
KD = D // P
EXPERTS, EXPERT_HID = 8, 512
HID_TILES = EXPERTS * EXPERT_HID // P
HEADS, HEAD_DIM = 16, 16
QKV = 3 * D
LN_EPS = 1e-5
F32_EPS = float(np.finfo(np.float32).eps)

WS = 16.0

RSQRT_STEPS = 11
LN_COLUMN_STEPS = 7 + RSQRT_STEPS
HEAD_STEPS = 102
NORM_CONSTANTS = (0.5, 0.25, 1.0 / D, LN_EPS, -0.5, 1.5)
VARIANCE_STEPS, NEWTON_STEPS = 10, 12
NORM_STEPS = TILES + VARIANCE_STEPS + 2 + NEWTON_STEPS + TILES
GATE_STEPS = 8 + NEWTON_STEPS + 8
STAGES = 2 * BATCH


def rsqrt_start(dve, step, at, v, y):
    yi = y.bitcast(I32)
    dve.wait_ge(step, at)
    dve.tensor_scalar(yi, v.bitcast(I32), 1, None, ALU.logical_shift_right).then_inc(step, 1)
    dve.wait_ge(step, at + 1)
    dve.tensor_scalar(yi, yi, -1.0, float(0x5F3759DF), ALU.mult, ALU.add).then_inc(step, 1)


def rsqrt_step(dve, step, at, v, y, t):
    dve.wait_ge(step, at)
    dve.tensor_tensor(t, y, y, ALU.mult).then_inc(step, 1)
    dve.wait_ge(step, at + 1)
    dve.scalar_tensor_tensor(t, t, -0.5, v, ALU.mult, ALU.mult).then_inc(step, 1)
    dve.wait_ge(step, at + 2)
    dve.scalar_tensor_tensor(y, t, 1.5, y, ALU.add, ALU.mult).then_inc(step, 1)


def rsqrt_newton(dve, step, at, v, y, t):
    rsqrt_start(dve, step, at, v, y)
    for n in range(3):
        rsqrt_step(dve, step, at + 2 + 3 * n, v, y, t)


def layernorm_stats(dve, step, x4, stats):
    for t in range(TILES):
        dve.bn_stats(stats[:, t, :], x4[:, t, :]).then_inc(step, 1)


def layernorm_variance(dve, step, at, stats, col, var):
    twice_mean, gap, squares, mean = (col[:, i, :] for i in range(4))
    dve.wait_ge(step, at)
    dve.tensor_tensor(twice_mean, stats[:, :, 1], stats[:, :, 4], ALU.add).then_inc(step, 1)
    dve.tensor_tensor(gap, stats[:, :, 1], stats[:, :, 4], ALU.subtract).then_inc(step, 1)
    dve.tensor_tensor(squares, stats[:, :, 2], stats[:, :, 5], ALU.add).then_inc(step, 1)
    dve.wait_ge(step, at + 3)
    dve.tensor_scalar(mean, twice_mean, 0.5, None, ALU.mult).then_inc(step, 1)
    dve.tensor_tensor(gap, gap, gap, ALU.mult).then_inc(step, 1)
    dve.tensor_scalar(squares, squares, 1.0 / D, LN_EPS, ALU.mult, ALU.add).then_inc(step, 1)
    dve.wait_ge(step, at + 6)
    dve.scalar_tensor_tensor(var, gap, 0.25, squares, ALU.mult, ALU.add).then_inc(step, 1)


def layernorm_columns(dve, step, at, stats, col, var, rstd, tmp):
    layernorm_variance(dve, step, at, stats, col, var)
    rsqrt_newton(dve, step, at + 7, var, rstd, tmp)


def layernorm_apply(dve, step, at, x4, y4, col, rstd):
    mean = col[:, 3, :]
    dve.wait_ge(step, at)
    for t in range(TILES):
        dve.tensor_scalar(y4[:, t, :], x4[:, t, :], mean[:, t:t + 1], rstd[:, t:t + 1],
                          ALU.subtract, ALU.mult).then_inc(step, 1)


def pool_variance(pool, step, at, stats, col, const, var, minus_half):
    twice_mean, gap, squares, mean = (col[:, i, :] for i in range(4))
    half, quarter, per_element, eps, minus, _ = (const[:, i, :] for i in range(6))
    pool.wait_ge(step, at)
    pool.tensor_tensor(twice_mean, stats[:, :, 1], stats[:, :, 4], ALU.add).then_inc(step, 1)
    pool.tensor_tensor(gap, stats[:, :, 1], stats[:, :, 4], ALU.subtract).then_inc(step, 1)
    pool.tensor_tensor(squares, stats[:, :, 2], stats[:, :, 5], ALU.add).then_inc(step, 1)
    pool.wait_ge(step, at + 3)
    pool.tensor_tensor(mean, twice_mean, half, ALU.mult).then_inc(step, 1)
    pool.tensor_tensor(gap, gap, gap, ALU.mult).then_inc(step, 1)
    pool.tensor_tensor(squares, squares, per_element, ALU.mult).then_inc(step, 1)
    pool.wait_ge(step, at + 6)
    pool.tensor_tensor(gap, gap, quarter, ALU.mult).then_inc(step, 1)
    pool.tensor_tensor(squares, squares, eps, ALU.add).then_inc(step, 1)
    pool.wait_ge(step, at + 8)
    pool.tensor_tensor(var, gap, squares, ALU.add).then_inc(step, 1)
    pool.wait_ge(step, at + 9)
    pool.tensor_tensor(minus_half, var, minus, ALU.mult).then_inc(step, 1)


def pool_newton(pool, step, at, const, minus_half, y, t):
    for n in range(3):
        pool.wait_ge(step, at + 4 * n)
        pool.tensor_tensor(t, y, y, ALU.mult).then_inc(step, 1)
        pool.wait_ge(step, at + 4 * n + 1)
        pool.tensor_tensor(t, t, minus_half, ALU.mult).then_inc(step, 1)
        pool.wait_ge(step, at + 4 * n + 2)
        pool.tensor_tensor(t, t, const[:, 5, :], ALU.add).then_inc(step, 1)
        pool.wait_ge(step, at + 4 * n + 3)
        pool.tensor_tensor(y, y, t, ALU.mult).then_inc(step, 1)


def transpose_tiles(pe, y4, out2, ident):
    for k in range(KD):
        for t in range(TILES):
            last = pe.transpose(out2[:, k, t * P:(t + 1) * P], y4[:, t, k * P:(k + 1) * P], ident)
    return last


def split_matmul(pe, out, w_hi, w_lo, v_hi, v_lo, first, final):
    pe.matmul(out, w_hi, v_hi, start=first, stop=False)
    pe.matmul(out, w_hi, v_lo, start=False, stop=False)
    return pe.matmul(out, w_lo, v_hi, start=False, stop=final)


def expert_and_head_layers(nc, keep, x, ident, io):
    with ExitStack() as ctx:
        def sb(name, shape, dt=F32):
            return ctx.enter_context(nc.sbuf_tensor(name, shape, dt))

        def sem(name):
            return keep.enter_context(nc.semaphore(name))

        w1_hi = sb("w1_hi", [P, KD, HID_TILES * P], F16)
        w1_lo = sb("w1_lo", [P, KD, HID_TILES * P], F16)
        w2_hi = sb("w2_hi", [P, HID_TILES, D], F16)
        w2_lo = sb("w2_lo", [P, HID_TILES, D], F16)
        wqkv_hi = sb("wqkv_hi", [P, KD, QKV], F16)
        wqkv_lo = sb("wqkv_lo", [P, KD, QKV], F16)
        gate_hi = sb("gate_hi", [P, KD, EXPERTS], F16)
        gate_lo = sb("gate_lo", [P, KD, EXPERTS], F16)
        gate_bias = sb("gate_bias", [EXPERTS, 1])
        rms_w = sb("rms_w", [P, EXPERTS])
        b1_col = sb("b1_col", [P, HID_TILES])
        b2_sum = sb("b2_sum", [P, KD])
        qkv_bias = sb("qkv_bias", [P, QKV])
        rope = sb("rope", [P, TILES, 2, HEAD_DIM // 2])

        SLOTS = 4
        stage = sb("stage", [P, SLOTS, KD * EXPERT_HID])
        slot_in = [sem(f"slot_in{i}") for i in range(SLOTS)]
        chunk_head = sem("chunk_head")
        chunk_tail = sem("chunk_tail")
        x_first = sem("x_first")
        x_rest = sem("x_rest")
        chunks = []
        for e in range(EXPERTS):
            cols = slice(e * EXPERT_HID, (e + 1) * EXPERT_HID)
            chunks.append((io["w1"][e].rearrange("(k p) h -> p k h", p=P), (KD, EXPERT_HID),
                           w1_hi[:, :, cols], w1_lo[:, :, cols]))
            rows = slice(e * EXPERT_HID // P, (e + 1) * EXPERT_HID // P)
            chunks.append((io["w2"][e].rearrange("(j p) d -> p j d", p=P), (EXPERT_HID // P, D),
                           w2_hi[:, rows, :], w2_lo[:, rows, :]))
        for w, lo, hi in ((io["Wq"], 0, D), (io["Wk"], D, 2 * D), (io["Wv"], 2 * D, QKV)):
            chunks.append((w.rearrange("(k p) n -> p k n", p=P), (KD, D), wqkv_hi[:, :, lo:hi], wqkv_lo[:, :, lo:hi]))

        def staged(c):
            a, b = chunks[c][1]
            return stage[:, c % SLOTS, 0:a * b].rearrange("p (a b) -> p a b", a=a)

        def load_chunk(sp, c):
            if c >= SLOTS:
                sp.wait_ge(chunk_tail, c - SLOTS + 1)
            sp.dma_start(staged(c), chunks[c][0]).then_inc(slot_in[c % SLOTS], 16)

        def split_chunk_head(act, c):
            act.wait_ge(slot_in[c % SLOTS], 16 * (c // SLOTS + 1))
            act.activation(chunks[c][2], staged(c), ACT.Copy, scale=WS).then_inc(chunk_head, 1)

        def split_chunk_tail(dve, c):
            dve.wait_ge(chunk_head, c + 1)
            dve.scalar_tensor_tensor(chunks[c][3], staged(c), WS, chunks[c][2], ALU.mult,
                                     ALU.subtract).then_inc(chunk_tail, 1)

        def chunks_at(ht):
            if ht % (EXPERT_HID // P) != 0:
                return []
            e = ht // (EXPERT_HID // P) + 1
            return [2 * e, 2 * e + 1] if e < EXPERTS else list(range(2 * EXPERTS, len(chunks)))

        with ExitStack() as setup:
            def tmp(name, shape, dt=F32):
                return setup.enter_context(nc.sbuf_tensor(name, shape, dt))

            def tsem(name):
                return keep.enter_context(nc.semaphore(name))

            b1_rows = tmp("b1_rows", [HID_TILES, P])
            gate_rows = tmp("gate_rows", [EXPERTS, D])
            b2_rows = tmp("b2_rows", [EXPERTS, D])
            ones = tmp("ones", [EXPERTS, 1])
            gate_t = tmp("gate_t", [P, KD, EXPERTS])
            small = setup.enter_context(nc.psum_tensor("small", [P, 3, 512], F32))
            small_in = keep.software(nc.semaphore("small_in"))
            small_t = tsem("small_t")
            ones_set = tsem("ones_set")
            gate_step = tsem("gate_split_step")

            SMALL_LOADS = 8
            with nc.Block() as block:
                @block.sync
                def _(sp):
                    sp.dma_start(x[:, 0], io["x"][0].rearrange("(t p) d -> p t d", p=P)).then_inc(x_first, 16)
                    for c in range(SLOTS):
                        load_chunk(sp, c)

                @block.gpsimd
                def _(pool):
                    pool.memset(ones[:, :], 1.0).then_inc(ones_set, 1)
                    pool.dma_start(b1_rows[:, :], io["b1"].rearrange("e (j p) -> (e j) p", p=P)).then_inc(small_in, 16)
                    pool.dma_start(gate_rows[:, :], io["gate_w"]).then_inc(small_in, 16)
                    pool.dma_start(b2_rows[:, :], io["b2"]).then_inc(small_in, 16)
                    pool.dma_start(gate_bias[:, :], io["gate_b"].rearrange("(e o) -> e o", o=1)).then_inc(small_in, 16)
                    pool.dma_start(rms_w[:, :], io["rms_w"].partition_broadcast(P)).then_inc(small_in, 16)
                    for i, name in enumerate(("bq", "bk", "bv")):
                        pool.dma_start(qkv_bias[:, i * D:(i + 1) * D],
                                       io[name].partition_broadcast(P)).then_inc(small_in, 16)
                    pool.dma_start(rope[:, :, :, :],
                                   io["rope_tab"].rearrange("(t p) c i -> p t c i", p=P)).then_inc(small_in, 16)

                @block.vector
                def _(dve):
                    dve.wait_ge(small_t, 3)
                    dve.tensor_copy(b1_col[:, :], small[:, 0, 0:HID_TILES])
                    dve.tensor_copy(b2_sum[:, :], small[:, 1, 0:KD])
                    dve.tensor_scalar(gate_t[:, :, :], small[:, 2, 0:KD * EXPERTS].rearrange("p (k e) -> p k e", k=KD),
                                      WS, None, ALU.mult).then_inc(gate_step, 1)
                    dve.wait_ge(gate_step, 1)
                    dve.tensor_copy(gate_hi[:, :, :], gate_t[:, :, :]).then_inc(gate_step, 1)
                    dve.wait_ge(gate_step, 2)
                    dve.tensor_tensor(gate_lo[:, :, :], gate_t[:, :, :], gate_hi[:, :, :], ALU.subtract)

                @block.tensor
                def _(pe):
                    pe.wait_ge(small_in, 16 * (SMALL_LOADS + 1))
                    pe.wait_ge(ones_set, 1)
                    pe.transpose(small[:, 0, 0:HID_TILES], b1_rows[:, :],
                                 ident[0:HID_TILES, 0:HID_TILES]).then_inc(small_t, 1)
                    for k in range(KD):
                        last = pe.matmul(small[:, 1, k:k + 1], b2_rows[:, k * P:(k + 1) * P], ones[:, :],
                                         start=True, stop=True)
                    last.then_inc(small_t, 1)
                    for k in range(KD):
                        last = pe.transpose(small[:, 2, k * EXPERTS:(k + 1) * EXPERTS],
                                            gate_rows[:, k * P:(k + 1) * P], ident[0:EXPERTS, 0:EXPERTS])
                    last.then_inc(small_t, 1)

        GBUF = 4
        AHEAD = 2
        GROUP = 4
        y = sb("y", [P, TILES, D])
        y_hi = sb("y_hi", [P, 2, KD, SEQ], F16)
        y_lo = sb("y_lo", [P, 2, KD, SEQ], F16)
        z_hi = sb("z_hi", [P, KD, SEQ], F16)
        z_lo = sb("z_lo", [P, KD, SEQ], F16)
        g_full = sb("g_full", [P, GBUF, SEQ])
        g_hi = sb("g_hi", [P, GBUF, SEQ], F16)
        g_lo = sb("g_lo", [P, GBUF, SEQ], F16)
        acc_sb = sb("acc_sb", [P, KD, SEQ])
        stats = sb("stats", [P, TILES, 6])
        ln_col = sb("ln_col", [P, 4, TILES])
        var = sb("var", [P, TILES])
        rstd = sb("rstd", [P, TILES])
        newton = sb("newton", [P, TILES])
        minus_half = sb("minus_half", [P, TILES])
        norm_const = sb("norm_const", [P, len(NORM_CONSTANTS), TILES])
        logit_rows = sb("logit_rows", [EXPERTS, SEQ])
        logit = sb("logit", [P, TILES, EXPERTS])
        logit_sq = sb("logit_sq", [P, TILES, EXPERTS])
        gate_c = sb("gate_c", [P, 6, TILES])
        half_gain = sb("half_gain", [P, TILES])
        qk = sb("qk", [P, 2 * D])
        qk_rot = sb("qk_rot", [P, 2 * D])
        rot = sb("rot", [P, 4, D])
        v_rows = sb("v_rows", [P, TILES, D])
        prod = sb("prod", [P, GROUP * HEADS * HEAD_DIM])
        score = sb("score", [P, TILES * HEADS, HEADS])
        s_col = sb("s_col", [P, 3, TILES * HEADS])
        o_rows = sb("o_rows", [P, TILES, D])
        hid = ctx.enter_context(nc.psum_tensor("hid", [P, 4, SEQ], F32))
        acc = ctx.enter_context(nc.psum_tensor("acc", [P, KD, SEQ], F32))
        turn = ctx.enter_context(nc.psum_tensor("turn", [P, 2, 512], F32))
        turn_rows = turn[:, :, :].rearrange("p a (b d) -> p (a b) d", d=D)

        const_set = sem("const_set")
        norm_step = sem("norm_step")
        y_turned = sem("y_turned")
        y_split = sem("y_split")
        up_done = sem("up_done")
        gelu_done = sem("gelu_done")
        tail_done = sem("g_tail_done")
        down_done = sem("down_done")
        acc_out = sem("acc_out")
        acc_turned = sem("acc_turned")
        x_added = sem("x_added")
        logit_done = sem("logit_done")
        logit_turned = sem("logit_turned")
        gate_step = sem("gate_step")
        gate_exp = sem("gate_exp")
        z_turned = sem("z_turned")
        z_split = sem("z_split")
        qkv_done = sem("qkv_done")
        head_step = sem("head_step")
        head_exp = sem("head_exp")

        DENSE, FRONT, BACK = "dense", "front", "back"
        GROUPS = HEADS // GROUP
        TILE_PIECES = 1 + GROUPS
        SHIFT = TILES * TILE_PIECES
        PIECES = SHIFT + 2 + TILES * GROUPS + 1
        SCORE_EXP_AT = {DENSE: 17, BACK: 3}
        GATE_EXP_AT = 7
        GAIN_AT = 9
        GATE_AT = (4, 6)
        Z_AT = 2
        LN_PARTS = 4
        PREP_AT = HID_TILES - 6
        NEXT_AT = PREP_AT + LN_PARTS

        def slot_of(piece, mode):
            late = piece - SHIFT - 1
            if mode == DENSE:
                return 8 + 3 * piece // 7 if late < 0 else 18 + 7 * late // 17
            return 8 + 13 * piece // 10 if late < 0 else 36 + 21 * late // 17

        def pieces_at(ht, mode):
            slot = ht + (HID_TILES if mode == BACK else 0)
            return [i for i in range(PIECES) if slot_of(i, mode) == slot] if mode else []

        def qkv_at(ht, mode):
            slot = ht + (HID_TILES if mode == BACK else 0)
            return [t for t in range(TILES) if slot_of(t * TILE_PIECES, mode) == slot + 1] if mode else []

        def pe_stage(pe, n, odd=0, first=False, mode=None, k_batch=None, z_norm=None, prep=None):
            def up(ht):
                if ht == 0:
                    pe.wait_ge(y_split, 4 * (n + 1))
                if first and ht % (EXPERT_HID // P) == 0:
                    pe.wait_ge(chunk_tail, 2 * (ht // (EXPERT_HID // P) + 1))
                if not (first and ht < 4):
                    pe.wait_ge(gelu_done, 2 * (n * HID_TILES + ht - 3))
                cols = slice(ht * P, (ht + 1) * P)
                for k in range(KD):
                    last = split_matmul(pe, hid[:, ht % 4, :], w1_hi[:, k, cols], w1_lo[:, k, cols],
                                        y_hi[:, odd, k, :], y_lo[:, odd, k, :], k == 0, k == KD - 1)
                last.then_inc(up_done, 1)

            def down(ht):
                if ht == 0 and not first:
                    pe.wait_ge(acc_out, 2 * n)
                pe.wait_ge(tail_done, n * HID_TILES + ht + 1)
                for k in range(KD):
                    cols = slice(k * P, (k + 1) * P)
                    last = split_matmul(pe, acc[:, k, :], w2_hi[:, ht, cols], w2_lo[:, ht, cols],
                                        g_hi[:, ht % GBUF, :], g_lo[:, ht % GBUF, :],
                                        ht == 0, ht == HID_TILES - 1)
                last.then_inc(down_done, 1)

            for ht in range(AHEAD):
                up(ht)
            for ht in range(HID_TILES):
                if ht + AHEAD < HID_TILES:
                    up(ht + AHEAD)
                if ht == 3:
                    pe.wait_ge(gate_step, n * GATE_STEPS + 1)
                down(ht)
                if ht == 0 and not first:
                    turn_acc(pe, n)
                if ht == 2:
                    if not first:
                        pe.wait_ge(x_added, 4 * n)
                    for k in range(KD):
                        last = split_matmul(pe, turn[0:EXPERTS, 0, :], gate_hi[:, k, :], gate_lo[:, k, :],
                                            y_hi[:, odd, k, :], y_lo[:, odd, k, :], k == 0, k == KD - 1)
                    last.then_inc(logit_done, 1)
                if ht == 3:
                    for t in range(TILES):
                        last = pe.transpose(turn[:, 1, t * EXPERTS:(t + 1) * EXPERTS],
                                            logit_rows[:, t * P:(t + 1) * P], ident[0:EXPERTS, 0:EXPERTS])
                    last.then_inc(logit_turned, 1)
                if mode in (DENSE, FRONT) and ht == Z_AT + LN_PARTS:
                    pe.wait_ge(norm_step, NORM_STEPS * (z_norm + 1))
                    pe.wait_ge(gate_step, n * GATE_STEPS + 2)
                    transpose_tiles(pe, y, turn, ident[:, :]).then_inc(z_turned, 1)
                for t in qkv_at(ht, mode):
                    pe.wait_ge(z_split, 4 * (k_batch + 1))
                    if t > 0:
                        pe.wait_ge(head_step, HEAD_STEPS * k_batch + 16 * (t - 1) + 2)
                    for lo, hi, out in ((0, 2 * D, turn[:, 0, :]), (2 * D, QKV, turn[:, 1, 0:D])):
                        for k in range(KD):
                            for a, (zz, ww) in enumerate(((z_hi, wqkv_hi), (z_hi, wqkv_lo), (z_lo, wqkv_hi))):
                                last = pe.matmul(out, zz[:, k, t * P:(t + 1) * P], ww[:, k, lo:hi],
                                                 start=(k == 0 and a == 0), stop=(k == KD - 1 and a == 2))
                    last.then_inc(qkv_done, 1)
                if ht == NEXT_AT and prep is not None:
                    pe.wait_ge(norm_step, NORM_STEPS * (prep + 1))
                    if mode in (DENSE, FRONT):
                        pe.wait_ge(head_step, HEAD_STEPS * k_batch + 16 * (TILES - 1) + 2)
                    else:
                        pe.wait_ge(gate_step, n * GATE_STEPS + 2)
                    transpose_tiles(pe, y, turn, ident[:, :]).then_inc(y_turned, 1)

        def turn_acc(pe, n):
            pe.wait_ge(acc_out, 2 * n)
            for t in range(TILES):
                for k in range(KD):
                    last = pe.transpose(turn_rows[:, t, k * P:(k + 1) * P],
                                        acc_sb[:, k, t * P:(t + 1) * P], ident[:, :])
            last.then_inc(acc_turned, 1)

        def copy_acc(act, n):
            act.wait_ge(down_done, n * HID_TILES)
            for k in range(KD):
                act.activation(acc_sb[:, k, :], acc[:, k, :], ACT.Identity, bias=b2_sum[:, k:k + 1],
                               scale=1.0 / WS).then_inc(acc_out, 1)

        def add_stage(dve, n, batch):
            dve.wait_ge(acc_turned, n)
            dve.wait_ge(gate_step, n * GATE_STEPS)
            for t in range(TILES):
                xt = x[:, batch, t, :]
                dve.scalar_tensor_tensor(xt, turn_rows[:, t, :], half_gain[:, t:t + 1], xt,
                                         ALU.mult, ALU.add).then_inc(x_added, 1)

        def gate_logits(dve, n):
            dve.wait_ge(logit_done, n + 1)
            dve.tensor_scalar(logit_rows[:, :], turn[0:EXPERTS, 0, :], 1.0 / WS, gate_bias[:, 0:1],
                              ALU.mult, ALU.add).then_inc(gate_step, 1)

        def gate_norm(dve, n, part):
            at = n * GATE_STEPS
            ms, r, mx, minus = (gate_c[:, i, :] for i in (0, 1, 3, 5))
            wide = [P, TILES, EXPERTS]
            if part == 1:
                return gate_shift(dve, at + 8 + NEWTON_STEPS, r, mx, wide)
            dve.wait_ge(logit_turned, n + 1)
            dve.tensor_copy(logit[:, :, :], turn[:, 1, 0:TILES * EXPERTS].rearrange("p (t e) -> p t e", t=TILES)
                            ).then_inc(gate_step, 1)
            dve.wait_ge(gate_step, at + 2)
            dve.tensor_tensor(logit_sq[:, :, :], logit[:, :, :], logit[:, :, :], ALU.mult).then_inc(gate_step, 1)
            dve.wait_ge(gate_step, at + 3)
            dve.tensor_reduce(ms, logit_sq[:, :, :], AX.X, ALU.add).then_inc(gate_step, 1)
            dve.wait_ge(gate_step, at + 4)
            dve.tensor_scalar(ms, ms, 1.0 / EXPERTS, F32_EPS, ALU.mult, ALU.add).then_inc(gate_step, 1)
            rsqrt_start(dve, gate_step, at + 5, ms, r)
            dve.tensor_scalar(minus, ms, -0.5, None, ALU.mult).then_inc(gate_step, 1)

        def gate_shift(dve, at, r, mx, wide):
            dve.wait_ge(gate_step, at)
            dve.tensor_tensor(logit[:, :, :], logit[:, :, :], r.unsqueeze(2).to_broadcast(wide),
                              ALU.mult).then_inc(gate_step, 1)
            dve.wait_ge(gate_step, at + 1)
            dve.tensor_tensor(logit[:, :, :], logit[:, :, :], rms_w[:, :].unsqueeze(1).to_broadcast(wide),
                              ALU.mult).then_inc(gate_step, 1)
            dve.wait_ge(gate_step, at + 2)
            dve.tensor_reduce(mx, logit[:, :, :], AX.X, ALU.max).then_inc(gate_step, 1)
            dve.wait_ge(gate_step, at + 3)
            dve.tensor_tensor(logit[:, :, :], logit[:, :, :], mx.unsqueeze(2).to_broadcast(wide),
                              ALU.subtract).then_inc(gate_step, 1)

        def gate_gain(dve, n):
            at = (n + 1) * GATE_STEPS - 4
            s = gate_c[:, 4, :]
            dve.wait_ge(gate_exp, n + 1)
            dve.tensor_reduce(s, logit[:, :, :], AX.X, ALU.add).then_inc(gate_step, 1)
            dve.wait_ge(gate_step, at + 1)
            dve.tensor_scalar(s, s, 1e-6, 1.0, ALU.mult, ALU.add).then_inc(gate_step, 1)
            dve.wait_ge(gate_step, at + 2)
            dve.reciprocal(s, s).then_inc(gate_step, 1)
            dve.wait_ge(gate_step, at + 3)
            dve.tensor_scalar(half_gain[:, :], s, 0.5, None, ALU.mult).then_inc(gate_step, 1)

        def split_turned(dve, hi, lo, turned, count, split, at):
            dve.wait_ge(turned, count)
            for k in range(KD):
                dve.tensor_copy(hi[:, k, :], turn[:, k, :]).then_inc(split, 1)
            dve.wait_ge(split, at + KD)
            for k in range(KD):
                dve.tensor_tensor(lo[:, k, :], turn[:, k, :], hi[:, k, :], ALU.subtract).then_inc(split, 1)

        def rows_qkv(dve, j, t):
            at = HEAD_STEPS * j + 16 * t
            dve.wait_ge(qkv_done, TILES * j + t + 1)
            dve.scalar_tensor_tensor(qk[:, :], turn[:, 0, :], 1.0 / WS, qkv_bias[:, 0:2 * D],
                                     ALU.mult, ALU.add).then_inc(head_step, 1)
            dve.scalar_tensor_tensor(v_rows[:, t, :], turn[:, 1, 0:D], 1.0 / WS, qkv_bias[:, 2 * D:QKV],
                                     ALU.mult, ALU.add).then_inc(head_step, 1)
            pairs = qk[:, :].rearrange("p (h i two) -> p h i two", i=HEAD_DIM // 2, two=2)
            out = qk_rot[:, :].rearrange("p (h i two) -> p h i two", i=HEAD_DIM // 2, two=2)
            wide = [P, 2 * HEADS, HEAD_DIM // 2]
            cos = rope[:, t, 0, :].unsqueeze(1).to_broadcast(wide)
            sin = rope[:, t, 1, :].unsqueeze(1).to_broadcast(wide)
            r = [rot[:, i, :].rearrange("p (h i) -> p h i", i=HEAD_DIM // 2) for i in range(4)]
            dve.wait_ge(head_step, at + 1)
            for i, (half, table) in enumerate(((0, cos), (1, sin), (0, sin), (1, cos))):
                dve.tensor_tensor(r[i], pairs[:, :, :, half], table, ALU.mult).then_inc(head_step, 1)
            dve.wait_ge(head_step, at + 6)
            dve.tensor_tensor(out[:, :, :, 0], r[0], r[1], ALU.subtract).then_inc(head_step, 1)
            dve.tensor_tensor(out[:, :, :, 1], r[2], r[3], ALU.add).then_inc(head_step, 1)


        def rows_score(dve, j, t, g):
            at = HEAD_STEPS * j + 16 * t + 8 + 2 * g
            wide = [P, GROUP, HEADS, HEAD_DIM]
            q4 = qk_rot[:, g * GROUP * HEAD_DIM:(g + 1) * GROUP * HEAD_DIM].rearrange(
                "p (i d) -> p i d", d=HEAD_DIM).unsqueeze(2).to_broadcast(wide)
            k4 = qk_rot[:, D:2 * D].rearrange("p (j d) -> p j d", d=HEAD_DIM).unsqueeze(1).to_broadcast(wide)
            pr = prod[:, :].rearrange("p (i j d) -> p i j d", i=GROUP, j=HEADS)
            dve.wait_ge(head_step, at)
            dve.tensor_tensor(pr, q4, k4, ALU.mult).then_inc(head_step, 1)
            dve.wait_ge(head_step, at + 1)
            row = t * HEADS + g * GROUP
            dve.tensor_reduce(score[:, row:row + GROUP, :], pr, AX.X, ALU.add).then_inc(head_step, 1)

        def score_shift(dve, j):
            at = HEAD_STEPS * j + 64
            dve.wait_ge(head_step, at)
            dve.tensor_reduce(s_col[:, 0, :], score[:, :, :], AX.X, ALU.max).then_inc(head_step, 1)
            dve.wait_ge(head_step, at + 1)
            dve.tensor_tensor(score[:, :, :], score[:, :, :],
                              s_col[:, 0, :].unsqueeze(2).to_broadcast([P, TILES * HEADS, HEADS]),
                              ALU.subtract).then_inc(head_step, 1)

        def score_sum(dve, j):
            at = HEAD_STEPS * j + 66
            dve.wait_ge(head_exp, j + 1)
            dve.tensor_reduce(s_col[:, 1, :], score[:, :, :], AX.X, ALU.add).then_inc(head_step, 1)
            dve.wait_ge(head_step, at + 1)
            dve.reciprocal(s_col[:, 2, :], s_col[:, 1, :]).then_inc(head_step, 1)

        def rows_values(dve, j, t, g):
            at = HEAD_STEPS * j + 68 + 8 * t + 2 * g
            wide = [P, GROUP, HEAD_DIM, HEADS]
            row = t * HEADS + g * GROUP
            e4 = score[:, row:row + GROUP, :].unsqueeze(2).to_broadcast(wide)
            v4 = v_rows[:, t, :].rearrange("p (j d) -> p d j", d=HEAD_DIM).unsqueeze(1).to_broadcast(wide)
            pr = prod[:, :].rearrange("p (i d j) -> p i d j", i=GROUP, d=HEAD_DIM)
            dve.wait_ge(head_step, at)
            dve.tensor_tensor(pr, e4, v4, ALU.mult).then_inc(head_step, 1)
            dve.wait_ge(head_step, at + 1)
            dve.tensor_reduce(o_rows[:, t, g * GROUP * HEAD_DIM:(g + 1) * GROUP * HEAD_DIM].rearrange(
                "p (i d) -> p i d", d=HEAD_DIM), pr, AX.X, ALU.add).then_inc(head_step, 1)

        def add_attention(dve, j):
            at = HEAD_STEPS * j + 100
            heads = o_rows[:, :, :].rearrange("p t (i d) -> p (t i) d", d=HEAD_DIM)
            dve.wait_ge(head_step, at)
            dve.tensor_tensor(heads, heads, s_col[:, 2, :].unsqueeze(2).to_broadcast([P, TILES * HEADS, HEAD_DIM]),
                              ALU.mult).then_inc(head_step, 1)
            dve.wait_ge(head_step, at + 1)
            dve.tensor_tensor(x[:, j, :, :], x[:, j, :, :], o_rows[:, :, :], ALU.add).then_inc(head_step, 1)

        def normalise(dve, q, batch, part):
            at = NORM_STEPS * q + TILES
            if part == 0:
                layernorm_stats(dve, norm_step, x[:, batch, :, :], stats)
            elif part == 1:
                rsqrt_start(dve, norm_step, at + VARIANCE_STEPS, var[:, :], rstd[:, :])
            elif part == LN_PARTS - 1:
                layernorm_apply(dve, norm_step, NORM_STEPS * (q + 1) - TILES, x[:, batch, :, :], y, ln_col, rstd[:, :])

        def pool_normalise(pool, q):
            at = NORM_STEPS * q + TILES
            pool_variance(pool, norm_step, at, stats, ln_col, norm_const, var[:, :], minus_half[:, :])
            pool_newton(pool, norm_step, at + VARIANCE_STEPS + 2, norm_const, minus_half[:, :], rstd[:, :], newton[:, :])

        def pool_stage(pool, n, z_norm=None, prep=None):
            if z_norm is not None:
                pool_normalise(pool, z_norm)
            pool_newton(pool, gate_step, GATE_STEPS * n + 8, norm_const, gate_c[:, 5, :], gate_c[:, 1, :], gate_c[:, 2, :])
            if prep is not None:
                pool_normalise(pool, prep)

        def head_piece(dve, j, i):
            if i < SHIFT:
                t, part = i // TILE_PIECES, i % TILE_PIECES
                if part == 0:
                    rows_qkv(dve, j, t)
                else:
                    rows_score(dve, j, t, part - 1)
            elif i == SHIFT:
                score_shift(dve, j)
            elif i == SHIFT + 1:
                score_sum(dve, j)
            elif i < PIECES - 1:
                rows_values(dve, j, (i - SHIFT - 2) // GROUPS, (i - SHIFT - 2) % GROUPS)
            else:
                add_attention(dve, j)

        def dve_stage(dve, n, odd=0, first=False, prev=None, mode=None, k_batch=None, z_norm=None, prep=None):
            if first:
                split_turned(dve, y_hi[:, 0, :, :], y_lo[:, 0, :, :], y_turned, 1, y_split, 0)
            for ht in range(HID_TILES):
                g = ht % GBUF
                if mode in (DENSE, FRONT) and ht == Z_AT:
                    dve.wait_ge(x_added, 4 * n)
                if first and ht == PREP_AT:
                    dve.wait_ge(x_rest, 16 * (BATCH - 1))
                if mode in (DENSE, BACK) and prep is not None and ht == PREP_AT:
                    dve.wait_ge(head_step, HEAD_STEPS * (k_batch + 1))
                dve.wait_ge(gelu_done, 2 * (n * HID_TILES + ht + 1))
                if not (first and ht < GBUF):
                    dve.wait_ge(down_done, n * HID_TILES + ht - GBUF + 1)
                dve.tensor_tensor(g_lo[:, g, :], g_full[:, g, :], g_hi[:, g, :],
                                  ALU.subtract).then_inc(tail_done, 1)
                for c in chunks_at(ht) if first else ():
                    split_chunk_tail(dve, c)
                if ht == 1 and not first:
                    add_stage(dve, n, prev)
                if ht == 2:
                    gate_logits(dve, n)
                if ht in GATE_AT:
                    gate_norm(dve, n, GATE_AT.index(ht))
                if ht == GAIN_AT:
                    gate_gain(dve, n)
                if mode in (DENSE, FRONT) and Z_AT <= ht < Z_AT + LN_PARTS:
                    normalise(dve, z_norm, k_batch, ht - Z_AT)
                if mode in (DENSE, FRONT) and ht == Z_AT + LN_PARTS + 1:
                    split_turned(dve, z_hi, z_lo, z_turned, k_batch + 1, z_split, 4 * k_batch)
                for i in pieces_at(ht, mode):
                    head_piece(dve, k_batch, i)
                if prep is not None and PREP_AT <= ht < PREP_AT + LN_PARTS:
                    normalise(dve, prep[0], prep[1], ht - PREP_AT)
                if prep is not None and ht == NEXT_AT + 1:
                    for k in range(KD):
                        dve.wait_ge(y_split, 4 * (n + 1) + KD)
                        dve.tensor_tensor(y_lo[:, 1 - odd, k, :], turn[:, k, :], y_hi[:, 1 - odd, k, :],
                                          ALU.subtract).then_inc(y_split, 1)

        def act_stage(act, n, odd=0, first=False, mode=None, k_batch=None, last=False):
            if not first:
                copy_acc(act, n)
            for ht in range(HID_TILES):
                g = ht % GBUF
                act.wait_ge(up_done, n * HID_TILES + ht + 1)
                if not (first and ht < GBUF):
                    act.wait_ge(down_done, n * HID_TILES + ht - GBUF + 1)
                for out in (g_full, g_hi):
                    act.activation(out[:, g, :], hid[:, ht % 4, :], ACT.Gelu, bias=b1_col[:, ht:ht + 1],
                                   scale=1.0 / WS).then_inc(gelu_done, 1)
                for c in chunks_at(ht) if first else ():
                    split_chunk_head(act, c)
                if ht == NEXT_AT + 1 and not last:
                    act.wait_ge(y_turned, n + 2)
                    for k in range(KD):
                        act.activation(y_hi[:, 1 - odd, k, :], turn[:, k, :], ACT.Copy).then_inc(y_split, 1)
                if ht == SCORE_EXP_AT.get(mode):
                    act.wait_ge(head_step, HEAD_STEPS * k_batch + 66)
                    act.activation(score[:, :, :], score[:, :, :], ACT.Exp,
                                   scale=float(HEAD_DIM) ** -0.5).then_inc(head_exp, 1)
                if ht == GATE_EXP_AT:
                    act.wait_ge(gate_step, (n + 1) * GATE_STEPS - 4)
                    act.activation(logit[:, :, :], logit[:, :, :], ACT.Exp, scale=2.0).then_inc(gate_exp, 1)

        LAST = BATCH - 1

        with nc.Block() as block:
            @block.tensor
            def _(pe):
                pe.wait_ge(norm_step, NORM_STEPS)
                transpose_tiles(pe, y, turn, ident[:, :]).then_inc(y_turned, 1)
                pe_stage(pe, 0, first=True, prep=1)
                pe.wait_ge(chunk_tail, len(chunks))
                pe_stage(pe, 1, odd=1, mode=DENSE, k_batch=0, z_norm=2, prep=3)
                with pe.Fori(1, LAST) as k:
                    pe_stage(pe, 2 * k, mode=FRONT, k_batch=k, z_norm=3 * k + 1, prep=3 * k + 2)
                    pe_stage(pe, 2 * k + 1, odd=1, mode=BACK, k_batch=k, prep=3 * k + 3)
                pe_stage(pe, 2 * LAST, mode=DENSE, k_batch=LAST, z_norm=3 * LAST + 1, prep=3 * LAST + 2)
                pe_stage(pe, 2 * LAST + 1, odd=1)
                turn_acc(pe, STAGES)

            @block.vector
            def _(dve):
                dve.wait_ge(x_first, 16)
                for part in range(LN_PARTS):
                    normalise(dve, 0, 0, part)
                for c in range(2):
                    split_chunk_tail(dve, c)
                dve_stage(dve, 0, first=True, prep=(1, 1))
                dve_stage(dve, 1, odd=1, prev=0, mode=DENSE, k_batch=0, z_norm=2, prep=(3, 0))
                with dve.Fori(1, LAST) as k:
                    dve_stage(dve, 2 * k, prev=k, mode=FRONT, k_batch=k, z_norm=3 * k + 1,
                              prep=(3 * k + 2, k + 1))
                    dve_stage(dve, 2 * k + 1, odd=1, prev=k - 1, mode=BACK, k_batch=k,
                              prep=(3 * k + 3, k))
                dve_stage(dve, 2 * LAST, prev=LAST, mode=DENSE, k_batch=LAST, z_norm=3 * LAST + 1,
                          prep=(3 * LAST + 2, LAST))
                dve_stage(dve, 2 * LAST + 1, odd=1, prev=LAST - 1)
                add_stage(dve, STAGES, LAST)

            @block.sync
            def _(sp):
                for c in range(SLOTS, len(chunks)):
                    if c == SLOTS + 2:
                        for b in range(1, BATCH):
                            sp.dma_start(x[:, b], io["x"][b].rearrange("(t p) d -> p t d", p=P)).then_inc(x_rest, 16)
                    load_chunk(sp, c)

            @block.gpsimd
            def _(pool):
                for i, value in enumerate(NORM_CONSTANTS):
                    pool.memset(norm_const[:, i, :], value).then_inc(const_set, 1)
                pool.wait_ge(const_set, len(NORM_CONSTANTS))
                pool_normalise(pool, 0)
                pool_stage(pool, 0, prep=1)
                pool_stage(pool, 1, z_norm=2, prep=3)
                with pool.Fori(1, LAST) as k:
                    pool_stage(pool, 2 * k, z_norm=3 * k + 1, prep=3 * k + 2)
                    pool_stage(pool, 2 * k + 1, prep=3 * k + 3)
                pool_stage(pool, 2 * LAST, z_norm=3 * LAST + 1, prep=3 * LAST + 2)
                pool_stage(pool, 2 * LAST + 1)

            @block.scalar
            def _(act):
                for c in range(2):
                    split_chunk_head(act, c)
                act_stage(act, 0, first=True)
                act_stage(act, 1, odd=1, mode=DENSE, k_batch=0)
                with act.Fori(1, LAST) as k:
                    act_stage(act, 2 * k, mode=FRONT, k_batch=k)
                    act_stage(act, 2 * k + 1, odd=1, mode=BACK, k_batch=k)
                act_stage(act, 2 * LAST, mode=DENSE, k_batch=LAST)
                act_stage(act, 2 * LAST + 1, odd=1, last=True)
                copy_acc(act, STAGES)


ROWS = 64
TAKEN = ROWS - 1
PAIRS = BATCH // 2
ALL_TILES = BATCH * TILES
FFN = 1024
ROUTED_EXT = D + 4
SENTINEL = -3.0e38
MASK_FLOOR = -1.0e38
RMS_EPS = 1e-6
TWO_PI_PARTS = (6.28125, 0.0019350051879882812, 3.019916050561733e-07)
ROUND = 1.5 * 2.0 ** 23


def routed_layer(nc, keep, tag, x, ident, io, out=None):
    with ExitStack() as ctx:
        def sb(name, shape, dt=F32):
            return ctx.enter_context(nc.sbuf_tensor(f"{tag}_{name}", shape, dt))

        def sem(name):
            return keep.enter_context(nc.semaphore(f"{tag}_{name}"))

        ps = ctx.enter_context(nc.psum_tensor(f"{tag}_ps", [P, 8, 512], F32))
        y = sb("y", [P, BATCH, TILES, ROUTED_EXT])
        one_hot = sb("one_hot", [P, PAIRS, TILES, 2, ROWS])
        slot_hot = sb("slot_hot", [P, PAIRS, TILES, P], F16)
        stay = sb("stay", [P, TILES, BATCH])
        xs = sb("xs", [P, PAIRS, ROUTED_EXT])
        mask_sel = sb("mask_sel", [P, PAIRS, ROWS])
        wqkv = sb("wqkv", [P, KD, QKV])
        wo = sb("wo", [P, KD, D])
        w1 = sb("w1", [P, KD, FFN])
        w2 = sb("w2", [P, FFN // P, D])
        ln1 = sb("ln1", [P, D])
        ln2 = sb("ln2", [P, D])
        inv_freq = sb("inv_freq", [P, HEAD_DIM // 2])
        iota_row = sb("iota_row", [P, ROWS])
        head_block = sb("head_block", [P, 8])

        with ExitStack() as part:
            def tmp(name, shape, dt=F32):
                return part.enter_context(nc.sbuf_tensor(f"{tag}_{name}", shape, dt))

            def tsem(name):
                return keep.enter_context(nc.semaphore(f"{tag}_{name}"))

            router = tmp("router", [P, D])
            router_bias = tmp("router_bias", [P, 1])
            weighed = tmp("weighed", [P, 2, TILES, D])
            w_col = tmp("w_col", [P, BATCH, TILES])
            w_row = tmp("w_row", [BATCH, SEQ])
            work = tmp("work", [BATCH, SEQ])
            best = tmp("best", [BATCH, 8])
            row = tmp("row", [BATCH, 6, SEQ])
            last_at = tmp("last_at", [BATCH, 1])
            slot_col = tmp("slot_col", [P, TILES, BATCH])
            pos_rows = tmp("pos_rows", [16, P], I32)
            pos_rows_f = tmp("pos_rows_f", [16, P])
            mask_idx = tmp("mask_idx", [P, PAIRS], I32)
            mask_rows = tmp("mask_rows", [P, PAIRS, SEQ])
            mask_t = tmp("mask_t", [P, TILES, P])
            stats = tmp("stats", [P, ALL_TILES, 6])
            ln_col = tmp("ln_col", [P, 4, ALL_TILES])
            var = tmp("var", [P, ALL_TILES])
            rstd = tmp("rstd", [P, ALL_TILES])
            shift = tmp("shift", [P, ALL_TILES])
            newton = tmp("newton", [P, ALL_TILES])

            small_in = tsem("small_in")
            weights_in = sem("weights_in")
            made = tsem("made")
            norm_step = tsem("norm_step")
            normed = tsem("normed")
            weigh_step = tsem("weigh_step")
            rows_turned = tsem("rows_turned")
            pick_step = tsem("pick_step")
            cols_turned = tsem("cols_turned")
            hot_step = tsem("hot_step")
            gathered = tsem("gathered")
            sel_out = tsem("sel_out")
            hot_turned = tsem("hot_turned")
            hot_out = tsem("hot_out")
            mask_in = [keep.software(nc.semaphore(f"{tag}_mask_in{i}")) for i in range(PAIRS)]
            mask_turned = tsem("mask_turned")
            mask_out = tsem("mask_out")
            mask_picked = tsem("mask_picked")
            mask_done = tsem("mask_done")

            COLUMNS_AT = ALL_TILES + LN_COLUMN_STEPS
            LN_ON_ACT = TILES - 1
            MASK_BATCHES = 4
            idx_row = row[:, 0, :]
            ones_row = row[:, 1, :]

            with nc.Block() as block:
                @block.sync
                def _(sp):
                    for name in ("router_w",):
                        sp.dma_start(router[:, :], io["router_w"].rearrange("d o -> (d o)").partition_broadcast(P)).then_inc(small_in, 16)
                    sp.dma_start(router_bias[:, :], io["router_b"].partition_broadcast(P)).then_inc(small_in, 16)
                    sp.dma_start(pos_rows[:, :], io["position_ids"][:, 0:SEQ].rearrange("b (t p) -> b t p", p=P)
                                 ).then_inc(small_in, 16)
                    for i, name in enumerate(("wq", "wk", "wv")):
                        sp.dma_start(wqkv[:, :, i * D:(i + 1) * D], io[name].rearrange("(k p) n -> p k n", p=P)).then_inc(weights_in, 16)
                    sp.dma_start(wo[:, :, :], io["wo"].rearrange("(k p) n -> p k n", p=P)).then_inc(weights_in, 16)
                    sp.dma_start(w1[:, :, :], io["w1"].rearrange("(k p) n -> p k n", p=P)).then_inc(weights_in, 16)
                    sp.dma_start(w2[:, :, :], io["w2"].rearrange("(f p) n -> p f n", p=P)).then_inc(weights_in, 16)
                    sp.dma_start(ln1[:, :], io["ln1"].partition_broadcast(P)).then_inc(weights_in, 16)
                    sp.dma_start(ln2[:, :], io["ln2"].partition_broadcast(P)).then_inc(weights_in, 16)
                    sp.dma_start(inv_freq[:, :], io["inv_freq"].partition_broadcast(P)).then_inc(weights_in, 16)

                @block.gpsimd
                def _(pool):
                    pool.iota(iota_row[:, :], pattern=[[1, ROWS]], base=0, channel_multiplier=0,
                              allow_small_or_imprecise_dtypes=True).then_inc(made, 1)
                    pool.iota(idx_row, pattern=[[1, SEQ]], base=1, channel_multiplier=0,
                              allow_small_or_imprecise_dtypes=True).then_inc(made, 1)
                    pool.memset(ones_row, 1.0).then_inc(made, 1)
                    for b in range(BATCH):
                        pool.iota(y[:, b, :, D + 2], pattern=[[P, TILES]], base=min(b, MASK_BATCHES - 1) * 1024,
                                  channel_multiplier=1, allow_small_or_imprecise_dtypes=True).then_inc(made, 1)
                    pool.memset(y[:, :, :, D + 3], 0.0).then_inc(made, 1)
                    pool.memset(head_block[:, :], 1.0).then_inc(made, 1)
                    pool.wait_ge(made, 13)
                    pool.affine_select(out=head_block[:, :], in_=head_block[:, :], compare_op=ALU.is_ge, fill=0.0,
                                       base=0, pattern=[[-HEAD_DIM, 8]], channel_multiplier=1).then_inc(made, 1)
                    pool.wait_ge(made, 14)
                    pool.affine_select(out=head_block[:, :], in_=head_block[:, :], compare_op=ALU.is_ge, fill=0.0,
                                       base=HEAD_DIM - 1, pattern=[[HEAD_DIM, 8]],
                                       channel_multiplier=-1).then_inc(made, 1)
                    mask_view = io["attention_mask"].rearrange("b o q (h k) -> (b o q h) k", k=SEQ)
                    for pr in range(PAIRS):
                        pool.wait_ge(sel_out, 2 * (pr + 1))
                        pool.indirect_dma_start(out=mask_rows[:, pr, :], out_offset=None, in_=mask_view,
                                                in_offset=bass.IndirectOffsetOnAxis(ap=mask_idx[:, pr:pr + 1], axis=0)
                                                ).then_inc(mask_in[pr], 16)

                @block.vector
                def _(dve):
                    dve.wait_ge(small_in, 48)
                    dve.tensor_copy(pos_rows_f[:, :], pos_rows[:, :]).then_inc(hot_step, 1)
                    with dve.Fori(0, BATCH) as b:
                        for t in range(TILES):
                            dve.bn_stats(stats[:, TILES * b + t, :], x[:, b, t, :]).then_inc(norm_step, 1)
                    layernorm_columns(dve, norm_step, ALL_TILES, stats, ln_col, var[:, :], rstd[:, :], newton[:, :])
                    dve.wait_ge(norm_step, COLUMNS_AT)
                    dve.scalar_tensor_tensor(shift[:, :], ln_col[:, 3, :], -1.0, rstd[:, :], ALU.mult,
                                             ALU.mult).then_inc(norm_step, 1)
                    dve.wait_ge(norm_step, COLUMNS_AT + 1)
                    with dve.Fori(0, BATCH // 2) as two:
                        for i in range(2):
                            b = 2 * two + i
                            col = TILES * b + LN_ON_ACT
                            dve.tensor_scalar(y[:, b, LN_ON_ACT, 0:D], x[:, b, LN_ON_ACT, :], rstd[:, bass.ds(col, 1)],
                                              shift[:, bass.ds(col, 1)], ALU.mult, ALU.add).then_inc(weigh_step, 1)
                            dve.wait_ge(normed, LN_ON_ACT * (b + 1))
                            dve.wait_ge(weigh_step, 3 * b + 1)
                            dve.tensor_tensor(weighed[:, i, :, :], y[:, b, :, 0:D],
                                              router[:, :].unsqueeze(1).to_broadcast([P, TILES, D]),
                                              ALU.mult).then_inc(weigh_step, 1)
                            dve.wait_ge(weigh_step, 3 * b + 2)
                            dve.tensor_reduce(w_col[:, b, :], weighed[:, i, :, :], AX.X, ALU.add).then_inc(weigh_step, 1)
                    dve.wait_ge(weigh_step, 3 * BATCH)
                    dve.tensor_scalar(w_col[:, :, :], w_col[:, :, :], router_bias[:, 0:1], None,
                                      ALU.add).then_inc(weigh_step, 1)
                    dve.wait_ge(weigh_step, 3 * BATCH + 1)
                    dve.wait_ge(made, 15)
                    dve.tensor_copy(y[:, :, :, D], w_col[:, :, :]).then_inc(hot_step, 1)
                    dve.wait_ge(cols_turned, 1)
                    pos_cols = ps[:, 1, 0:16].rearrange("p (b t) -> p b t", t=TILES)
                    dve.tensor_copy(y[:, 0:MASK_BATCHES, :, D + 1], pos_cols).then_inc(hot_step, 1)
                    dve.tensor_copy(y[:, MASK_BATCHES:BATCH, :, D + 1],
                                    pos_cols[:, MASK_BATCHES - 1:MASK_BATCHES, :].to_broadcast(
                                        [P, BATCH - MASK_BATCHES, TILES])).then_inc(hot_step, 1)
                    dve.wait_ge(rows_turned, 1)
                    dve.tensor_copy(w_row[:, :], ps[0:BATCH, 0, :]).then_inc(pick_step, 1)
                    dve.wait_ge(pick_step, 1)
                    dve.tensor_copy(work[:, :], w_row[:, :]).then_inc(pick_step, 1)
                    for r in range(ROWS // 8):
                        dve.wait_ge(pick_step, 2 + 2 * r)
                        dve.max(best[:, :], work[:, :]).then_inc(pick_step, 1)
                        dve.wait_ge(pick_step, 3 + 2 * r)
                        dve.match_replace(out=work[:, :], in_to_replace=best[:, :], in_values=work[:, :],
                                          imm_value=SENTINEL).then_inc(pick_step, 1)
                    at = 2 + 2 * (ROWS // 8)
                    least = best[:, 7:8]
                    taken, tied, cum = row[:, 2, :], row[:, 3, :], row[:, 4, :]
                    slot, pass_row = row[:, 5, :], row[:, 3, :]
                    dve.wait_ge(pick_step, at)
                    dve.tensor_scalar(taken, work[:, :], SENTINEL, None, ALU.is_equal).then_inc(pick_step, 1)
                    dve.wait_ge(pick_step, at + 1)
                    dve.scalar_tensor_tensor(tied, w_row[:, :], least, taken, ALU.is_equal, ALU.mult).then_inc(pick_step, 1)
                    dve.wait_ge(pick_step, at + 2)
                    dve.tensor_tensor(tied, tied, idx_row, ALU.mult).then_inc(pick_step, 1)
                    dve.wait_ge(pick_step, at + 3)
                    dve.tensor_reduce(last_at[:, :], tied, AX.X, ALU.max).then_inc(pick_step, 1)
                    dve.wait_ge(pick_step, at + 4)
                    dve.scalar_tensor_tensor(taken, idx_row, last_at[:, 0:1], taken, ALU.not_equal,
                                             ALU.mult).then_inc(pick_step, 1)
                    dve.wait_ge(pick_step, at + 5)
                    dve.tensor_tensor_scan(cum, ones_row, taken, 0.0, ALU.mult, ALU.add).then_inc(pick_step, 1)
                    dve.wait_ge(pick_step, at + 6)
                    dve.tensor_tensor(slot, cum, taken, ALU.mult).then_inc(pick_step, 1)
                    dve.wait_ge(pick_step, at + 7)
                    dve.tensor_scalar(slot, slot, -1.0, None, ALU.add).then_inc(pick_step, 1)
                    dve.tensor_scalar(pass_row, w_row[:, :], least, 0.5, ALU.is_le, ALU.mult).then_inc(pick_step, 1)
                    dve.wait_ge(cols_turned, 2)
                    dve.tensor_copy(slot_col[:, :, :], ps[:, 2, 0:TILES * BATCH].rearrange("p (t b) -> p t b", b=BATCH)
                                    ).then_inc(hot_step, 1)
                    dve.tensor_copy(stay[:, :, :], ps[:, 2, 64:64 + TILES * BATCH].rearrange("p (t b) -> p t b", b=BATCH)
                                    ).then_inc(hot_step, 1)
                    dve.wait_ge(hot_step, 6)
                    for b in range(BATCH):
                        dve.tensor_tensor(one_hot[:, b // 2, :, b % 2, :],
                                          iota_row[:, :].unsqueeze(1).to_broadcast([P, TILES, ROWS]),
                                          slot_col[:, :, b:b + 1].to_broadcast([P, TILES, ROWS]),
                                          ALU.is_equal).then_inc(hot_step, 1)
                    for pr in range(PAIRS):
                        dve.wait_ge(gathered, pr + 1)
                        dve.tensor_copy(xs[:, pr, :], ps[:, 3 + pr, 0:ROUTED_EXT]).then_inc(sel_out, 1)
                        dve.tensor_scalar(mask_idx[:, pr:pr + 1], ps[:, 3 + pr, D + 2:D + 3], 2.0, None,
                                          ALU.mult).then_inc(sel_out, 1)
                    for pr in range(PAIRS):
                        dve.wait_ge(mask_turned, pr + 1)
                        if pr > 0:
                            dve.wait_ge(mask_picked, pr)
                        dve.tensor_scalar(mask_t[:, :, :], ps[:, 3 + pr % 2, :].rearrange("p (t r) -> p t r", t=TILES),
                                          MASK_FLOOR, None, ALU.max).then_inc(mask_out, 1)
                        dve.wait_ge(mask_picked, pr + 1)
                        for i in range(2):
                            own = slice(i * ROWS, (i + 1) * ROWS)
                            dve.tensor_copy(mask_sel[own, pr, :], ps[own, 5 + pr % 2, own]).then_inc(mask_done, 1)
                    dve.wait_ge(mask_done, 2 * PAIRS)
                    dve.memset(mask_sel[:, :, TAKEN:ROWS], SENTINEL)

                @block.tensor
                def _(pe):
                    pe.wait_ge(hot_step, 1)
                    pe.transpose(ps[:, 1, 0:16], pos_rows_f[:, :], ident[0:16, 0:16]).then_inc(cols_turned, 1)
                    pe.wait_ge(weigh_step, 3 * BATCH + 1)
                    for t in range(TILES):
                        last = pe.transpose(ps[0:BATCH, 0, t * P:(t + 1) * P], w_col[:, :, t], ident[:, :])
                    last.then_inc(rows_turned, 1)
                    pe.wait_ge(pick_step, 2 + 2 * (ROWS // 8) + 9)
                    for i, r in ((0, 5), (1, 3)):
                        for t in range(TILES):
                            at = 64 * i + t * BATCH
                            last = pe.transpose(ps[:, 2, at:at + BATCH], row[:, r, t * P:(t + 1) * P],
                                                ident[0:BATCH, 0:BATCH])
                    last.then_inc(cols_turned, 1)
                    for pr in range(PAIRS):
                        pe.wait_ge(hot_step, 6 + 2 * (pr + 1))
                        for i in range(2):
                            for t in range(TILES):
                                last = pe.matmul(ps[i * ROWS:(i + 1) * ROWS, 3 + pr, 0:ROUTED_EXT],
                                                 one_hot[:, pr, t, i, :], y[:, 2 * pr + i, t, :],
                                                 start=(t == 0), stop=(t == TILES - 1))
                        last.then_inc(gathered, 1)
                    for pr in range(PAIRS):
                        bank = (7, 0)[pr % 2]
                        if pr >= 2:
                            pe.wait_ge(hot_out, pr - 1)
                        for t in range(TILES):
                            last = pe.transpose(ps[:, bank, t * P:(t + 1) * P],
                                                one_hot[:, pr, t, :, :].rearrange("p i r -> p (i r)"), ident[:, :])
                        last.then_inc(hot_turned, 1)
                    for pr in range(PAIRS):
                        pe.wait_ge(mask_in[pr], 16)
                        if pr == 0:
                            pe.wait_ge(sel_out, 2 * PAIRS)
                        if pr >= 2:
                            pe.wait_ge(mask_done, 2 * (pr - 1))
                        for t in range(TILES):
                            last = pe.transpose(ps[:, 3 + pr % 2, t * P:(t + 1) * P],
                                                mask_rows[:, pr, t * P:(t + 1) * P], ident[:, :])
                        last.then_inc(mask_turned, 1)
                        pe.wait_ge(mask_out, pr + 1)
                        for t in range(TILES):
                            last = pe.matmul(ps[:, 5 + pr % 2, 0:P], mask_t[:, t, :],
                                             one_hot[:, pr, t, :, :].rearrange("p i r -> p (i r)"),
                                             start=(t == 0), stop=(t == TILES - 1))
                        last.then_inc(mask_picked, 1)

                @block.scalar
                def _(act):
                    act.wait_ge(norm_step, COLUMNS_AT + 1)
                    with act.Fori(0, BATCH) as b:
                        for t in range(LN_ON_ACT):
                            col = TILES * b + t
                            act.activation(y[:, b, t, 0:D], x[:, b, t, :], ACT.Identity, bias=shift[:, bass.ds(col, 1)],
                                           scale=rstd[:, bass.ds(col, 1)]).then_inc(normed, 1)
                    for pr in range(PAIRS):
                        act.wait_ge(hot_turned, pr + 1)
                        act.activation(slot_hot[:, pr, :, :].rearrange("p t n -> p (t n)"),
                                       ps[:, (7, 0)[pr % 2], :], ACT.Copy).then_inc(hot_out, 1)

        h = sb("h", [P, PAIRS, D])
        h_t = sb("h_t", [P, KD, PAIRS * P])
        sq = sb("sq", [P, PAIRS, D])
        col = sb("col", [P, 4, PAIRS])
        ang = sb("ang", [P, 4, PAIRS * HEAD_DIM // 2])
        rope = sb("rope", [P, 2, PAIRS, HEAD_DIM // 2])
        rot = sb("rot", [P, 4, D])
        qk = sb("qk", [P, 2, 2 * D])
        q_t = sb("q_t", [P, PAIRS, KD, P])
        k_blk = sb("k_blk", [P, PAIRS, KD, 2, 8, ROWS])
        v_blk = sb("v_blk", [P, BATCH, 8, 2, HEAD_DIM])
        s = sb("s", [P, 2, HEADS, ROWS])
        s_col = sb("s_col", [P, 2, 3, HEADS])
        p_t = sb("p_t", [P, 2, 8, P])
        o = sb("o", [P, 2, D])
        o_t = sb("o_t", [P, 2, KD, P])
        x1 = sb("x1", [P, PAIRS, D])
        gel = k_blk[:, :, :, :, :, :].rearrange("p r a i h c -> p (r a i) (h c)")[:, 0:FFN // P, :]
        proc = sb("proc", [P, PAIRS, D])
        proc_hi = sb("proc_hi", [P, PAIRS, D], F16)
        proc_lo = sb("proc_lo", [P, PAIRS, D], F16)

        rms_step = sem("rms_step")
        h_turned = sem("h_turned")
        h_out = sem("h_out")
        qk_done = sem("qk_done")
        v_done = sem("v_done")
        v_zeroed = sem("v_zeroed")
        v_out = sem("v_out")
        ang_step = sem("ang_step")
        sin_done = sem("sin_done")
        rot_step = sem("rot_step")
        qk_turned = sem("qk_turned")
        qt_out = sem("qt_out")
        kb_out = sem("kb_out")
        s_done = sem("s_done")
        s_step = sem("s_step")
        sum_step = sem("sum_step")
        s_exp = sem("s_exp")
        p_turned = sem("p_turned")
        p_out = sem("p_out")
        o_done = sem("o_done")
        o_out = sem("o_out")
        o_turned = sem("o_turned")
        ot_out = sem("ot_out")
        wo_done = sem("wo_done")
        x1_out = sem("x1_out")
        up_done = sem("up_done")
        gel_out = sem("gel_out")
        down_done = sem("down_done")
        proc_step = sem("proc_step")
        put_done = sem("put_done")
        passed = sem("passed")
        x_out = sem("x_out")
        put_out = sem("put_out")

        RMS_STEPS = 3 + RSQRT_STEPS + PAIRS

        def rmsnorm(dve, call, src, gain, bank_src=None):
            at = call * RMS_STEPS
            dve.tensor_tensor(sq[:, :, :], src, src, ALU.mult).then_inc(rms_step, 1)
            dve.wait_ge(rms_step, at + 1)
            dve.tensor_reduce(col[:, 0, :], sq[:, :, :], AX.X, ALU.add).then_inc(rms_step, 1)
            dve.wait_ge(rms_step, at + 2)
            dve.tensor_scalar(col[:, 0, :], col[:, 0, :], 1.0 / D, RMS_EPS, ALU.mult, ALU.add).then_inc(rms_step, 1)
            rsqrt_newton(dve, rms_step, at + 3, col[:, 0, :], col[:, 1, :], col[:, 2, :])
            dve.wait_ge(rms_step, at + 3 + RSQRT_STEPS)
            for pr in range(PAIRS):
                dve.scalar_tensor_tensor(h[:, pr, :], src[:, pr, :], col[:, 1, pr:pr + 1], gain[:, :],
                                         ALU.mult, ALU.mult).then_inc(rms_step, 1)

        def angles(dve):
            n = PAIRS * HEAD_DIM // 2
            a, k, r = ang[:, 0, :], ang[:, 1, :], ang[:, 2:4, :]
            dve.tensor_tensor(a.rearrange("p (r i) -> p r i", r=PAIRS),
                              xs[:, :, D + 1:D + 2].to_broadcast([P, PAIRS, HEAD_DIM // 2]),
                              inv_freq[:, :].unsqueeze(1).to_broadcast([P, PAIRS, HEAD_DIM // 2]),
                              ALU.mult).then_inc(ang_step, 1)
            at = 1
            for i, quarter in enumerate((0.0, 0.25)):
                dve.wait_ge(ang_step, at)
                dve.tensor_scalar(k, a, float(1.0 / (2.0 * np.pi)), quarter, ALU.mult, ALU.add).then_inc(ang_step, 1)
                dve.wait_ge(ang_step, at + 1)
                dve.tensor_scalar(k, k, ROUND, None, ALU.add).then_inc(ang_step, 1)
                dve.wait_ge(ang_step, at + 2)
                dve.tensor_scalar(k, k, ROUND, None, ALU.subtract).then_inc(ang_step, 1)
                src = a
                for m, part in enumerate(TWO_PI_PARTS):
                    dve.wait_ge(ang_step, at + 3 + m)
                    dve.scalar_tensor_tensor(r[:, i, :], k, -part, src, ALU.mult, ALU.add).then_inc(ang_step, 1)
                    src = r[:, i, :]
                dve.wait_ge(ang_step, at + 6)
                dve.tensor_scalar(r[:, i, :], r[:, i, :], float(np.pi / 2) * i, float(np.float32(np.pi)) * (1 - 1e-7),
                                  ALU.add, ALU.min).then_inc(ang_step, 1)
                dve.wait_ge(ang_step, at + 7)
                dve.tensor_scalar(r[:, i, :], r[:, i, :], -float(np.float32(np.pi)) * (1 - 1e-7), None,
                                  ALU.max).then_inc(ang_step, 1)
                at += 8

        ANG_STEPS = 1 + 16

        S_BANK, W_BANK = (6, 0, 6, 0), (2, 4, 2, 4)
        PUT_BANK = (2, 4, 6, 0)

        def turn_qk(pe, pr):
            pe.wait_ge(rot_step, 6 * (pr + 1))
            for m in range(4):
                last = pe.transpose(ps[:, 2 + pr, m * P:(m + 1) * P], qk[:, pr % 2, m * P:(m + 1) * P], ident[:, :])
            last.then_inc(qk_turned, 1)

        def scores(pe, pr):
            lo = S_BANK[pr]
            if pr < 2:
                pe.wait_ge(v_out, (8, 16)[pr])
            else:
                pe.wait_ge(s_step, 4 * (pr - 2) + 2)
            pe.wait_ge(qt_out, pr + 1)
            pe.wait_ge(kb_out, 4 * (pr + 1))
            for half in range(KD):
                for i in range(2):
                    last = pe.matmul(ps[i * ROWS:(i + 1) * ROWS, lo + half, :],
                                     q_t[:, pr, half, i * ROWS:(i + 1) * ROWS],
                                     k_blk[:, pr, half, i, :, :].rearrange("p h c -> p (h c)"),
                                     start=True, stop=True)
            last.then_inc(s_done, 1)

        def turn_p(pe, pr):
            lo = W_BANK[pr]
            pe.wait_ge(s_exp, pr + 1)
            pe.wait_ge(qt_out, lo)
            if pr >= 2:
                pe.wait_ge(x1_out, pr - 1)
            for m in range(8):
                last = pe.transpose(ps[:, lo + m // 4, (m % 4) * P:(m % 4 + 1) * P],
                                    s[:, pr % 2, 2 * m:2 * m + 2, :].rearrange("p h c -> p (h c)"), ident[:, :])
            last.then_inc(p_turned, 1)

        def values(pe, pr):
            pe.wait_ge(p_out, 2 * (pr + 1))
            for i in range(2):
                for m in range(8):
                    last = pe.matmul(ps[i * ROWS:(i + 1) * ROWS, W_BANK[pr], m * 32:(m + 1) * 32],
                                     p_t[:, pr % 2, m, i * ROWS:(i + 1) * ROWS],
                                     v_blk[:, 2 * pr + i, m, :, :].rearrange("p h d -> p (h d)"),
                                     start=True, stop=True)
            last.then_inc(o_done, 1)

        def turn_o(pe, pr):
            pe.wait_ge(o_out, pr + 1)
            for k in range(KD):
                last = pe.transpose(ps[:, W_BANK[pr] + 1, k * P:(k + 1) * P], o[:, pr % 2, k * P:(k + 1) * P], ident[:, :])
            last.then_inc(o_turned, 1)

        def project(pe, pr):
            pe.wait_ge(ot_out, pr + 1)
            for k in range(KD):
                last = pe.matmul(ps[:, W_BANK[pr], D:2 * D], o_t[:, pr % 2, k, :], wo[:, k, :],
                                 start=(k == 0), stop=(k == KD - 1))
            last.then_inc(wo_done, 1)

        def rotate(dve, pr):
            half = HEAD_DIM // 2
            wide = [P, 2 * HEADS, half]
            src = ps[:, 2 + pr, :].rearrange("p (h two i) -> p h two i", two=2, i=half)
            out = qk[:, pr % 2, :].rearrange("p (h two i) -> p h two i", two=2, i=half)
            cos = rope[:, 1, pr, :].unsqueeze(1).to_broadcast(wide)
            sin = rope[:, 0, pr, :].unsqueeze(1).to_broadcast(wide)
            r = [rot[:, m, :].rearrange("p (h i) -> p h i", i=half) for m in range(4)]
            dve.wait_ge(qk_done, pr + 1)
            if pr > 0:
                dve.wait_ge(rot_step, 6 * pr)
            for m, (a, table) in enumerate(((0, cos), (1, sin), (0, sin), (1, cos))):
                dve.tensor_tensor(r[m], src[:, :, a, :], table, ALU.mult).then_inc(rot_step, 1)
            dve.wait_ge(rot_step, 6 * pr + 4)
            dve.tensor_tensor(out[:, :, 0, :], r[0], r[1], ALU.subtract).then_inc(rot_step, 1)
            dve.tensor_tensor(out[:, :, 1, :], r[2], r[3], ALU.add).then_inc(rot_step, 1)

        def key_blocks(dve, pr):
            dve.wait_ge(qk_turned, pr + 1)
            for half in range(KD):
                for i in range(2):
                    at = (2 + half) * P + i * ROWS
                    dve.tensor_tensor(k_blk[:, pr, half, i, :, :],
                                      ps[:, 2 + pr, at:at + ROWS].unsqueeze(1).to_broadcast([P, 8, ROWS]),
                                      head_block[:, :].unsqueeze(2).to_broadcast([P, 8, ROWS]),
                                      ALU.mult).then_inc(kb_out, 1)

        def softmax_shift(dve, pr):
            lo = S_BANK[pr]
            at = 4 * pr
            sv, mx = s[:, pr % 2, :, :], s_col[:, pr % 2, 0, :]
            dve.wait_ge(s_done, pr + 1)
            if pr >= 2:
                dve.wait_ge(p_turned, pr - 1)
            for half in range(KD):
                dve.scalar_tensor_tensor(sv[:, half * 8:(half + 1) * 8, :],
                                         ps[:, lo + half, :].rearrange("p (h c) -> p h c", c=ROWS), 0.25,
                                         mask_sel[:, pr, :].unsqueeze(1).to_broadcast([P, 8, ROWS]),
                                         ALU.mult, ALU.add).then_inc(s_step, 1)
            dve.wait_ge(s_step, at + 2)
            dve.tensor_reduce(mx, sv, AX.X, ALU.max).then_inc(s_step, 1)
            dve.wait_ge(s_step, at + 3)
            dve.tensor_tensor(sv, sv, mx.unsqueeze(2).to_broadcast([P, HEADS, ROWS]), ALU.subtract).then_inc(s_step, 1)

        def softmax_sum(dve, pr):
            total, inv = (s_col[:, pr % 2, m, :] for m in (1, 2))
            dve.wait_ge(s_exp, pr + 1)
            dve.tensor_reduce(total, s[:, pr % 2, :, :], AX.X, ALU.add).then_inc(sum_step, 1)
            dve.wait_ge(sum_step, 2 * pr + 1)
            dve.reciprocal(inv, total).then_inc(sum_step, 1)

        def divide(dve, pr):
            dve.wait_ge(o_done, pr + 1)
            dve.wait_ge(sum_step, 2 * (pr + 1))
            dve.tensor_tensor(o[:, pr % 2, :].rearrange("p (h d) -> p h d", d=HEAD_DIM),
                              ps[:, W_BANK[pr], 0:D].rearrange("p (h d) -> p h d", d=HEAD_DIM),
                              s_col[:, pr % 2, 2, :].unsqueeze(2).to_broadcast([P, HEADS, HEAD_DIM]),
                              ALU.mult).then_inc(o_out, 1)

        def add_selected(dve, pr):
            dve.wait_ge(wo_done, pr + 1)
            dve.tensor_tensor(x1[:, pr, :], ps[:, W_BANK[pr], D:2 * D], xs[:, pr, 0:D], ALU.add).then_inc(x1_out, 1)

        with nc.Block() as block:
            @block.gpsimd
            def _(pool):
                pool.memset(v_blk[:, :, :, :, :], 0.0).then_inc(v_zeroed, 1)

            @block.sync
            def _(sp):
                if out is not None:
                    for b in range(BATCH):
                        sp.wait_ge(put_out, b + 1)
                        sp.dma_start(out[b].rearrange("(t p) d -> p t d", p=P), x[:, b]).then_inc(x_out, 16)
                    sp.wait_ge(x_out, 16 * BATCH)

            @block.tensor
            def _(pe):
                def turn_h(call, count):
                    pe.wait_ge(rms_step, count)
                    for k in range(KD):
                        for pr in range(PAIRS):
                            last = pe.transpose(ps[:, k, pr * P:(pr + 1) * P], h[:, pr, k * P:(k + 1) * P], ident[:, :])
                    last.then_inc(h_turned, 1)

                turn_h(0, RMS_STEPS)
                pe.wait_ge(h_out, 2)
                pe.wait_ge(weights_in, 16 * 9)
                for pr in range(PAIRS):
                    for k in range(KD):
                        last = pe.matmul(ps[:, 2 + pr, :], h_t[:, k, pr * P:(pr + 1) * P], wqkv[:, k, 0:2 * D],
                                         start=(k == 0), stop=(k == KD - 1))
                    last.then_inc(qk_done, 1)
                for pr in range(PAIRS):
                    for k in range(KD):
                        last = pe.matmul(ps[:, (6, 7, 0, 1)[pr], 0:D], h_t[:, k, pr * P:(pr + 1) * P],
                                         wqkv[:, k, 2 * D:QKV], start=(k == 0), stop=(k == KD - 1))
                    last.then_inc(v_done, 1)
                for piece, pr in ((turn_qk, 0), (scores, 0), (turn_qk, 1), (scores, 1), (turn_qk, 2), (turn_p, 0),
                                  (scores, 2), (values, 0), (turn_qk, 3), (turn_o, 0), (scores, 3), (project, 0),
                                  (turn_p, 1), (values, 1), (turn_p, 2), (turn_o, 1), (values, 2), (project, 1),
                                  (turn_p, 3), (turn_o, 2), (values, 3), (project, 2), (turn_o, 3), (project, 3)):
                    piece(pe, pr)
                turn_h(1, 2 * RMS_STEPS)
                pe.wait_ge(h_out, 4)
                for f in range(FFN // P):
                    if f >= 4:
                        pe.wait_ge(gel_out, f - 3)
                    for k in range(KD):
                        last = pe.matmul(ps[:, 2 + f % 4, :], w1[:, k, f * P:(f + 1) * P], h_t[:, k, :],
                                         start=(k == 0), stop=(k == KD - 1))
                    last.then_inc(up_done, 1)
                for pr in range(PAIRS):
                    for f in range(FFN // P):
                        if pr == 0:
                            pe.wait_ge(gel_out, f + 1)
                        last = pe.matmul(ps[:, (6, 7, 0, 1)[pr], 0:D], gel[:, f, pr * P:(pr + 1) * P],
                                         w2[:, f, :], start=(f == 0), stop=(f == FFN // P - 1))
                    last.then_inc(down_done, 1)
                for b in range(BATCH):
                    pr, i = b // 2, b % 2
                    pe.wait_ge(proc_step, 4 * max(pr + 1, 2 if b == 2 else 0))
                    if b == 3:
                        pe.wait_ge(proc_step, 4 * PAIRS)
                    if b >= 4:
                        pe.wait_ge(put_out, b - 3)
                    rows = slice(i * ROWS, (i + 1) * ROWS)
                    for t in range(TILES):
                        out = ps[:, PUT_BANK[b % 4] + t // 2, (t % 2) * D:(t % 2 + 1) * D]
                        pe.matmul(out, slot_hot[rows, pr, t, :], proc_hi[rows, pr, :], start=True, stop=False)
                        last = pe.matmul(out, slot_hot[rows, pr, t, :], proc_lo[rows, pr, :], start=False, stop=True)
                    last.then_inc(put_done, 1)

            @block.vector
            def _(dve):
                dve.wait_ge(weights_in, 16 * 9)
                rmsnorm(dve, 0, xs[:, :, 0:D], ln1)
                angles(dve)
                for b in range(BATCH):
                    pr, i = b // 2, b % 2
                    dve.wait_ge(v_done, pr + 1)
                    if b == 0:
                        dve.wait_ge(v_zeroed, 1)
                    own = ps[i * ROWS:(i + 1) * ROWS, (6, 7, 0, 1)[pr], 0:D].rearrange("p (m h d) -> p m h d", m=8, h=2)
                    for c in range(2):
                        dve.tensor_copy(v_blk[c * ROWS:(c + 1) * ROWS, b, :, c, :], own[:, :, c, :]).then_inc(v_out, 1)
                dve.wait_ge(sin_done, 1)
                for piece, pr in ((rotate, 0), (key_blocks, 0), (rotate, 1), (key_blocks, 1), (softmax_shift, 0),
                                  (rotate, 2), (softmax_shift, 1), (key_blocks, 2), (softmax_sum, 0), (rotate, 3),
                                  (divide, 0), (key_blocks, 3), (softmax_sum, 1), (softmax_shift, 2),
                                  (add_selected, 0), (divide, 1), (softmax_shift, 3), (softmax_sum, 2),
                                  (add_selected, 1), (divide, 2), (softmax_sum, 3), (add_selected, 2),
                                  (divide, 3), (add_selected, 3)):
                    piece(dve, pr)
                dve.wait_ge(x1_out, PAIRS)
                rmsnorm(dve, 1, x1[:, :, :], ln2)
                for b in range(BATCH):
                    for t in range(TILES):
                        xt = x[:, b, t, :]
                        dve.scalar_tensor_tensor(xt, y[:, b, t, 0:D], stay[:, t, b:b + 1], xt,
                                                 ALU.mult, ALU.add).then_inc(passed, 1)
                for pr in range(PAIRS):
                    dve.wait_ge(down_done, pr + 1)
                    dve.tensor_tensor(proc[:, pr, :], ps[:, (6, 7, 0, 1)[pr], 0:D], x1[:, pr, :],
                                      ALU.add).then_inc(proc_step, 1)
                    dve.wait_ge(proc_step, 4 * pr + 1)
                    dve.tensor_scalar(proc[:, pr, :], proc[:, pr, :], xs[:, pr, D:D + 1], None,
                                      ALU.mult).then_inc(proc_step, 1)
                    dve.wait_ge(proc_step, 4 * pr + 2)
                    dve.tensor_copy(proc_hi[:, pr, :], proc[:, pr, :]).then_inc(proc_step, 1)
                    dve.wait_ge(proc_step, 4 * pr + 3)
                    dve.tensor_tensor(proc_lo[:, pr, :], proc[:, pr, :], proc_hi[:, pr, :],
                                      ALU.subtract).then_inc(proc_step, 1)
                for b in range(BATCH):
                    dve.wait_ge(put_done, b + 1)
                    dve.wait_ge(passed, TILES * (b + 1))
                    two = PUT_BANK[b % 4]
                    dve.scalar_tensor_tensor(x[:, b, :, :].rearrange("p t d -> p (t d)"),
                                             ps[:, two:two + 2, :].rearrange("p a n -> p (a n)"), 0.5,
                                             x[:, b, :, :].rearrange("p t d -> p (t d)"),
                                             ALU.mult, ALU.add).then_inc(put_out, 1)

            @block.scalar
            def _(act):
                def h_copy(call):
                    act.wait_ge(h_turned, call + 1)
                    for k in range(KD):
                        act.activation(h_t[:, k, :], ps[:, k, :], ACT.Copy).then_inc(h_out, 1)

                def queries_copy(pr):
                    act.wait_ge(kb_out, 4 * (pr + 1))
                    act.activation(q_t[:, pr, :, :].rearrange("p k n -> p (k n)"), ps[:, 2 + pr, 0:2 * P],
                                   ACT.Copy).then_inc(qt_out, 1)

                def exponential(pr):
                    act.wait_ge(s_step, 4 * (pr + 1))
                    act.activation(s[:, pr % 2, :, :], s[:, pr % 2, :, :], ACT.Exp).then_inc(s_exp, 1)

                def p_copy(pr):
                    act.wait_ge(p_turned, pr + 1)
                    for m in range(2):
                        act.activation(p_t[:, pr % 2, 4 * m:4 * m + 4, :].rearrange("p m n -> p (m n)"),
                                       ps[:, W_BANK[pr] + m, :], ACT.Copy).then_inc(p_out, 1)

                def o_copy(pr):
                    act.wait_ge(o_turned, pr + 1)
                    act.activation(o_t[:, pr % 2, :, :].rearrange("p k n -> p (k n)"), ps[:, W_BANK[pr] + 1, 0:D],
                                   ACT.Copy).then_inc(ot_out, 1)

                h_copy(0)
                act.wait_ge(ang_step, ANG_STEPS)
                act.activation(rope[:, :, :, :].rearrange("p c r i -> p (c r i)"),
                               ang[:, 2:4, :].rearrange("p c n -> p (c n)"), ACT.Sin).then_inc(sin_done, 1)
                for piece, pr in ((queries_copy, 0), (queries_copy, 1), (exponential, 0), (queries_copy, 2),
                                  (p_copy, 0), (exponential, 1), (queries_copy, 3), (o_copy, 0), (p_copy, 1),
                                  (exponential, 2), (p_copy, 2), (o_copy, 1), (exponential, 3), (p_copy, 3),
                                  (o_copy, 2), (o_copy, 3)):
                    piece(pr)
                h_copy(1)
                for f in range(FFN // P):
                    act.wait_ge(up_done, f + 1)
                    act.activation(gel[:, f, :], ps[:, 2 + f % 4, :], ACT.Gelu_apprx_tanh).then_inc(gel_out, 1)


BF16 = mybir.dt.bfloat16
LATENT = 64
MLA_HEADS, MLA_DIM = 16, 64
MLA_PAIRS = MLA_HEADS // 2
BLOCKED = -1.0e30
M_SCALE, INV_SCALE = 64.0, 256.0
GROUP_HEADS = 4
LEAD = 8
RING = LEAD
SUM_SLOTS = 4
SUM_ROWS = P // MLA_HEADS
KEY_AT = (0, 512, 1024, 896)
KEY_COLS = sum(SEQ - t * P for t in range(TILES))
QUERY_AT = (512 + 384, 0, 512, 0)
QUERY_TILES = (3, 2, 0, 1)
PV_BANK = (7, 2)


def latent_attention_layer(nc, keep, x, ident, io):
    with ExitStack() as ctx:
        def sb(name, shape, dt=F32):
            return ctx.enter_context(nc.sbuf_tensor(f"mla_{name}", shape, dt))

        def sem(name):
            return keep.enter_context(nc.semaphore(f"mla_{name}"))

        ps = ctx.enter_context(nc.psum_tensor("mla_ps", [P, 8, 512], F32))
        a_hi = sb("a_hi", [P, KD, MLA_HEADS, LATENT], F16)
        a_lo = sb("a_lo", [P, KD, MLA_HEADS, LATENT], F16)
        b_hi = sb("b_hi", [P, MLA_PAIRS, D], F16)
        b_lo = sb("b_lo", [P, MLA_PAIRS, D], F16)
        down_hi = sb("down_hi", [P, KD, 2, LATENT], F16)
        down_lo = sb("down_lo", [P, KD, 2, LATENT], F16)
        ident_b = sb("ident_b", [P, P], BF16)
        block_q = sb("block_q", [P, P], BF16)
        block_k = sb("block_k", [P, P], BF16)
        spread = sb("spread", [P, MLA_HEADS, LATENT], F16)
        val_hi = sb("val_hi", [P, 2, TILES, P], F16)
        val_lo = sb("val_lo", [P, 2, TILES, P], F16)
        key_top = sb("key_top", [P, 2, SEQ], F16)
        q_lo = sb("q_lo", [P, RING, SEQ], F16)
        inv_hl = sb("inv_hl", [P, SEQ], F16)

        norm_const = sb("norm_const", [P, len(NORM_CONSTANTS), TILES])

        with ExitStack() as part:
            def tmp(name, shape, dt=F32):
                return part.enter_context(nc.sbuf_tensor(f"mla_{name}", shape, dt))

            def tsem(name):
                return keep.enter_context(nc.semaphore(f"mla_{name}"))

            wq = tmp("wq", [P, KD, MLA_HEADS * MLA_DIM])
            wk = tmp("wk", [LATENT, MLA_HEADS * MLA_DIM])
            wv = tmp("wv", [LATENT, MLA_HEADS * MLA_DIM])
            wout = tmp("wout", [P, MLA_PAIRS, D])
            down = tmp("down", [P, KD, LATENT])
            wq_t = tmp("wq_t", [P, MLA_PAIRS, D])
            wk_t = tmp("wk_t", [P, MLA_PAIRS, LATENT])
            wv_t = tmp("wv_t", [P, MLA_PAIRS, LATENT])
            spread_f = tmp("spread_f", [P, MLA_HEADS, LATENT])
            block_f = tmp("block_f", [P, 2, P])
            k_in, v_in, q_in = tsem("k_in"), tsem("v_in"), tsem("q_in")
            out_in, down_in = tsem("out_in"), tsem("down_in")
            made = tsem("made")
            turned = tsem("turned")
            turn_out = tsem("turn_out")
            folded = tsem("folded")
            split_head = tsem("split_head")
            split_tail = tsem("split_tail")
            const_done = tsem("const_done")
            zeroed = tsem("zeroed")

            def folded_a(m, i):
                return ps[:, 4 * i + m % 4, 0:KD * LATENT].rearrange("p (k c) -> p k c", k=KD)

            with nc.Block() as block:
                @block.sync
                def _(sp):
                    sp.dma_start(wk[:, :], io["Wk_up"].rearrange("c h n -> c (h n)")).then_inc(k_in, 16)
                    sp.dma_start(wv[:, :], io["Wv_up"].rearrange("c h n -> c (h n)")).then_inc(v_in, 16)
                    sp.dma_start(wq[:, :, :], io["Wq"].rearrange("(k p) h n -> p k (h n)", p=P)).then_inc(q_in, 16)
                    sp.dma_start(wout[:, :, :], io["Wout"].rearrange("(m h) n d -> (h n) m d", h=2)).then_inc(out_in, 16)
                    sp.dma_start(down[:, :, :], io["Wkv_down"].rearrange("(k p) c -> p k c", p=P)).then_inc(down_in, 16)

                @block.gpsimd
                def _(pool):
                    for i, value in enumerate(NORM_CONSTANTS):
                        pool.memset(norm_const[:, i, :], value)
                    pool.memset(spread_f[:, :, :], 0.0).then_inc(made, 1)
                    pool.memset(block_f[:, :, :], 0.0).then_inc(made, 1)
                    for n, base in enumerate((0, -32)):
                        pool.wait_ge(made, 2 + n)
                        pool.affine_select(out=spread_f[:, :, :], in_=spread_f[:, :, :], compare_op=ALU.not_equal,
                                           fill=1.0 / INV_SCALE, base=base, pattern=[[-1, MLA_HEADS], [0, LATENT]],
                                           channel_multiplier=1).then_inc(made, 1)
                    pool.affine_select(out=block_f[:, 0, :], in_=block_f[:, 0, :], compare_op=ALU.is_ge, fill=BLOCKED,
                                       base=0, pattern=[[-1, P]], channel_multiplier=1).then_inc(made, 1)
                    pool.affine_select(out=block_f[:, 1, :], in_=block_f[:, 1, :], compare_op=ALU.is_ge, fill=BLOCKED,
                                       base=0, pattern=[[1, P]], channel_multiplier=-1).then_inc(made, 1)

                @block.tensor
                def _(pe):
                    for i, (w, there) in enumerate(((wk, k_in), (wv, v_in))):
                        pe.wait_ge(there, 16)
                        for m in range(MLA_PAIRS):
                            last = pe.transpose(ps[:, 4 + i, m * LATENT:(m + 1) * LATENT], w[:, m * P:(m + 1) * P],
                                                ident[0:LATENT, 0:LATENT])
                        last.then_inc(turned, 1)
                    pe.wait_ge(q_in, 16)
                    for m in range(MLA_PAIRS):
                        for k in range(KD):
                            last = pe.transpose(ps[:, m // 2, (m % 2) * D + k * P:(m % 2) * D + (k + 1) * P],
                                                wq[:, k, m * P:(m + 1) * P], ident[:, :])
                        if m % 2 == 1:
                            last.then_inc(turned, 1)
                    pe.wait_ge(out_in, 16)
                    pe.wait_ge(turn_out, 6)
                    for m in range(MLA_PAIRS):
                        if m >= 4:
                            pe.wait_ge(split_tail, m - 3)
                        for i in range(2):
                            bank = 4 * i + m % 4
                            rows = slice(i * MLA_DIM, (i + 1) * MLA_DIM)
                            for k in range(KD):
                                last = pe.matmul(ps[:, bank, k * LATENT:(k + 1) * LATENT],
                                                 wq_t[rows, m, k * P:(k + 1) * P], wk_t[rows, m, :],
                                                 start=True, stop=True)
                            last = pe.matmul(ps[i * LATENT:(i + 1) * LATENT, bank, D:2 * D],
                                             wv_t[rows, m, :], wout[rows, m, :], start=True, stop=True)
                        last.then_inc(folded, 1)

                @block.vector
                def _(dve):
                    dve.wait_ge(made, 6)
                    dve.tensor_copy(spread[:, :, :], spread_f[:, :, :])
                    dve.tensor_copy(block_q[:, :], block_f[:, 0, :])
                    dve.tensor_copy(block_k[:, :], block_f[:, 1, :])
                    dve.tensor_copy(ident_b[:, :], ident[:, :])
                    for slot in range(2):
                        dve.memset(val_hi[:, slot, :, LATENT:P], 1.0)
                        dve.memset(val_lo[:, slot, :, LATENT:P], 0.0)
                    dve.memset(inv_hl[:, :], 0.0)
                    dve.memset(q_lo[LATENT:P, :, :], 0.0)
                    dve.memset(key_top[LATENT:P, :, :], 0.0).then_inc(zeroed, 1)
                    dve.wait_ge(zeroed, 1)
                    dve.memset(key_top[LATENT:LATENT + 1, :, :], M_SCALE)
                    for i, w in enumerate((wk_t, wv_t)):
                        dve.wait_ge(turned, i + 1)
                        dve.tensor_copy(w[:, :, :].rearrange("p m c -> p (m c)"), ps[:, 4 + i, :]).then_inc(turn_out, 1)
                    for n in range(4):
                        dve.wait_ge(turned, n + 3)
                        dve.tensor_copy(wq_t[:, 2 * n:2 * n + 2, :].rearrange("p m d -> p (m d)"),
                                        ps[:, n, :]).then_inc(turn_out, 1)
                    dve.wait_ge(down_in, 16)
                    wide = [P, KD, 2, LATENT]
                    src = down[:, :, :].unsqueeze(2).to_broadcast(wide)
                    dve.tensor_scalar(down_hi[:, :, :, :], src, WS, None, ALU.mult).then_inc(const_done, 1)
                    dve.wait_ge(const_done, 1)
                    for k in range(KD):
                        dve.scalar_tensor_tensor(down_lo[:, k, :, :], down[:, k, :].unsqueeze(1).to_broadcast([P, 2, LATENT]),
                                                 WS, down_hi[:, k, :, :], ALU.mult, ALU.subtract)
                    for m in range(MLA_PAIRS):
                        dve.wait_ge(split_head, m + 1)
                        for i in range(2):
                            bank, rows = 4 * i + m % 4, slice(i * LATENT, (i + 1) * LATENT)
                            dve.scalar_tensor_tensor(b_lo[rows, m, :], ps[rows, bank, D:2 * D], WS, b_hi[rows, m, :],
                                                     ALU.mult, ALU.subtract)
                            last = dve.scalar_tensor_tensor(a_lo[:, :, 2 * m + i, :], folded_a(m, i), WS,
                                                            a_hi[:, :, 2 * m + i, :], ALU.mult, ALU.subtract)
                        last.then_inc(split_tail, 1)

                @block.scalar
                def _(act):
                    for m in range(MLA_PAIRS):
                        act.wait_ge(folded, m + 1)
                        for i in range(2):
                            bank, rows = 4 * i + m % 4, slice(i * LATENT, (i + 1) * LATENT)
                            act.activation(b_hi[rows, m, :], ps[rows, bank, D:2 * D], ACT.Copy, scale=WS)
                            last = act.activation(a_hi[:, :, 2 * m + i, :], folded_a(m, i), ACT.Copy, scale=WS)
                        last.then_inc(split_head, 1)

        y = sb("y", [P, TILES, D])
        y_hi = sb("y_hi", [P, 2, KD, SEQ], F16)
        y_lo = sb("y_lo", [P, 2, KD, SEQ], F16)
        stats = sb("stats", [P, TILES, 6])
        ln_col = sb("ln_col", [P, 4, TILES])
        var = sb("var", [P, TILES])
        minus_half = sb("minus_half", [P, TILES])
        rstd = sb("rstd", [P, TILES])
        newton = sb("newton", [P, TILES])
        lat = sb("lat", [P, SEQ])
        key_hl = sb("key_hl", [P, 2, SEQ], F16)
        q_hi = sb("q_hi", [P, RING, SEQ], F16)
        m_col = sb("m_col", [P, 2, TILES, GROUP_HEADS])
        m_neg = sb("m_neg", [GROUP_HEADS, 2, SEQ], F16)
        p_full = sb("p_full", [P, 2, KEY_COLS])
        p_hi = sb("p_hi", [P, 2, KEY_COLS], F16)
        p_lo = sb("p_lo", [P, 2, KEY_COLS], F16)
        o = sb("o", [P, 2, MLA_PAIRS, SEQ])
        o_hi = sb("o_hi", [P, MLA_PAIRS, SEQ], F16)
        o_lo = sb("o_lo", [P, MLA_PAIRS, SEQ], F16)
        sum_row = sb("sum_row", [1, SUM_SLOTS, SEQ])
        sums = sb("sums", [P, 2, SEQ // SUM_ROWS])
        inv = sb("inv", [P, SEQ // SUM_ROWS])
        inv_part = sb("inv_part", [P, 2, SEQ // SUM_ROWS], F16)

        norm_step = sem("norm_step")
        y_turned = sem("y_turned")
        y_split = sem("y_split")
        lat_done = sem("lat_done")
        lat_step = sem("lat_step")
        lat_turned = sem("lat_turned")
        val_out = sem("val_out")
        q_done = sem("q_done")
        q_head = sem("q_head")
        q_twin = sem("q_twin")
        q_tail = sem("q_tail")
        s_done = sem("s_done")
        s_rest = sem("s_rest")
        s_max = sem("s_max")
        m_turned = sem("m_turned")
        m_out = sem("m_out")
        m_put = [sem(f"m_put{i}") for i in range(2)]
        st_done = sem("st_done")
        exp_done = sem("exp_done")
        p_tail = sem("p_tail")
        pv_done = sem("pv_done")
        pv_out = sem("pv_out")
        sum_put = [sem(f"sum_put{i}") for i in range(SUM_SLOTS)]
        inv_step = sem("inv_step")
        inv_put = sem("inv_put")
        spread_done = sem("spread_done")
        scaled = sem("scaled")
        o_head = sem("o_head")
        o_tail = sem("o_tail")
        out_done = sem("out_done")
        x_added = sem("x_added")

        H = MLA_HEADS
        NORM_AT, GUESS_AT, APPLY_AT = 0, 2, 4
        TURN_AT, LATENT_AT, VALUE_AT = (5, 7), 8, 9
        INVERT_AT, SPREAD_AT, OUTPUT_AT = 1, 3, H - TILES - 1

        def exists(b):
            return not isinstance(b, int) or 0 <= b < BATCH

        def head_of(b, h):
            return (b + h // H, h % H, b * H + h)

        def group_of(b, h):
            if (h + LEAD - 3) % GROUP_HEADS != GROUP_HEADS - 1:
                return None
            last_b, last_h, _ = head_of(b, h + LEAD - 3)
            return (last_b, last_h // GROUP_HEADS) if exists(last_b) else None

        GROUPS = H // GROUP_HEADS

        def stream(engine, step):
            for b in (-1, 0):
                for h in range(H):
                    step(engine, b, b % 2, h)
            with engine.Fori(0, (BATCH - 2) // 2) as two:
                for i in range(2):
                    for h in range(H):
                        step(engine, 2 * two + (1 + i), (1 + i) % 2, h)
            for b in (BATCH - 1, BATCH):
                for h in range(H):
                    step(engine, b, b % 2, h)

        flat = ps[:, :, :].rearrange("p a n -> p (a n)")

        def query_scores(pe, slot, h, t):
            out = flat[:, QUERY_AT[t]:QUERY_AT[t] + (t + 1) * P]
            pe.matmul(out, q_hi[:, h % RING, t * P:(t + 1) * P], key_hl[:, slot, 0:(t + 1) * P], start=True, stop=False)
            return pe.matmul(out[:, t * P:(t + 1) * P], ident_b[:, :], block_q[:, :], start=False, stop=True)

        def queries_read(pe, b, h):
            n = b * H + h + LEAD + h % 2
            if not isinstance(n, int):
                pe.wait_ge(q_tail, n)
            elif n > 0:
                pe.wait_ge(q_tail, min(n, BATCH * H))

        def tensor_step(pe, b, slot, h):
            before, after, n = b - 1, b + 1, b * H + h
            own_bank, other_bank = PV_BANK[h % 2], PV_BANK[(h + 1) % 2]

            hb, hh, hn = head_of(b, h + 1)
            if exists(hb):
                if not isinstance(hn, int) or hn > 0:
                    pe.wait_ge(exp_done, 2 * hn)
                if hh % GROUP_HEADS == 0:
                    g = hh // GROUP_HEADS
                    pe.wait_ge(q_tail, hn + GROUP_HEADS)
                    pe.wait_ge(m_put[g % 2], 16 * (hb * (GROUPS // 2) + g // 2 + 1))
                for t in range(TILES):
                    at = 3 * 512 + KEY_AT[t]
                    cols, toks = SEQ - t * P, slice(t * P, (t + 1) * P)
                    pe.matmul(flat[:, at:at + cols], key_hl[:, (slot + (h + 1) // H) % 2, toks],
                              q_hi[:, hh % RING, t * P:], start=True, stop=False)
                    pe.matmul(flat[:, at:at + cols], key_top[:, (slot + (h + 1) // H) % 2, toks],
                              q_lo[:, hh % RING, t * P:], start=False, stop=False)
                    last = pe.matmul(flat[:, at:at + P], ident_b[:, :], block_k[:, :], start=False, stop=True)
                last.then_inc(st_done, 1)

            if exists(before) and OUTPUT_AT <= h < OUTPUT_AT + TILES:
                t = h - OUTPUT_AT
                if exists(b):
                    pe.wait_ge(pv_out, 2 * n)
                pe.wait_ge(o_tail, MLA_PAIRS * b)
                if t > 1:
                    pe.wait_ge(x_added, TILES * before + t - 1)
                toks = slice(t * P, (t + 1) * P)
                for m in range(MLA_PAIRS):
                    pe.matmul(ps[:, other_bank, 0:D], o_hi[:, m, toks], b_hi[:, m, :], start=(m == 0), stop=False)
                    pe.matmul(ps[:, other_bank, 0:D], o_hi[:, m, toks], b_lo[:, m, :], start=False, stop=False)
                    last = pe.matmul(ps[:, other_bank, 0:D], o_lo[:, m, toks], b_hi[:, m, :], start=False,
                                     stop=(m == MLA_PAIRS - 1))
                last.then_inc(out_done, 1)

            if exists(before) and SPREAD_AT <= h < SPREAD_AT + MLA_PAIRS:
                m = h - SPREAD_AT
                if exists(b):
                    pe.wait_ge(pv_out, 2 * n)
                pe.wait_ge(inv_put, 32 * b)
                if m > 1:
                    pe.wait_ge(scaled, MLA_PAIRS * before + m - 1)
                pe.matmul(ps[:, other_bank, :], spread[:, 2 * m:2 * m + 2, :].rearrange("p a c -> p (a c)"), inv_hl[:, :],
                          start=True, stop=True).then_inc(spread_done, 1)
            group = group_of(b, h)
            if group is not None:
                gb, g = group
                pe.wait_ge(s_max, TILES * (gb * H + (g + 1) * GROUP_HEADS))
                queries_read(pe, b, h)
                for t in range(TILES):
                    last = pe.transpose(ps[0:GROUP_HEADS, 6, t * P:(t + 1) * P], m_col[:, g % 2, t, :], ident[:, :])
                last.then_inc(m_turned, 1)

            if exists(after) and h in (*TURN_AT, LATENT_AT, VALUE_AT):
                queries_read(pe, b, h)
            if exists(after) and h in TURN_AT:
                k = TURN_AT.index(h)
                if k == 0:
                    pe.wait_ge(norm_step, NORM_STEPS * (after + 1))
                else:
                    pe.wait_ge(y_split, 2 * KD * after + 2 * k)
                for t in range(TILES):
                    last = pe.transpose(ps[:, 6, t * P:(t + 1) * P], y[:, t, k * P:(k + 1) * P], ident[:, :])
                last.then_inc(y_turned, 1)
            if exists(after) and h == LATENT_AT:
                pe.wait_ge(y_split, 2 * KD * (after + 1))
                for k in range(KD):
                    last = split_matmul(pe, ps[:, 6, :], down_hi[:, k, :, :].rearrange("p a c -> p (a c)"),
                                        down_lo[:, k, :, :].rearrange("p a c -> p (a c)"),
                                        y_hi[:, 1 - slot, k, :], y_lo[:, 1 - slot, k, :], k == 0, k == KD - 1)
                last.then_inc(lat_done, 1)
            if exists(after) and h == VALUE_AT:
                pe.wait_ge(lat_step, 4 * after + 1)
                for t in range(TILES):
                    last = pe.transpose(ps[:, 6, t * P:(t + 1) * P], lat[:, t * P:(t + 1) * P], ident[:, :])
                last.then_inc(lat_turned, 1)

            if exists(b):
                pe.wait_ge(p_tail, n + 1)
                if h == 0:
                    pe.wait_ge(val_out, 2 * (b + 1))
                if not isinstance(n, int) or n > 1:
                    pe.wait_ge(pv_out, 2 * (n - 1))
                if exists(before) and SPREAD_AT < h <= SPREAD_AT + MLA_PAIRS:
                    pe.wait_ge(scaled, MLA_PAIRS * before + h - SPREAD_AT)
                if exists(before) and OUTPUT_AT < h <= OUTPUT_AT + TILES:
                    pe.wait_ge(x_added, TILES * before + h - OUTPUT_AT)
                for t in range(TILES):
                    out = ps[:, own_bank, t * P:]
                    cols = slice(KEY_AT[t], KEY_AT[t] + SEQ - t * P)
                    hi, lo = p_hi[:, h % 2, cols], p_lo[:, h % 2, cols]
                    pe.matmul(out, val_hi[:, slot, t, :], hi, start=(t == 0), stop=False)
                    pe.matmul(out, val_hi[:, slot, t, :], lo, start=False, stop=False)
                    last = pe.matmul(out, val_lo[:, slot, t, :], hi, start=False, stop=(t == TILES - 1))
                last.then_inc(pv_done, 1)

            hb, hh, hn = head_of(b, h + LEAD - 2)
            if exists(hb):
                pe.wait_ge(s_max, TILES * hn + 1)
                query_scores(pe, (slot + (h + LEAD - 2) // H) % 2, hh, QUERY_TILES[-1]).then_inc(s_rest, 1)

            hb, hh, hn = head_of(b, h + LEAD)
            qslot = (slot + (h + LEAD) // H) % 2
            if exists(hb) and h % 2 == 0:
                if not isinstance(hn, int) or hn > 0:
                    pe.wait_ge(q_tail, hn)
                if hh == 0:
                    pe.wait_ge(y_split, 2 * KD * (hb + 1))
                if exists(after) and h == TURN_AT[0] + 1:
                    pe.wait_ge(y_split, 2 * KD * after + 2)
                if exists(after) and h == LATENT_AT:
                    pe.wait_ge(lat_step, 4 * after + 1)
                if exists(after) and h == VALUE_AT + 1:
                    pe.wait_ge(val_out, 2 * (after + 1))
                if group is not None:
                    pe.wait_ge(m_out, gb * GROUPS + g + 1)
                for k in range(KD):
                    last = split_matmul(pe, ps[:, 6, :], a_hi[:, k, hh:hh + 2, :].rearrange("p a c -> p (a c)"),
                                        a_lo[:, k, hh:hh + 2, :].rearrange("p a c -> p (a c)"),
                                        y_hi[:, qslot, k, :], y_lo[:, qslot, k, :], k == 0, k == KD - 1)
                last.then_inc(q_done, 1)

            hb, hh, hn = head_of(b, h + LEAD - 1)
            if exists(hb):
                pe.wait_ge(q_twin, hn + 1)
                if not isinstance(hn, int) or hn > 0:
                    pe.wait_ge(s_max, TILES * hn)
                if hh == 0:
                    pe.wait_ge(lat_step, 4 * (hb + 1))
                for t in QUERY_TILES[:-1]:
                    last = query_scores(pe, (slot + (h + LEAD - 1) // H) % 2, hh, t)
                last.then_inc(s_done, 1)

        def query_maxima(dve, h, t):
            j, g = h % GROUP_HEADS, h // GROUP_HEADS
            dve.tensor_reduce(m_col[:, g % 2, t, j:j + 1], flat[:, QUERY_AT[t]:QUERY_AT[t] + (t + 1) * P],
                              AX.X, ALU.max).then_inc(s_max, 1)

        def vector_step(dve, b, slot, h):
            before, after = b - 1, b + 1
            other_bank = PV_BANK[(h + 1) % 2]

            hb, hh, hn = head_of(b, h + LEAD - 2)
            if exists(hb):
                dve.wait_ge(s_done, hn + 1)
                for t in QUERY_TILES[:-1]:
                    query_maxima(dve, hh, t)

            if exists(before) and SPREAD_AT <= h < SPREAD_AT + MLA_PAIRS:
                m = h - SPREAD_AT
                dve.wait_ge(spread_done, MLA_PAIRS * before + m + 1)
                dve.tensor_tensor(o[:, 1 - slot, m, :], o[:, 1 - slot, m, :], ps[:, other_bank, :],
                                  ALU.mult).then_inc(scaled, 1)
            if exists(before) and OUTPUT_AT <= h < OUTPUT_AT + TILES:
                t = h - OUTPUT_AT
                dve.wait_ge(out_done, TILES * before + t + 1)
                xt = x[:, before, t, :]
                dve.scalar_tensor_tensor(xt, ps[:, other_bank, 0:D], 1.0 / WS, xt, ALU.mult,
                                         ALU.add).then_inc(x_added, 1)

            group = group_of(b, h)
            if group is not None:
                gb, g = group
                dve.wait_ge(m_turned, gb * GROUPS + g + 1)
                dve.tensor_scalar(m_neg[:, g % 2, :], ps[0:GROUP_HEADS, 6, :], -1.0 / M_SCALE, None,
                                  ALU.mult).then_inc(m_out, 1)

            if exists(after) and h == NORM_AT:
                layernorm_stats(dve, norm_step, x[:, after, :, :], stats)
            if exists(after) and h == GUESS_AT:
                rsqrt_start(dve, norm_step, NORM_STEPS * after + TILES + VARIANCE_STEPS, var[:, :], rstd[:, :])
            if exists(after) and h == APPLY_AT:
                layernorm_apply(dve, norm_step, NORM_STEPS * (after + 1) - TILES, x[:, after, :, :], y, ln_col, rstd[:, :])
            if exists(before) and h == INVERT_AT:
                for i in range(SUM_SLOTS):
                    dve.wait_ge(sum_put[i], 16 * (H // SUM_SLOTS) * b)
                dve.reciprocal(inv[:, :], sums[:, 1 - slot, :]).then_inc(inv_step, 1)
                dve.wait_ge(inv_step, 3 * before + 1)
                dve.tensor_scalar(inv_part[:, 0, :], inv[:, :], INV_SCALE, None, ALU.mult).then_inc(inv_step, 1)
                dve.wait_ge(inv_step, 3 * before + 2)
                dve.scalar_tensor_tensor(inv_part[:, 1, :], inv[:, :], INV_SCALE, inv_part[:, 0, :],
                                         ALU.mult, ALU.subtract).then_inc(inv_step, 1)

            if exists(after) and h in TURN_AT:
                k = TURN_AT.index(h)
                dve.wait_ge(y_split, 2 * (KD * after + k) + 1)
                dve.tensor_tensor(y_lo[:, 1 - slot, k, :], ps[:, 6, :], y_hi[:, 1 - slot, k, :],
                                  ALU.subtract).then_inc(y_split, 1)
            if exists(after) and h == LATENT_AT:
                dve.wait_ge(lat_done, after + 1)
                dve.tensor_scalar(lat[:, :], ps[:, 6, :], 1.0 / WS, None, ALU.mult).then_inc(lat_step, 1)
                dve.wait_ge(lat_step, 4 * after + 1)
                dve.tensor_copy(key_hl[:, 1 - slot, :], lat[:, :]).then_inc(lat_step, 1)
                dve.tensor_copy(key_top[0:LATENT, 1 - slot, :], lat[0:LATENT, :]).then_inc(lat_step, 1)
                dve.wait_ge(lat_step, 4 * after + 2)
                tails = slice(LATENT, P)
                dve.tensor_tensor(key_hl[tails, 1 - slot, :], lat[tails, :], key_hl[tails, 1 - slot, :],
                                  ALU.subtract).then_inc(lat_step, 1)
            if exists(after) and h == VALUE_AT:
                dve.wait_ge(lat_turned, after + 1)
                src = ps[:, 6, :].rearrange("p (t c) -> p t c", t=TILES)[:, :, 0:LATENT]
                dve.tensor_copy(val_hi[:, 1 - slot, :, 0:LATENT], src).then_inc(val_out, 1)
                dve.wait_ge(val_out, 2 * after + 1)
                dve.tensor_tensor(val_lo[:, 1 - slot, :, 0:LATENT], src, val_hi[:, 1 - slot, :, 0:LATENT],
                                  ALU.subtract).then_inc(val_out, 1)

            hb, hh, hn = head_of(b, h + LEAD - 2)
            if exists(hb):
                dve.wait_ge(s_rest, hn + 1)
                query_maxima(dve, hh, QUERY_TILES[-1])

            hb, hh, hn = head_of(b, h + 1)
            if exists(hb):
                dve.wait_ge(exp_done, 2 * (hn + 1))
                dve.tensor_tensor(p_lo[:, hh % 2, :], p_full[:, hh % 2, :], p_hi[:, hh % 2, :],
                                  ALU.subtract).then_inc(p_tail, 1)

            hb, hh, hn = head_of(b, h + LEAD)
            if exists(hb) and h % 2 == 0:
                for i in range(2):
                    ring = (hh + i) % RING
                    own = slice(i * LATENT, (i + 1) * LATENT)
                    dve.wait_ge(q_head, hn + i + 1)
                    dve.tensor_copy(q_hi[LATENT:P, ring, :], q_hi[0:LATENT, ring, :]).then_inc(q_twin, 1)
                    if i == 1:
                        dve.wait_ge(q_twin, hn + i + 1)
                    dve.scalar_tensor_tensor(q_lo[0:LATENT, ring, :], ps[own, 6, :], 1.0 / WS, q_hi[own, ring, :],
                                             ALU.mult, ALU.subtract).then_inc(q_tail, 1)

        def scalar_step(act, b, slot, h):
            before, after, n, own_bank = b - 1, b + 1, b * H + h, PV_BANK[h % 2]
            hb, hh, hn = head_of(b, h + 1)
            if exists(hb):
                act.wait_ge(st_done, hn + 1)
                for out in (p_full, p_hi):
                    act.activation(out[:, hh % 2, :], flat[:, 3 * 512:3 * 512 + KEY_COLS], ACT.Exp,
                                   scale=float(MLA_DIM) ** -0.5).then_inc(exp_done, 1)
            if exists(after) and h in TURN_AT:
                k = TURN_AT.index(h)
                act.wait_ge(y_turned, KD * after + k + 1)
                act.activation(y_hi[:, 1 - slot, k, :], ps[:, 6, :], ACT.Copy).then_inc(y_split, 1)
            if exists(before) and SPREAD_AT <= h < SPREAD_AT + MLA_PAIRS:
                m = h - SPREAD_AT
                act.wait_ge(scaled, MLA_PAIRS * before + m + 1)
                act.activation(o_hi[:, m, :], o[:, 1 - slot, m, :], ACT.Copy).then_inc(o_head, 1)
            if exists(b):
                i = h % SUM_SLOTS
                if not isinstance(b, int) or b > 0 or h >= SUM_SLOTS:
                    act.wait_ge(sum_put[i], 16 * (b * (H // SUM_SLOTS) + h // SUM_SLOTS))
                act.wait_ge(pv_done, n + 1)
                rows = slice((h % 2) * LATENT, (h % 2 + 1) * LATENT)
                act.activation(sum_row[:, i, :], ps[LATENT:LATENT + 1, own_bank, :], ACT.Copy).then_inc(pv_out, 1)
                act.activation(o[rows, slot, h // 2, :], ps[0:LATENT, own_bank, :], ACT.Copy).then_inc(pv_out, 1)
            hb, hh, hn = head_of(b, h + LEAD)
            if exists(hb) and h % 2 == 0:
                act.wait_ge(q_done, hb * MLA_PAIRS + hh // 2 + 1)
                for i in range(2):
                    act.activation(q_hi[0:LATENT, (hh + i) % RING, :], ps[i * LATENT:(i + 1) * LATENT, 6, :], ACT.Copy,
                                   scale=1.0 / WS).then_inc(q_head, 1)

        def pool_step(pool, b, slot, h):
            before, after = b - 1, b + 1
            if exists(after) and h == NORM_AT:
                pool_variance(pool, norm_step, NORM_STEPS * after + TILES, stats, ln_col, norm_const,
                              var[:, :], minus_half[:, :])
            if exists(after) and h == GUESS_AT:
                pool_newton(pool, norm_step, NORM_STEPS * after + TILES + VARIANCE_STEPS + 2, norm_const,
                            minus_half[:, :], rstd[:, :], newton[:, :])
            if exists(before) and SPREAD_AT <= h < SPREAD_AT + MLA_PAIRS:
                m = h - SPREAD_AT
                pool.wait_ge(o_head, MLA_PAIRS * before + m + 1)
                pool.tensor_tensor(o_lo[:, m, :], o[:, 1 - slot, m, :], o_hi[:, m, :], ALU.subtract).then_inc(o_tail, 1)

        def dma_step(sp, b, slot, h):
            group = group_of(b, h)
            if group is not None:
                gb, g = group
                at = (g * GROUP_HEADS) % RING
                sp.wait_ge(m_out, gb * GROUPS + g + 1)
                sp.dma_start(q_lo[LATENT:LATENT + 1, at:at + GROUP_HEADS, :], m_neg[:, g % 2, :]).then_inc(m_put[g % 2], 16)
            if exists(b):
                i = h % SUM_SLOTS
                sp.wait_ge(pv_out, 2 * (b * H + h) + 2)
                sp.dma_start(sums[h * SUM_ROWS:(h + 1) * SUM_ROWS, slot, :], sum_row[:, i, :]).then_inc(sum_put[i], 16)
            if exists(b - 1) and h == INVERT_AT:
                sp.wait_ge(inv_step, 3 * b)
                for i in range(2):
                    sp.dma_start(inv_hl[32 * i:32 * i + H, :], inv_part[:, i, :]).then_inc(inv_put, 16)

        with nc.Block() as block:
            @block.tensor
            def _(pe):
                stream(pe, tensor_step)

            @block.vector
            def _(dve):
                stream(dve, vector_step)

            @block.scalar
            def _(act):
                stream(act, scalar_step)

            @block.gpsimd
            def _(pool):
                stream(pool, pool_step)

            @block.sync
            def _(sp):
                stream(sp, dma_step)


class Kept:

    def __init__(self, stack, program):
        self.stack, self.program, self.semaphores = stack, program, []

    def enter_context(self, semaphore):
        self.semaphores.append(self.stack.enter_context(semaphore))
        return self.semaphores[-1]

    def software(self, semaphore):
        return self.program.enter_context(semaphore)


def macaron_kernel(nc, io, out):
    with ExitStack() as ctx:
        x = ctx.enter_context(nc.sbuf_tensor("x", [P, BATCH, TILES, D], F32))
        ident = ctx.enter_context(nc.sbuf_tensor("ident", [P, P], F32))
        ident_set = ctx.enter_context(nc.semaphore("ident_set"))

        with nc.Block() as block:
            @block.gpsimd
            def _(pool):
                pool.memset(ident[:, :], 0.0).then_inc(ident_set, 1)
                pool.wait_ge(ident_set, 1)
                pool.affine_select(out=ident[:, :], in_=ident[:, :], compare_op=ALU.not_equal, fill=1.0,
                                   base=0, pattern=[[-1, P]], channel_multiplier=1).then_inc(ident_set, 1)

        experts = {n: io["L0_attn_" + n] for n in ("Wq", "bq", "Wk", "bk", "Wv", "bv")}
        experts |= {n: io["L0_ffn_" + n] for n in ("gate_w", "gate_b", "rms_w", "w1", "b1", "w2", "b2")}
        experts |= {n: io[n] for n in ("x", "rope_tab")}
        routed = {n: io["L1_ffn_" + n] for n in ("attention_mask", "position_ids", "router_w", "router_b", "wq", "wk",
                                                 "wv", "wo", "w1", "w2", "ln1", "ln2")}
        routed["inv_freq"] = io["inv_freq"]
        latent = {n: io["L1_attn_" + n] for n in ("Wq", "Wkv_down", "Wk_up", "Wv_up", "Wout")}

        def layer(build, *args):
            with ExitStack() as kept:
                held = Kept(kept, ctx)
                build(nc, held, *args)
                with nc.Block() as block:
                    @block.sync
                    def _(sp):
                        for semaphore in held.semaphores:
                            sp.sem_clear(semaphore)

        layer(expert_and_head_layers, x, ident, experts)
        layer(routed_layer, "routed1", x, ident, routed)
        layer(latent_attention_layer, x, ident, latent)
        layer(routed_layer, "routed2", x, ident, routed, out)


def kernel(**inputs):
    import numpy as _np
    import concourse.bacc as _bacc
    from concourse import mybir as _mybir
    from concourse.bass_utils import run_bass_kernel_spmd as _run

    even = _np.arange(0, HEAD_DIM, 2, dtype=_np.float32)
    freqs = (_np.float32(10000.0) ** (-(even / _np.float32(D)))).astype(_np.float32)
    angles = _np.arange(SEQ, dtype=_np.float32)[:, None] * freqs[None, :]
    tables = {
        "rope_tab": _np.stack([_np.cos(angles.astype(_np.float64)), _np.sin(angles.astype(_np.float64))],
                              axis=1).astype(_np.float32),
        "inv_freq": (_np.float32(1.0) / _np.float32(10000.0) ** (even / _np.float32(HEAD_DIM))).astype(_np.float32),
    }
    nc = _bacc.Bacc("TRN2", target_bir_lowering=False, num_devices=1)
    arrays, io = {}, {}
    for name, value in {**inputs, **tables}.items():
        a = _np.ascontiguousarray(value)
        arrays[f"in_{name}_dram"] = a
        key = "x" if name == "L0_attn_x" else name
        io[key] = nc.dram_tensor(f"in_{name}_dram", a.shape, _mybir.dt.from_np(a.dtype), kind="ExternalInput").ap()
    out = nc.dram_tensor("out_0_dram", (BATCH, SEQ, D), F32, kind="ExternalOutput").ap()
    macaron_kernel(nc, io, out)
    r = _run(nc, [arrays], core_ids=[0])
    return r.results[0]["out_0_dram"]
```
